# Optimizing a Trainium2 kernel written in Bass

```python
import numpy as np
import jax
import jax.numpy as jnp

def _softmax(x, axis=-1):
    return jax.nn.softmax(x, axis=axis)

def _gelu(x):
    return jax.nn.gelu(x, approximate=True)

def _silu(x):
    return jax.nn.silu(x)

def _sigmoid(x):
    return jax.nn.sigmoid(x)

def _layernorm(x, axis=-1, eps=1e-05):
    m = jnp.mean(x, axis=axis, keepdims=True)
    v = jnp.var(x, axis=axis, keepdims=True)
    return (x - m) / jnp.sqrt(v + eps)

def _scatter_add(tgt, idx, src, axis=0):
    return tgt.at[idx].add(src)

def _segment_sum(src, seg, n):
    return jax.ops.segment_sum(src, seg, n)
kernel_name = 'mk_adj_ffn_d2_adj_r2_84ea00'

def setup_inputs(seed: int=0):
    np.random.seed(seed)
    _w = jnp.asarray

    def _rec_inputs():
        import jax
        import jax.numpy as jnp
        _gk = jax.random.key(seed)
        x = -0.0002928 + 1 * jax.random.normal(jax.random.fold_in(_gk, 1), (128, 64, 128), jnp.float32)
        _a = jax.random.bernoulli(jax.random.fold_in(_gk, 2), 0.0625, (128, 64, 64))
        _a = jnp.logical_or(_a, jnp.swapaxes(_a, -1, -2))
        _a = jnp.logical_or(_a, jnp.eye(64, dtype=bool))
        _af = _a.astype(jnp.float32)
        _af = _af * jax.random.uniform(jax.random.fold_in(_gk, 3), (128, 64, 64), jnp.float32, 0.05, 1)
        adj = _af
        return (x, adj)
    x, adj = _rec_inputs()

    def _L0_gnn_setup():
        import jax, jax.numpy as jnp
        import numpy as np
        key = jax.random.key(seed)
        k1, k2, k3, k4 = jax.random.split(key, 4)
        B, N, F_in, F_out = (8, 1024, 128, 128)
        x = jax.random.normal(k1, (B, N, F_in), dtype=jnp.float32)
        adj = jax.random.uniform(k2, (B, N, N), dtype=jnp.float32)
        stdv = 1.0 / np.sqrt(F_out)
        weight = jax.random.uniform(k3, (F_in, F_out), dtype=jnp.float32, minval=-stdv, maxval=stdv)
        bias = jax.random.uniform(k4, (F_out,), dtype=jnp.float32, minval=-stdv, maxval=stdv)
        return {'x': x, 'adj': adj, 'weight': weight, 'bias': bias}
    _L0_gnn_all = _L0_gnn_setup()
    _L0_gnn_in = {k: v for k, v in _L0_gnn_all.items() if k in ('weight', 'bias')}
    del _L0_gnn_all

    def _L0_ffn_setup():
        import jax, jax.numpy as jnp
        import numpy as np
        B, S, D, F, E, K = (8, 1024, 128, 512, 8, 2)
        key = jax.random.key(seed)
        ks = jax.random.split(key, 10)
        s = 0.02
        return {'x': jax.random.normal(ks[0], (B, S, D), dtype=jnp.float32), 'Wr': jax.random.normal(ks[1], (D, E), dtype=jnp.float32) * s, 'W1s': jax.random.normal(ks[2], (D, F), dtype=jnp.float32) * s, 'b1s': jnp.zeros((F,), dtype=jnp.float32), 'W2s': jax.random.normal(ks[3], (F, D), dtype=jnp.float32) * s, 'b2s': jnp.zeros((D,), dtype=jnp.float32), 'W1p': jax.random.normal(ks[4], (E, D, F), dtype=jnp.float32) * s, 'b1p': jnp.zeros((E, F), dtype=jnp.float32), 'W2p': jax.random.normal(ks[5], (E, F, D), dtype=jnp.float32) * s, 'b2p': jnp.zeros((E, D), dtype=jnp.float32)}
    _L0_ffn_all = _L0_ffn_setup()
    _L0_ffn_in = {k: v for k, v in _L0_ffn_all.items() if k in ('Wr', 'W1s', 'b1s', 'W2s', 'b2s', 'W1p', 'b1p', 'W2p', 'b2p')}
    del _L0_ffn_all

    def _L1_gnn_setup():
        import jax, jax.numpy as jnp
        import numpy as np
        GROUPS = [list(range(25)), [0, 1, 2, 3, 4, 5, 6, 7, 8], [0, 9, 10, 11, 12, 13, 14], [6, 7, 8, 12, 13, 14], [3, 4, 5, 9, 10, 11]]
        B, N, D_IN, D_HID = (4096, 25, 128, 256)

        def _graph_conv(x, adj, W, b):
            n = adj.shape[-1]
            A = adj + jnp.eye(n, dtype=adj.dtype)
            deg = jnp.sum(A, axis=-1)
            deg_safe = jnp.where(deg == 0, 1.0, deg)
            dinv = jnp.where(deg == 0, 0.0, deg_safe ** (-0.5))
            norm_adj = dinv[:, :, None] * A * dinv[:, None, :]
            support = jnp.einsum('bnd,de->bne', x, W)
            out = jnp.einsum('bnm,bme->bne', norm_adj, support) + b
            return jax.nn.relu(out)
        key = jax.random.key(seed)
        ks = jax.random.split(key, 7)
        s1 = float(np.sqrt(6.0 / (D_IN + D_HID)))
        s2 = float(np.sqrt(6.0 / (D_HID + D_IN)))
        return {'x': jax.random.normal(ks[0], (B, N, D_IN), dtype=jnp.float32), 'adj': jax.random.uniform(ks[1], (B, N, N), dtype=jnp.float32), 'W1': jax.random.uniform(ks[2], (5, D_IN, D_HID), jnp.float32, -s1, s1), 'b1': jnp.zeros((5, D_HID), dtype=jnp.float32), 'W2': jax.random.uniform(ks[3], (5, D_HID, D_IN), jnp.float32, -s2, s2), 'b2': jnp.zeros((5, D_IN), dtype=jnp.float32), 'fusion_w': jnp.ones((5,), dtype=jnp.float32)}
    _L1_gnn_all = _L1_gnn_setup()
    _L1_gnn_in = {k: v for k, v in _L1_gnn_all.items() if k in ('W1', 'b1', 'W2', 'b2', 'fusion_w')}
    del _L1_gnn_all

    def _L1_ffn_setup():
        import jax, jax.numpy as jnp
        import numpy as np
        B, S, D, H, E, K = (8, 4096, 128, 512, 8, 2)
        key = jax.random.key(seed)
        ks = jax.random.split(key, 7)
        s_in = 1.0 / np.sqrt(D)
        s_hid = 1.0 / np.sqrt(H)
        return {'x': jax.random.normal(ks[0], (B, S, D), dtype=jnp.float32), 'Wg': jax.random.uniform(ks[1], (E, D), jnp.float32, -s_in, s_in), 'bg': jax.random.uniform(ks[2], (E,), jnp.float32, -s_in, s_in), 'W1': jax.random.uniform(ks[3], (E, H, D), jnp.float32, -s_in, s_in), 'b1': jax.random.uniform(ks[4], (E, H), jnp.float32, -s_in, s_in), 'W2': jax.random.uniform(ks[5], (E, D, H), jnp.float32, -s_hid, s_hid), 'b2': jax.random.uniform(ks[6], (E, D), jnp.float32, -s_hid, s_hid)}
    _L1_ffn_all = _L1_ffn_setup()
    _L1_ffn_in = {k: v for k, v in _L1_ffn_all.items() if k in ('Wg', 'bg', 'W1', 'b1', 'W2', 'b2')}
    del _L1_ffn_all
    return {'x': x, 'adj': adj, 'L0_gnn_weight': _L0_gnn_in['weight'], 'L0_gnn_bias': _L0_gnn_in['bias'], 'L0_ffn_Wr': _L0_ffn_in['Wr'], 'L0_ffn_W1s': _L0_ffn_in['W1s'], 'L0_ffn_b1s': _L0_ffn_in['b1s'], 'L0_ffn_W2s': _L0_ffn_in['W2s'], 'L0_ffn_b2s': _L0_ffn_in['b2s'], 'L0_ffn_W1p': _L0_ffn_in['W1p'], 'L0_ffn_b1p': _L0_ffn_in['b1p'], 'L0_ffn_W2p': _L0_ffn_in['W2p'], 'L0_ffn_b2p': _L0_ffn_in['b2p'], 'L1_gnn_W1': _L1_gnn_in['W1'], 'L1_gnn_b1': _L1_gnn_in['b1'], 'L1_gnn_W2': _L1_gnn_in['W2'], 'L1_gnn_b2': _L1_gnn_in['b2'], 'L1_gnn_fusion_w': _L1_gnn_in['fusion_w'], 'L1_ffn_Wg': _L1_ffn_in['Wg'], 'L1_ffn_bg': _L1_ffn_in['bg'], 'L1_ffn_W1': _L1_ffn_in['W1'], 'L1_ffn_b1': _L1_ffn_in['b1'], 'L1_ffn_W2': _L1_ffn_in['W2'], 'L1_ffn_b2': _L1_ffn_in['b2']}

def reference(x, adj, L0_gnn_weight, L0_gnn_bias, L0_ffn_Wr, L0_ffn_W1s, L0_ffn_b1s, L0_ffn_W2s, L0_ffn_b2s, L0_ffn_W1p, L0_ffn_b1p, L0_ffn_W2p, L0_ffn_b2p, L1_gnn_W1, L1_gnn_b1, L1_gnn_W2, L1_gnn_b2, L1_gnn_fusion_w, L1_ffn_Wg, L1_ffn_bg, L1_ffn_W1, L1_ffn_b1, L1_ffn_W2, L1_ffn_b2):
    import jax
    import jax.numpy as jnp

    def _L0_gnn_ref(x, adj, weight, bias):
        import jax, jax.numpy as jnp
        import numpy as np
        support = jnp.einsum('bni,io->bno', x, weight)
        out = jnp.einsum('bnm,bmo->bno', adj, support)
        return out + bias

    def _L0_ffn_ref(x, Wr, W1s, b1s, W2s, b2s, W1p, b1p, W2p, b2p):
        import jax, jax.numpy as jnp
        import numpy as np
        B, S, D, F, E, K = (8, 1024, 128, 512, 8, 2)
        gelu = lambda t: jax.nn.gelu(t, approximate=False)
        shared = gelu(x @ W1s + b1s) @ W2s + b2s
        rw = jax.nn.softmax(x @ Wr, axis=-1)
        topw, topi = jax.lax.top_k(rw, K)
        topw = topw / jnp.sum(topw, axis=-1, keepdims=True)
        mask = jnp.sum(jax.nn.one_hot(topi, E, dtype=topw.dtype) * topw[..., None], axis=-2)
        h = gelu(jnp.einsum('bsd,edf->bsef', x, W1p) + b1p)
        priv = jnp.einsum('bsef,efd->bsed', h, W2p) + b2p
        routed = jnp.einsum('bsed,bse->bsd', priv, mask)
        return shared + routed

    def _L1_gnn_ref(x, adj, W1, b1, W2, b2, fusion_w):
        import jax, jax.numpy as jnp
        import numpy as np
        GROUPS = [list(range(25)), [0, 1, 2, 3, 4, 5, 6, 7, 8], [0, 9, 10, 11, 12, 13, 14], [6, 7, 8, 12, 13, 14], [3, 4, 5, 9, 10, 11]]
        B, N, D_IN, D_HID = (4096, 25, 128, 256)

        def _graph_conv(x, adj, W, b):
            n = adj.shape[-1]
            A = adj + jnp.eye(n, dtype=adj.dtype)
            deg = jnp.sum(A, axis=-1)
            deg_safe = jnp.where(deg == 0, 1.0, deg)
            dinv = jnp.where(deg == 0, 0.0, deg_safe ** (-0.5))
            norm_adj = dinv[:, :, None] * A * dinv[:, None, :]
            support = jnp.einsum('bnd,de->bne', x, W)
            out = jnp.einsum('bnm,bme->bne', norm_adj, support) + b
            return jax.nn.relu(out)
        norm_w = jax.nn.softmax(fusion_w)
        fused = jnp.zeros_like(x)
        for g, idx_list in enumerate(GROUPS):
            idx = jnp.asarray(idx_list)
            x_g = x[:, idx, :]
            adj_g = adj[:, idx][:, :, idx]
            h = _graph_conv(x_g, adj_g, W1[g], b1[g])
            out_g = _graph_conv(h, adj_g, W2[g], b2[g])
            fused = fused.at[:, idx, :].add(norm_w[g] * out_g)
        return fused

    def _L1_ffn_ref(x, Wg, bg, W1, b1, W2, b2):
        import jax, jax.numpy as jnp
        import numpy as np
        B, S, D, H, E, K = (8, 4096, 128, 512, 8, 2)
        gate_scores = jnp.einsum('bsd,ed->bse', x, Wg) + bg
        topk_scores, topk_idx = jax.lax.top_k(gate_scores, K)
        topk_probs = jax.nn.softmax(topk_scores, axis=-1)
        combine = jnp.sum(topk_probs[..., None] * jax.nn.one_hot(topk_idx, E, dtype=x.dtype), axis=-2)
        out = jnp.zeros_like(x)
        for e in range(E):
            h = jax.nn.relu(jnp.einsum('bsd,hd->bsh', x, W1[e]) + b1[e])
            y = jnp.einsum('bsh,dh->bsd', h, W2[e]) + b2[e]
            out = out + combine[..., e:e + 1] * y
        return out
    x = x + _L0_gnn_ref(_layernorm(x, axis=-1), adj, L0_gnn_weight, L0_gnn_bias)
    x = x + _L0_ffn_ref(_layernorm(x, axis=-1), L0_ffn_Wr, L0_ffn_W1s, L0_ffn_b1s, L0_ffn_W2s, L0_ffn_b2s, L0_ffn_W1p, L0_ffn_b1p, L0_ffn_W2p, L0_ffn_b2p)
    x = x + _L1_gnn_ref(_layernorm(x, axis=-1), adj, L1_gnn_W1, L1_gnn_b1, L1_gnn_W2, L1_gnn_b2, L1_gnn_fusion_w)
    x = x + _L1_ffn_ref(_layernorm(x, axis=-1), L1_ffn_Wg, L1_ffn_bg, L1_ffn_W1, L1_ffn_b1, L1_ffn_W2, L1_ffn_b2)
    return x

_drawn_inputs = setup_inputs


def setup_inputs(seed=0):
    import zlib

    import numpy as np

    out = dict(_drawn_inputs(seed))
    spreads = {'L0_ffn_b1s': (0.0, 0.354),
     'L0_ffn_b2s': (0.0, 0.1),
     'L0_ffn_b1p': (0.0, 0.457),
     'L0_ffn_b2p': (0.0, 0.1),
     'L1_gnn_b1': (0.0, 0.757),
     'L1_gnn_b2': (0.0, 0.629),
     'L1_gnn_fusion_w': (1.0, 0.6)}
    factors = {'L1_ffn_b1': 5.471, 'L1_ffn_b2': 4.33}
    for name, (base, spread) in spreads.items():
        noise = np.random.default_rng([zlib.crc32(name.encode()), seed]).standard_normal(out[name].shape)
        drawn = base * np.exp(spread * noise) if base else spread * noise
        out[name] = jnp.asarray(drawn.astype(out[name].dtype))
    for name, factor in factors.items():
        out[name] = (out[name] * factor).astype(out[name].dtype)
    return out
```

```python
from contextlib import ExitStack

import numpy as np

import concourse.bass as bass
from concourse import mybir

F32 = mybir.dt.float32
F16 = mybir.dt.float16
BF16 = mybir.dt.bfloat16
I32 = mybir.dt.int32
U32 = mybir.dt.uint32
ALU = mybir.AluOpType
ACT = mybir.ActivationFunctionType
AX = mybir.AxisListType.X
ABSMAX = bass.bass_isa.ReduceOp.absmax

P = 128
D = 128
NODES = 64
GRAPHS = 128
TOKENS = GRAPHS * NODES
SUBS = TOKENS // P
NG = 2
GSUB = SUBS // NG
BSUB = 4
GBLK = GSUB // BSUB
EXPERTS = 8
HID = 512
CH = HID // P
TS = 256
TSUB = TS // P
TILES = -(-(2 * GSUB * P // TS + EXPERTS - 1) // 4) * 4
STILES = GSUB * P // TS
GROWS = TILES * TS
EPS = 1e-5
XSCALE_LOG = 10
GRPS = [list(range(25)), list(range(9)), [0] + list(range(9, 15)), [6, 7, 8, 12, 13, 14], [3, 4, 5, 9, 10, 11]]
NGRP = len(GRPS)
LIVE = 25
QB = 4
QR = QB * LIVE
GQ = GRAPHS // NG // QB
GHID = 256
NE = [EXPERTS + 1, EXPERTS]
WP = 2 * HID


def pieces(layer):
    n = NE[layer] * HID
    return [(k, o, min(WP, n - o)) for k in range(2) for o in range(0, n, WP)]


def need(eng, sem, value):
    if not isinstance(value, int) or value > 0:
        eng.wait_ge(sem, value)


def loop(eng, n, unroll, step, head=False, tail=False):
    lo = unroll if head else 0
    hi = n - unroll if tail else n
    for i in range(lo):
        step(i, i)
    if hi > lo:
        with eng.Fori(lo // unroll, hi // unroll) as q:
            for j in range(unroll):
                step(q * unroll + j, j)
    for i in range(max(hi, lo), n):
        step(i, i % unroll)


def program(nc, t, out):
    ctx = ExitStack()
    with ctx:
        build(nc, ctx, t, out)


def build(nc, ctx, t, out):
    def sb(name, shape, dt=F32):
        return ctx.enter_context(nc.sbuf_tensor("sb_" + name, shape, dt))

    def sem(name):
        return ctx.enter_context(nc.semaphore(name))

    sorted_rows = [nc.dram_tensor(f"sorted_rows{g}", (GROWS, 2 * D), F16, kind="Internal").ap() for g in range(NG)]
    expert_rows = [nc.dram_tensor(f"expert_rows{g}", (GROWS, D), F32, kind="Internal").ap() for g in range(NG)]
    stream = nc.dram_tensor("stream", (TOKENS, D), F32, kind="Internal").ap()

    ident = sb("ident", [P, P])
    ident16 = sb("ident16", [P, P], F16)
    upper = sb("upper", [P, P], BF16)
    ones16 = sb("ones16", [P, P], BF16)
    neghalf = sb("neghalf", [P, 8])
    rankkey = sb("rankkey", [P, EXPERTS])
    tileno = sb("tileno", [1, TILES])
    ones_row = sb("ones_row", [1, P])
    zeros = sb("zeros", [P, 512], F16)
    X = sb("X", [P, SUBS, D])
    R = sb("R", [P, SUBS, 2 * D], F16)
    W1h = sb("W1h", [P, NE[0] * HID], F16)
    W1l = sb("W1l", [P, NE[0] * HID], F16)
    W2h = sb("W2h", [P, NE[0] * HID], F16)
    W2l = sb("W2l", [P, NE[0] * HID], F16)
    wstage = [sb(f"wstage{k}", [P, WP]) for k in range(2)]
    wmax = sb("wmax", [P, 16])
    b1all = sb("b1all", [P, NE[0], CH])
    rstage = sb("rstage", [P, 2, EXPERTS])
    Rh = sb("Rh", [P, 2, EXPERTS], F16)
    Rl = sb("Rl", [P, 2, EXPERTS], F16)
    gate_bias = sb("gate_bias", [P, EXPERTS])
    big = sb("big", [P, 2, 4])
    pw = sb("pw", [P, 2, 4])
    sc = sb("sc", [P, 2, 4])
    inv = sb("inv", [P, 2, 4])
    inv_z = sb("inv_z", [P, 2])
    inv_y = sb("inv_y", [P, 2])
    inv_l = sb("inv_l", [P, 2])
    Wg = sb("Wg", [P, D])
    bg4 = sb("bg4", [1, BSUB, D])
    AB = [sb(f"AB{b}", [P, BSUB, P]) for b in range(2)]
    adjT = [sb(f"adjT{b}", [P, BSUB * P]) for b in range(2)]
    aT2 = sb("aT", [P, 2, BSUB * P])
    aT = [aT2[:, b, :] for b in range(2)]
    xn2 = sb("xn", [P, 2, BSUB, D])
    xn = [xn2[:, b] for b in range(2)]
    stats = [sb(f"stats{b}", [P, BSUB, 6]) for b in range(2)]
    mv = [sb(f"mv{b}", [P, BSUB, 2]) for b in range(2)]
    ve = [sb(f"ve{b}", [P, BSUB]) for b in range(2)]
    rstd = [sb(f"rstd{b}", [P, BSUB]) for b in range(2)]
    xs = [sb(f"xs{b}", [P, BSUB, D]) for b in range(2)]
    RT = [sb(f"RT{b}", [P, 2, BSUB * P], F16) for b in range(2)]
    lg = sb("lg", [P, GSUB, EXPERTS])
    lg2 = sb("lg2", [P, GSUB, EXPERTS])
    keyed = sb("keyed", [P, GSUB, EXPERTS])
    top = sb("top", [P, 2, GSUB])
    kmax = sb("kmax", [P, GSUB])
    sel = sb("sel", [P, 2, GSUB, EXPERTS], BF16)
    selw = sb("selw", [P, 2 * GSUB, EXPERTS])
    tot = sb("tot", [2 * GSUB, EXPERTS], BF16)
    totm = sb("totm", [2 * GSUB, 2 * GSUB, EXPERTS], BF16)
    cnt = sb("cnt", [P, EXPERTS])
    cnti = sb("cnti", [P, EXPERTS], I32)
    ntile = sb("ntile", [P, EXPERTS])
    scan = [sb(f"scan{k}", [P, EXPERTS]) for k in range(3)]
    start = sb("start", [P, EXPERTS])
    posf = sb("posf", [P, 2 * GSUB])
    POS = [sb(f"POS{g}", [P, 2 * GSUB], U32) for g in range(NG)]
    PW = [sb(f"PW{g}", [P, 2, GSUB]) for g in range(NG)]
    expd = sb("expd", [P, GSUB])
    den = sb("den", [P, GSUB])
    tcmp = sb("tcmp", [1, TILES, EXPERTS])
    texp = sb("texp", [1, TILES])
    EXP = [sb(f"EXP{g}", [1, TILES], I32) for g in range(NG)]
    XR = [sb(f"XR{b}", [P, TSUB, 2 * D], F16) for b in range(4)]
    BB = [sb(f"BB{b}", [P, CH + D]) for b in range(4)]
    BBs = sb("BBs", [P, CH + D])
    XTt = [sb(f"XTt{b}", [P, 2, TS], F16) for b in range(2)]
    h32 = [sb(f"h32{b}", [P, CH, TS]) for b in range(2)]
    hh = [sb(f"hh{b}", [P, CH, TS], F16) for b in range(2)]
    hl = [sb(f"hl{b}", [P, CH, TS], F16) for b in range(2)]
    ytmp = [sb(f"ytmp{b}", [P, TSUB, D]) for b in range(4)]
    G = [sb(f"G{b}", [P, 2, D]) for b in range(4)]
    gW1 = sb("gW1", [P, NGRP, GHID])
    gW2 = sb("gW2", [P, NGRP, 2, D])
    gb1 = sb("gb1", [P, NGRP, 2])
    gb2 = sb("gb2", [P, NGRP, D])
    indc = sb("indc", [P, NGRP, LIVE])
    self25 = sb("self25", [P, LIVE])
    diagq = sb("diagq", [P, QB])
    wind = sb("wind", [P, NGRP])
    fw = sb("fw", [P, NGRP])
    fwt = sb("fwt", [P, 4])
    rowind = sb("rowind", [P, NGRP])
    Aq = [sb(f"Aq{b}", [P, LIVE]) for b in range(2)]
    xq = [sb(f"xq{b}", [P, D]) for b in range(2)]
    xqn = [sb(f"xqn{b}", [P, D]) for b in range(2)]
    qst = [sb(f"qst{b}", [P, 8]) for b in range(2)]
    qv = [sb(f"qv{b}", [P, 8]) for b in range(2)]
    qp = [sb(f"qp{b}", [P, 8]) for b in range(2)]
    a25 = sb("a25", [P, LIVE])
    am = [sb(f"am{b}", [P, NGRP, LIVE]) for b in range(2)]
    deg = [sb(f"deg{b}", [P, NGRP]) for b in range(2)]
    isz = [sb(f"isz{b}", [P, NGRP]) for b in range(2)]
    dinv = [sb(f"dinv{b}", [P, NGRP]) for b in range(2)]
    nb = [AB[b][:].rearrange("p s m -> p (s m)")[:, 0:NGRP * QR].rearrange("p (g b m) -> p g b m", g=NGRP, b=QB)
          for b in range(2)]
    NT = [adjT[b][:, 0:NGRP * QR].rearrange("p (g n) -> p g n", g=NGRP) for b in range(2)]
    h1T = aT2[:].rearrange("p b n -> p (b n)")[:, 0:2 * NGRP * QR].rearrange("p (c g n) -> p c g n", c=2, g=NGRP)
    qt = xn2[:].rearrange("p b s d -> p (b s) d")[:, 0:NGRP, :]
    qaT = sb("qaT", [P, NGRP, QR])
    s2 = sb("s2", [P, NGRP, D])
    qt2 = sb("qt2", [P, NGRP, D])
    qsum = sb("qsum", [P, D])
    xo = [sb(f"xo{b}", [P, D]) for b in range(2)]

    bk = [ctx.enter_context(nc.psum_tensor(f"bank{k}", [P, 512], F32)) for k in range(8)]

    ld_small = sem("small_loaded")
    ld_w = [sem(f"weights_loaded{k}") for k in range(2)]
    s_const = sem("constants_made")
    s_vconst = sem("vector_constants_made")
    s_zero = sem("sorted_rows_zeroed")
    s_rmax = sem("router_reduced")
    s_rall = sem("router_max_everywhere")
    s_rscale = sem("router_scaled")
    s_fusx = sem("fusion_exp")
    s_prep = sem("prep_reduced")
    s_prepall = sem("prep_max_everywhere")
    s_scale = sem("weights_scales_ready")
    s_whi = sem("weights_hi_ready")
    s_wfree = sem("weights_piece_used")
    ld_b1 = sem("hidden_biases_loaded")
    ld_g = sem("grouped_weights_loaded")
    v = sem("vector_step")
    ld_a = [sem(f"block_loaded{b}") for b in range(2)]
    s_var = sem("variance_ready")
    s_rstd = sem("rstd_ready")
    s_xn = sem("normalised")
    s_adjt = sem("adj_transposed")
    s_adjc = sem("adjT_copied")
    s_at = sem("aggregated")
    s_atc = sem("aggregated_copied")
    s_conv = sem("convolved")
    s_x1 = sem("residual_added")
    s_rows = sem("rows_split")
    s_rt = sem("rows_transposed")
    s_rtc = sem("rowsT_copied")
    s_log = sem("logits_ready")
    s_lgr = sem("logits_read")
    s_sel = sem("selected")
    s_tot = sem("totals_ready")
    s_totm = sem("totals_masked")
    s_rank = sem("ranks_ready")
    s_diff = sem("logit_difference")
    s_exp = sem("gate_exp")
    s_route = sem("routes_ready")
    s_scat = [sem(f"rows_scattered{g}") for g in range(NG)]
    s_xr = [sem(f"tile_loaded{b}") for b in range(4)]
    s_tt = sem("tile_transposed")
    s_ttc = sem("tileT_copied")
    s_h = sem("hidden_ready")
    s_act = sem("hidden_activated")
    s_hh = sem("hidden_hi")
    s_hl = sem("hidden_split")
    s_yp = sem("expert_out_ready")
    s_y = sem("expert_out_scaled")
    s_xsh = sem("shared_added")
    s_st = [sem(f"expert_rows_stored{b}") for b in range(4)]
    s_g = [sem(f"rows_gathered{b}") for b in range(4)]
    s_comb = sem("combined")
    s_xst = [sem(f"stream_stored{g}") for g in range(NG)]
    ld_q = [sem(f"quad_loaded{b}") for b in range(2)]
    s_qv = sem("degrees_ready")
    s_qp = sem("degree_roots_ready")
    s_qn = sem("quad_normalised")
    s_nb = sem("norm_rows_ready")
    s_nt = sem("norm_transposed")
    s_ntc = sem("normT_ready")
    s_qa = sem("quad_aggregated")
    s_qac = sem("quad_aggregated_copied")
    s_h1 = sem("quad_hidden")
    s_h1c = sem("quad_hidden_activated")
    s_s2 = sem("quad_support")
    s_s2c = sem("quad_support_copied")
    s_o2 = sem("quad_out")
    s_o2r = sem("quad_out_read")
    s_xo = sem("quad_added")
    s_qst = [sem(f"quad_stored{b}") for b in range(2)]
    s_out = sem("outputs_stored")
    s_alone = sem("waits_alone")
    s_vx = sem("rows_normalised")
    s_vh = sem("rows_hi")
    s_half = sem("half_combined")

    block = ctx.enter_context(nc.Block())

    def a0(layer, g):
        return (layer * NG + g) * GBLK

    def e0(layer, g):
        return NG * STILES + (layer * NG + g) * TILES

    def q0(g):
        return g * GQ

    def piece0(layer, again):
        return layer * 2 * len(pieces(0)) + again * len(pieces(layer))

    NSMALL = 12 + 2 * 2

    @block.sync
    def _(sp):
        sp.dma_start(rstage[:, 0, :], t["wr0"]).then_inc(ld_small, 16)
        sp.dma_start(rstage[:, 1, :], t["wr1"]).then_inc(ld_small, 16)
        sp.dma_start(Wg[:], t["gnn_w"]).then_inc(ld_small, 16)
        for s in range(BSUB):
            sp.dma_start(bg4[0:1, s, :], t["gnn_b"]).then_inc(ld_small, 16)
        sp.dma_start(gate_bias[:], t["bg"].broadcast_to([P, EXPERTS])).then_inc(ld_small, 16)
        sp.dma_start(fw[:], t["fusion"].broadcast_to([P, NGRP])).then_inc(ld_small, 16)
        sp.dma_start(gb2[:].rearrange("p g d -> p (g d)"), t["gb2"].broadcast_to([P, NGRP * D])).then_inc(ld_small, 16)
        sp.dma_start(gb1[:], t["gb1"]).then_inc(ld_small, 16)
        sp.dma_start(BBs[:], t["bb0"][EXPERTS]).then_inc(ld_small, 16)
        sp.dma_start(indc[0:QR].rearrange("p g m -> p (g m)"), t["indc"]).then_inc(ld_small, 16)
        sp.dma_start(self25[0:QR], t["self25"]).then_inc(ld_small, 16)
        sp.dma_start(diagq[0:QR], t["diagq"]).then_inc(ld_small, 16)
        sp.dma_start(rowind[0:QR], t["rowind"]).then_inc(ld_small, 16)

        def load_block(layer, g):
            def step(i, j):
                b = j % 2
                n = a0(layer, g) + i
                blk = g * GBLK + i
                rows = bass.ds(blk * (BSUB * P), BSUB * P)
                dst = X[:, bass.ds(blk * BSUB, BSUB), :]
                if layer == 0:
                    src = t["x"][rows, :]
                    need(sp, s_adjt, n - 1)
                    for h in range(2):
                        hs = slice(h * NODES, (h + 1) * NODES)
                        sp.dma_start(AB[b][hs, :, hs],
                                     t["adj2"][bass.ds(blk * BSUB, BSUB), hs, :].rearrange("s n m -> n s m")
                                     ).then_inc(ld_a[b], 16)
                else:
                    need(sp, s_rows, n - 1)
                    src = stream[rows, :]
                sp.dma_start(dst, src.rearrange("(s p) d -> p s d", p=P)).then_inc(ld_a[b], 16)
            return step

        sp.wait_ge(s_const, 1)
        loop(sp, GBLK, 2, load_block(0, 0), head=True)
        sp.dma_start(gW1[:], t["gW1"]).then_inc(ld_g, 16)
        sp.dma_start(gW2[:], t["gW2"]).then_inc(ld_g, 16)
        zr = P * 2
        for g in range(NG):
            for r in range(0, GROWS, zr):
                sp.dma_start(sorted_rows[g][r:r + zr, :].rearrange("(p k) d -> p (k d)", p=P), zeros[:]).then_inc(s_zero, 16)
        for g in range(1, NG):
            loop(sp, GBLK, 2, load_block(0, g))

        def load_weights(layer):
            sp.dma_start(b1all[:, 0:NE[layer]], t[f"bb{layer}"].rearrange("e p n -> p e n")[:, :, 0:CH]).then_inc(ld_b1, 16)
            for r, (k, o, n) in enumerate(2 * pieces(layer)):
                r += layer * 2 * len(pieces(0))
                need(sp, s_wfree, r - 1)
                sp.dma_start(wstage[r % 2][:, 0:n], t[f"w{k + 1}_{layer}"][:, o:o + n]).then_inc(ld_w[r % 2], 16)

        load_weights(0)

        def routed(layer, g, rides):
            base = e0(layer, g)
            bb = t["bb0"] if layer == 0 else t["bb1"]

            def load(i, j):
                n = base + i
                e = sp.value_load(EXP[g][0:1, bass.ds(i, 1)], min_val=0, max_val=EXPERTS - 1)
                need(sp, s_tt, n - 3)
                need(sp, s_y, n - 3)
                sp.dma_start(XR[j % 4][:], sorted_rows[g][bass.ds(i * TS, TS), :].rearrange("(s p) d -> p s d", p=P)
                             ).then_inc(s_xr[j % 4], 16)
                sp.dma_start(BB[j % 4][:], bb[bass.ds(e, 1)].rearrange("a p n -> p (a n)")).then_inc(s_xr[j % 4], 16)

            def step(i, j):
                n = base + i
                sp.wait_ge(s_y, n + 1)
                sp.dma_start(expert_rows[g][bass.ds(i * TS, TS), :].rearrange("(s p) d -> p s d", p=P),
                             ytmp[j % 4][:]).then_inc(s_st[j % 4], 16)
                if rides is not None:
                    store_combined(layer, rides, i, j)

            sp.wait_ge(s_route, layer * NG + g + 1)
            sp.wait_ge(s_scat[g], 16 * 2 * GSUB * (layer + 1))
            for i in range(4):
                load(i, i)
            with sp.Fori(0, TILES // 4 - 1) as q:
                for j in range(4):
                    step(q * 4 + j, j)
                    load(q * 4 + j + 4, j)
            for i in range(TILES - 4, TILES):
                step(i, i % 4)

        def store_combined(layer, g, i, j):
            if isinstance(i, int) and i >= GSUB:
                return
            raise AssertionError

        def store_sub(layer, g, i):
            need(sp, s_comb, (layer * NG + g) * GSUB + i + 1)
            dst = stream if layer == 0 else out
            done = s_xst[g] if layer == 0 else s_out
            sp.dma_start(dst[bass.ds((g * GSUB + i) * P, P), :], X[:, bass.ds(g * GSUB + i, 1), :].rearrange("p a d -> p (a d)")
                         ).then_inc(done, 16)

        def store_group(layer, g):
            loop(sp, GSUB, 4, lambda i, j: store_sub(layer, g, i))

        def quads(g):
            sp.wait_ge(s_xst[g], 16 * GSUB)

            def load(i, j):
                b = j % 2
                n = q0(g) + i
                gr = (g * GQ + i) * QB
                need(sp, s_xo, n - 1)
                need(sp, s_nb, n - 1)
                for k in range(QB):
                    rs = slice(k * LIVE, (k + 1) * LIVE)
                    sp.dma_start(xq[b][rs, :], stream[bass.ds((gr + k) * NODES, LIVE), :]).then_inc(ld_q[b], 16)
                sp.dma_start(Aq[b][0:QR, :], t["adj25"][bass.ds((g * GQ + i) * QR, QR), :]).then_inc(ld_q[b], 16)

            def step(i, j):
                b = j % 2
                gr = (g * GQ + i) * QB
                sp.wait_ge(s_xo, q0(g) + i + 1)
                for k in range(QB):
                    rs = slice(k * LIVE, (k + 1) * LIVE)
                    sp.dma_start(stream[bass.ds((gr + k) * NODES, LIVE), :], xo[b][rs, :]).then_inc(s_qst[b], 16)

            for i in range(2):
                load(i, i)
            with sp.Fori(0, GQ // 2 - 1) as q:
                for j in range(2):
                    step(q * 2 + j, j)
                    load(q * 2 + j + 2, j)
            for i in range(GQ - 2, GQ):
                step(i, i % 2)

        for g in range(NG):
            routed(0, g, None)
            store_group(0, g)
        load_weights(1)
        for g in range(NG):
            quads(g)
            for b in range(2):
                sp.wait_ge(s_qst[b], 16 * QB * GQ // 2 * (g + 1))
            loop(sp, GBLK, 2, load_block(1, g))
        for g in range(NG):
            routed(1, g, None)
            store_group(1, g)
        sp.wait_ge(s_out, 16 * SUBS)

    @block.gpsimd
    def _(pool):
        nc.gpsimd.memset(AB[0][:], 0.0)
        nc.gpsimd.memset(AB[1][:], 0.0).then_inc(s_const, 1)
        nc.gpsimd.memset(zeros[:], 0.0)
        nc.gpsimd.memset(ident[:], 0.0)
        nc.gpsimd.memset(upper[:], 0.0)
        nc.gpsimd.memset(ones16[:], 1.0)
        nc.gpsimd.memset(ones_row[:], 1.0)
        nc.gpsimd.memset(neghalf[:], -0.5)
        nc.gpsimd.iota(rankkey[:], pattern=[[-1, EXPERTS]], base=EXPERTS, channel_multiplier=0,
                       allow_small_or_imprecise_dtypes=True)
        nc.gpsimd.iota(tileno[:], pattern=[[1, TILES]], base=0, channel_multiplier=0,
                       allow_small_or_imprecise_dtypes=True).then_inc(s_const, 1)
        pool.wait_ge(s_const, 2)
        nc.gpsimd.affine_select(out=ident[:], in_=ident[:], compare_op=ALU.not_equal, fill=1.0, base=0,
                                pattern=[[-1, P]], channel_multiplier=1)
        nc.gpsimd.affine_select(out=upper[:], in_=upper[:], compare_op=ALU.is_ge, fill=1.0, base=0,
                                pattern=[[-1, P]], channel_multiplier=1).then_inc(s_const, 1)
        pool.wait_ge(s_const, 3)
        nc.gpsimd.tensor_copy(ident16[:], ident[:]).then_inc(s_const, 1)
        pool.wait_ge(s_rmax, 1)
        nc.gpsimd.partition_all_reduce(big[:, :, 3], big[:, :, 3], P, ABSMAX).then_inc(s_rall, 1)

        def rstds(layer, g):
            def step(i, j):
                n = a0(layer, g) + i
                b = j % 2
                for k in range(2 if layer == 0 else 1):
                    m = 2 * n + k if layer == 0 else a0(1, 0) * 2 + (n - a0(1, 0))
                    pool.wait_ge(s_var, m + 1)
                    nc.gpsimd.tensor_tensor(rstd[b][:], ve[b][:], neghalf[:, 0:BSUB], ALU.pow).then_inc(s_rstd, 1)
            loop(pool, GBLK, 2, step)

        def scatter(layer, g):
            pool.wait_ge(s_route, layer * NG + g + 1)
            if layer == 0 and g == 0:
                pool.wait_ge(s_zero, 16 * (NG * GROWS // (P * 2)))
            if layer == 1:
                for b in range(4):
                    pool.wait_ge(s_xr[b], 32 * (TILES // 4) * (g + 1))
            for s in range(GSUB):
                for k in range(2):
                    c = k * GSUB + s
                    nc.gpsimd.indirect_dma_start(sorted_rows[g], bass.IndirectOffsetOnAxis(ap=POS[g][:, c:c + 1], axis=0),
                                                 R[:, g * GSUB + s, :], None).then_inc(s_scat[g], 16)

        def gather(layer, g):
            for b in range(4):
                pool.wait_ge(s_st[b], 16 * (TILES // 4) * (layer * NG + g + 1))
            for s in range(GSUB):
                need(pool, s_comb, (layer * NG + g) * GSUB + s - 3)
                for k in range(2):
                    c = k * GSUB + s
                    nc.gpsimd.indirect_dma_start(G[s % 4][:, k, :], None, expert_rows[g],
                                                 bass.IndirectOffsetOnAxis(ap=POS[g][:, c:c + 1], axis=0)
                                                 ).then_inc(s_g[s % 4], 16)

        def roots(g):
            def step(i, j):
                b = j % 2
                pool.wait_ge(s_qv, q0(g) + i + 1)
                nc.gpsimd.tensor_tensor(qp[b][0:QR, 0:NGRP + 1], qv[b][0:QR, 0:NGRP + 1], neghalf[0:QR, 0:NGRP + 1],
                                        ALU.pow).then_inc(s_qp, 1)
            loop(pool, GQ, 2, step)

        for g in range(NG):
            rstds(0, g)
        pool.wait_ge(s_prep, 1)
        nc.gpsimd.partition_all_reduce(big[:, 0, 0:3], big[:, 0, 0:3], P, ABSMAX).then_inc(s_prepall, 1)
        for g in range(NG):
            scatter(0, g)
        for g in range(NG):
            gather(0, g)
        pool.wait_ge(s_prep, 2)
        nc.gpsimd.partition_all_reduce(big[:, 1, 0:3], big[:, 1, 0:3], P, ABSMAX).then_inc(s_prepall, 1)
        for g in range(NG):
            roots(g)
            rstds(1, g)
            scatter(1, g)
        for g in range(NG):
            gather(1, g)

    @block.scalar
    def _(act):
        act.wait_ge(ld_small, 16 * NSMALL)
        act.wait_ge(s_vconst, 2)
        nc.scalar.activation(fw[:], fw[:], ACT.Exp, bias=fwt[:, 1:2]).then_inc(s_fusx, 1)

        def blocks(layer, g):
            def step(i, j):
                b = j % 2
                n = a0(layer, g) + i
                if layer == 0:
                    act.wait_ge(s_adjt, n + 1)
                    need(act, s_at, n - 1)
                    nc.scalar.activation(adjT[b][:], bk[b][:], ACT.Copy).then_inc(s_adjc, 1)
                    act.wait_ge(s_at, n + 1)
                    need(act, s_conv, n - 1)
                    nc.scalar.activation(aT[b][:], bk[2 + b][:], ACT.Copy).then_inc(s_atc, 1)
                act.wait_ge(s_rt, n + 1)
                need(act, s_log, n - 1)
                nc.scalar.activation(RT[b][:].rearrange("p h t -> p (h t)"), bk[5 + b][:].bitcast(F16), ACT.Copy
                                     ).then_inc(s_rtc, 1)
            loop(act, GBLK, 2, step, head=(layer, g) == (0, 0))

        def gate(layer, g):
            act.wait_ge(s_diff, layer * NG + g + 1)
            nc.scalar.activation(expd[:], den[:], ACT.Exp).then_inc(s_exp, 1)

        def prep(layer):
            act.wait_ge(s_scale, layer + 1)
            if layer == 1:
                act.wait_ge(s_yp, e0(1, 0))
            for r, (k, o, n) in enumerate(pieces(layer)):
                p = piece0(layer, 1) + r
                act.wait_ge(ld_w[p % 2], 16 * (p // 2 + 1))
                nc.scalar.activation((W1h, W2h)[k][:, o:o + n], wstage[p % 2][:, 0:n], ACT.Copy, scale=sc[:, layer, k:k + 1]
                                     ).then_inc(s_whi, 1)

        def tiles(base, n_tiles, layer, shared, first):
            def step(i, j):
                b = j % 2
                n = base + i
                act.wait_ge(s_tt, n + 1)
                need(act, s_h, 2 * (n - 1))
                nc.scalar.activation(XTt[b][:].rearrange("p h t -> p (h t)"), bk[4 + b][:, 0:TS].bitcast(F16), ACT.Copy
                                     ).then_inc(s_ttc, 1)
                bias = BBs if shared else BB[j % 4]
                if not shared:
                    act.wait_ge(s_xr[j % 4], 32 * ((n - NG * STILES) // 4 + 1) if isinstance(i, int) else 32 * ((base - NG * STILES) // 4 + 1) + (i - j) * 8)
                for half in range(2):
                    act.wait_ge(s_h, 2 * n + half + 1)
                    need(act, s_hl, 2 * (n - 2) + half + 1)
                    for c in (2 * half, 2 * half + 1):
                        a = nc.scalar.activation(h32[b][:, c, :], bk[2 * b + half][:, (c % 2) * TS:(c % 2 + 1) * TS],
                                                 ACT.Gelu if layer == 0 else ACT.Relu,
                                                 bias=bias[:, c:c + 1], scale=inv_z[:, layer:layer + 1])
                    a.then_inc(s_act, 1)
            loop(act, n_tiles, 4, step, head=first)

        def quads(g):
            def step(i, j):
                n = q0(g) + i
                act.wait_ge(s_qa, n + 1)
                need(act, s_h1, 2 * n)
                nc.scalar.activation(qaT[:], bk[1][:, 0:NGRP * QR].rearrange("p (g n) -> p g n", g=NGRP), ACT.Copy
                                     ).then_inc(s_qac, 1)
                for c in range(2):
                    act.wait_ge(s_h1, 2 * n + c + 1)
                    if c == 0:
                        need(act, s_s2, n)
                    for k in range(NGRP):
                        a = nc.scalar.activation(h1T[:, c, k, :], bk[2 + c][:, k * QR:(k + 1) * QR], ACT.Relu,
                                                 bias=gb1[:, k, c:c + 1])
                    a.then_inc(s_h1c, 1)
                act.wait_ge(s_s2, n + 1)
                need(act, s_o2, n)
                nc.scalar.activation(s2[0:QR, 0:4, :], bk[4][0:QR, :].rearrange("p (g d) -> p g d", g=4), ACT.Copy)
                nc.scalar.activation(s2[0:QR, 4, :], bk[5][0:QR, 0:D], ACT.Copy).then_inc(s_s2c, 1)
            loop(act, GQ, 2, step, head=g == 0)

        for g in range(NG):
            blocks(0, g)
            gate(0, g)
        prep(0)
        for g in range(NG):
            tiles(g * STILES, STILES, 0, True, g == 0)
        for g in range(NG):
            tiles(e0(0, g), TILES, 0, False, False)
        prep(1)
        for g in range(NG):
            quads(g)
            blocks(1, g)
            gate(1, g)
        for g in range(NG):
            tiles(e0(1, g), TILES, 1, False, False)

    @block.tensor
    def _(pe):
        pe.wait_ge(s_const, 4)
        pe.wait_ge(ld_small, 16 * NSMALL)
        pe.wait_ge(s_rscale, 1)

        def blocks(layer, g):
            if (layer, g) != (0, 0):
                pe.wait_ge(s_route, layer * NG + g)
            if layer == 1:
                pe.wait_ge(s_s2c, q0(g) + GQ)

            def adj_side(i, j):
                b = j % 2
                n = a0(layer, g) + i
                pe.wait_ge(ld_a[b], 48 * (n // 2 + 1) if isinstance(i, int) else 48 * (a0(layer, g) // 2 + 1) + (i - j) * 24)
                need(pe, s_adjc, n - 1)
                for s in range(BSUB):
                    m = pe.transpose(bk[b][:, s * P:(s + 1) * P], AB[b][:, s, :], ident[:])
                m.then_inc(s_adjt, 1)

            def step(i, j):
                b = j % 2
                n = a0(layer, g) + i
                if layer == 0:
                    adj_side(i, j)
                    pe.wait_ge(s_xn, n + 1)
                    pe.wait_ge(s_adjc, n + 1)
                    need(pe, s_atc, n - 1)
                    for s in range(BSUB):
                        m = pe.matmul(bk[2 + b][:, s * P:(s + 1) * P], xn[b][:, s, :], adjT[b][:, s * P:(s + 1) * P],
                                      start=True, stop=True)
                    m.then_inc(s_at, 1)
                    need(pe, s_x1, n)
                    pe.matmul(bk[4][:], ones_row[:], bg4[:].rearrange("p s d -> p (s d)"), start=True, stop=False,
                              skip_group_check=True)
                    pe.wait_ge(s_atc, n + 1)
                    for s in range(BSUB):
                        m = pe.matmul(bk[4][:, s * P:(s + 1) * P], aT[b][:, s * P:(s + 1) * P], Wg[:],
                                      start=False, stop=(s == BSUB - 1), skip_group_check=True)
                    m.then_inc(s_conv, 1)
                pe.wait_ge(s_rows, n + 1)
                need(pe, s_rtc, n - 1)
                bank = bk[5 + b][:].bitcast(F16)
                for h in range(2):
                    for s in range(BSUB):
                        o = (h * BSUB + s) * P
                        row = R[:, bass.ds((g * GBLK + i) * BSUB + s, 1), h * D:(h + 1) * D].rearrange("p a d -> p (a d)")
                        m = pe.transpose(bank[:, o:o + P], row, ident16[:])
                m.then_inc(s_rt, 1)
                pe.wait_ge(s_rtc, n + 1)
                for s in range(BSUB):
                    o = bk[7][:, bass.ds((i * BSUB + s) * EXPERTS, EXPERTS)]
                    terms = [(0, Rh), (1, Rh), (0, Rl), (1, Rl)]
                    for k, (h, w) in enumerate(terms):
                        m = pe.matmul(o, RT[b][:, h, s * P:(s + 1) * P], w[:, layer, :], start=k == 0, stop=k == 3)
                m.then_inc(s_log, 1)
            loop(pe, GBLK, 2, step, head=(layer, g) == (0, 0))

        def gate(layer, g):
            c = layer * NG + g
            pe.wait_ge(s_sel, c + 1)
            J = 2 * GSUB
            selj = sel[:].rearrange("p k s e -> p (k s) e")
            for e in range(EXPERTS):
                m = pe.matmul(bk[0][0:J, e:e + 1], selj[:, :, e], ones16[:, 0:1], start=True, stop=True)
            m.then_inc(s_tot, 1)
            pe.wait_ge(s_totm, c + 1)
            pe.matmul(bk[1][:, 0:J * EXPERTS], upper[:], selj.rearrange("p j e -> p (j e)"), start=True, stop=False)
            pe.matmul(bk[1][:, 0:J * EXPERTS], ones16[0:J, :], totm[:].rearrange("q j e -> q (j e)"), start=False, stop=True)
            pe.matmul(bk[2][:, 0:EXPERTS], ones16[0:J, :], tot[:], start=True, stop=True).then_inc(s_rank, 1)

        def tiles(base, n_tiles, layer, shared, g):
            def wait_loaded(i, j):
                if not shared:
                    r0 = (base - NG * STILES) // 4
                    pe.wait_ge(s_xr[j % 4], 32 * (r0 + i // 4 + 1) if isinstance(i, int) else 32 * (r0 + 1) + (i - j) * 8)

            def turn(i, j):
                b = j % 2
                wait_loaded(i, j)
                need(pe, s_ttc, base + i - 1)
                bank = bk[4 + b][:, 0:TS].bitcast(F16)
                for h in range(2):
                    for s in range(TSUB):
                        o = (h * TSUB + s) * P
                        if shared:
                            row = R[:, bass.ds(g * GSUB + i * TSUB + s, 1), h * D:(h + 1) * D].rearrange("p a d -> p (a d)")
                        else:
                            row = XR[j % 4][:, s, h * D:(h + 1) * D]
                        m = pe.transpose(bank[:, o:o + P], row, ident16[:])
                m.then_inc(s_tt, 1)

            def hidden(i, j, e):
                b = j % 2
                n = base + i
                pe.wait_ge(s_ttc, n + 1)
                for half in range(2):
                    need(pe, s_act, 2 * (n - 2) + half + 1)
                    for c in (2 * half, 2 * half + 1):
                        o = bk[2 * b + half][:, (c % 2) * TS:(c % 2 + 1) * TS]
                        for k, (w, h) in enumerate(((W1h, 0), (W1h, 1), (W1l, 0))):
                            m = pe.matmul(o, w[:, at(e, c)], XTt[b][:, h, :], start=k == 0, stop=k == 2)
                    m.then_inc(s_h, 1)

            def outs(i, j, e):
                b = j % 2
                n = base + i
                pe.wait_ge(s_hl, 2 * n + 2)
                need(pe, s_y, n - 1)
                for s in range(TSUB):
                    o = bk[6 + b][:, s * D:(s + 1) * D]
                    rows = slice(s * P, (s + 1) * P)
                    for c in range(CH):
                        for k, (h, w) in enumerate(((hh, W2h), (hl, W2h), (hh, W2l))):
                            m = pe.matmul(o, h[b][:, c, rows], w[:, at(e, c)],
                                          start=c == 0 and k == 0, stop=c == CH - 1 and k == 2)
                m.then_inc(s_yp, 1)

            def at(e, c):
                if isinstance(e, int):
                    return slice(e * HID + c * P, e * HID + (c + 1) * P)
                return bass.ds(e * HID + c * P, P)

            def expert(i):
                if shared:
                    return EXPERTS
                return pe.value_load(EXP[g][0:1, bass.ds(i, 1)], min_val=0, max_val=EXPERTS - 1)

            turn(0, 0)
            turn(1, 1)
            e_now = expert(0)
            hidden(0, 0, e_now)

            def steps(base_i, count, last):
                e = [expert(base_i + k) for k in range(count + (0 if last else 1))]
                for j in range(count):
                    i = base_i + j
                    if not last or j + 2 < count:
                        turn(i + 2, (j + 2) % 4)
                    if not last or j + 1 < count:
                        hidden(i + 1, (j + 1) % 4, e[j + 1])
                    outs(i, j, e[j])

            first = 0
            if shared and g == 0:
                steps(0, 4, False)
                first = 1
            with pe.Fori(first, n_tiles // 4 - 1) as q:
                steps(q * 4, 4, False)
            steps(n_tiles - 4, 4, True)

        def quads(g):
            def turn(i, j):
                b = j % 2
                n = q0(g) + i
                pe.wait_ge(s_nb, n + 1)
                need(pe, s_ntc, n)
                for k in range(NGRP):
                    m = pe.transpose(bk[0][0:QR, k * QR:(k + 1) * QR], nb[b][0:QR, k, :, :].rearrange("p b m -> p (b m)"),
                                     ident[0:QR, 0:QR])
                m.then_inc(s_nt, 1)

            def aggregate(i, j):
                b = j % 2
                n = q0(g) + i
                pe.wait_ge(s_ntc, n + 1)
                pe.wait_ge(s_qn, n + 1)
                need(pe, s_qac, n)
                pe.matmul(bk[1][:, 0:NGRP * QR], xqn[b][0:QR, :], NT[b][0:QR].rearrange("p g n -> p (g n)"),
                          start=True, stop=True).then_inc(s_qa, 1)

            def hidden(i, j):
                n = q0(g) + i
                pe.wait_ge(s_qac, n + 1)
                for c in range(2):
                    need(pe, s_h1c, 2 * (n - 1) + c + 1)
                    for k in range(NGRP):
                        m = pe.matmul(bk[2 + c][:, k * QR:(k + 1) * QR], gW1[:, k, c * P:(c + 1) * P], qaT[:, k, :],
                                      start=True, stop=True)
                    m.then_inc(s_h1, 1)

            def support(i, j):
                n = q0(g) + i
                pe.wait_ge(s_h1c, 2 * n + 2)
                need(pe, s_s2c, n)
                for k in range(NGRP):
                    for c in range(2):
                        m = pe.matmul(bk[4 + k // 4][0:QR, (k % 4) * D:(k % 4 + 1) * D], h1T[:, c, k, :], gW2[:, k, c, :],
                                      start=c == 0, stop=c == 1)
                m.then_inc(s_s2, 1)

            def outs(i, j):
                b = j % 2
                n = q0(g) + i
                pe.wait_ge(s_s2c, n + 1)
                need(pe, s_o2r, n)
                for k in range(NGRP):
                    m = pe.matmul(bk[6 + k // 4][0:QR, (k % 4) * D:(k % 4 + 1) * D], NT[b][0:QR, k, :], s2[0:QR, k, :],
                                  start=True, stop=True)
                m.then_inc(s_o2, 1)

            turn(0, 0)
            aggregate(0, 0)
            hidden(0, 0)

            def step(i, j, last=False):
                if not last:
                    turn(i + 1, j + 1)
                    aggregate(i + 1, j + 1)
                support(i, j)
                if not last:
                    hidden(i + 1, j + 1)
                outs(i, j)

            first = 0
            if g == 0:
                step(0, 0)
                step(1, 1)
                first = 1
            with pe.Fori(first, GQ // 2 - 1) as q:
                for j in range(2):
                    step(q * 2 + j, j)
            step(GQ - 2, 0)
            step(GQ - 1, 1, last=True)

        for g in range(NG):
            blocks(0, g)
            gate(0, g)
        pe.wait_ge(s_wfree, piece0(0, 2))
        pe.wait_ge(s_route, NG)
        for g in range(NG):
            tiles(g * STILES, STILES, 0, True, g)
        for g in range(NG):
            tiles(e0(0, g), TILES, 0, False, g)
        pe.wait_ge(s_y, e0(1, 0))
        pe.wait_ge(ld_g, 32)
        for g in range(NG):
            if g:
                pe.wait_ge(s_route, NG + g)
            quads(g)
            pe.wait_ge(s_o2r, q0(g) + GQ)
            blocks(1, g)
            gate(1, g)
        pe.wait_ge(s_wfree, piece0(1, 2))
        pe.wait_ge(s_route, 2 * NG)
        for g in range(NG):
            tiles(e0(1, g), TILES, 1, False, g)

    @block.vector
    def _(dve):
        count = [0]

        def own(ins):
            count[0] += 1
            ins.then_inc(v, 1)
            dve.wait_ge(v, count[0])

        class InLoop:

            def __init__(self, per):
                self.base, self.per = count[0], per

            def at(self, i):
                self.first, self.k = self.base + i * self.per, 0

            def mark(self, ins):
                self.k += 1
                ins.then_inc(v, 1)

            def wait(self, alone=False):
                w = dve.wait_ge(v, self.first + self.k)
                if alone:
                    w.then_inc(s_alone, 1)

            def end(self, n):
                assert self.k == self.per, (self.k, self.per)
                count[0] = self.base + n * self.per

        dve.wait_ge(ld_small, 16 * NSMALL)
        for l in range(2):
            m = nc.vector.tensor_reduce(big[:, l, 3:4], rstage[:, l, :], AX, ALU.max, apply_absolute_value=True)
        m.then_inc(s_rmax, 1)
        own(nc.vector.tensor_reduce(fwt[:, 0:1], fw[:], AX, ALU.max))
        nc.vector.memset(wind[:], 0.0).then_inc(s_vconst, 1)
        nc.vector.tensor_scalar(fwt[:, 1:2], fwt[:, 0:1], -1.0, None, ALU.mult).then_inc(s_vconst, 1)
        dve.wait_ge(s_fusx, 1)
        own(nc.vector.tensor_reduce(fwt[:, 2:3], fw[:], AX, ALU.add))
        own(nc.vector.reciprocal(fwt[:, 3:4], fwt[:, 2:3]))
        own(nc.vector.tensor_scalar(fw[:], fw[:], fwt[:, 3:4], None, ALU.mult))
        nc.vector.tensor_tensor(wind[0:QR], fw[0:QR], rowind[0:QR], ALU.mult)

        def scales(layer, cols):
            own(nc.vector.tensor_scalar(big[:, layer, cols], big[:, layer, cols], 1e-30, None, ALU.max))
            own(nc.vector.tensor_scalar(pw[:, layer, cols].bitcast(U32), big[:, layer, cols].bitcast(U32), 0x7F800000, None,
                                        ALU.bitwise_and))
            own(nc.vector.reciprocal(sc[:, layer, cols], pw[:, layer, cols]))
            own(nc.vector.tensor_scalar(sc[:, layer, cols], sc[:, layer, cols], 2.0 ** 14, None, ALU.mult))
            own(nc.vector.tensor_scalar(inv[:, layer, cols], pw[:, layer, cols], 2.0 ** -14, None, ALU.mult))

        dve.wait_ge(s_rall, 1)
        for l in range(2):
            scales(l, slice(3, 4))
            nc.vector.tensor_scalar(inv_l[:, l:l + 1], inv[:, l, 3:4], 2.0 ** -XSCALE_LOG, None, ALU.mult)
            own(nc.vector.tensor_scalar(Rh[:, l, :], rstage[:, l, :], sc[:, l, 3:4], None, ALU.mult))
            m = nc.vector.scalar_tensor_tensor(out=Rl[:, l, :], in0=rstage[:, l, :], scalar=sc[:, l, 3:4], in1=Rh[:, l, :],
                                               op0=ALU.mult, op1=ALU.subtract)
        m.then_inc(s_rscale, 1)

        def blocks(layer, g):
            ks = InLoop(4 if layer == 0 else 2)

            def moments(b, src, scale, order):
                for s in range(BSUB):
                    m = nc.vector.bn_stats(stats[b][:, s, :], src(s))
                ks.mark(m)
                ks.wait(alone=True)
                for s in range(BSUB):
                    m = nc.vector.bn_aggr(mv[b][:, s, :], stats[b][:, s, :])
                ks.mark(m)
                ks.wait()
                nc.vector.tensor_scalar(ve[b][:], mv[b][:, :, 1], EPS, scale, ALU.add, ALU.mult).then_inc(s_var, 1)
                dve.wait_ge(s_rstd, order + 1)

            def step(i, j):
                b = j % 2
                n = a0(layer, g) + i
                ks.at(i)
                if layer == 0:
                    loaded, per = 48 * (a0(0, g) // 2 + 1), 24
                else:
                    loaded, per = 48 * NG * GBLK // 2 + 16 * (g * GBLK // 2 + 1), 8
                dve.wait_ge(ld_a[b], loaded + (i - j) * per).then_inc(s_alone, 1)

                def row(s):
                    return X[:, bass.ds((g * GBLK + i) * BSUB + s, 1), :].rearrange("p a d -> p (a d)")

                rows4 = X[:, bass.ds((g * GBLK + i) * BSUB, BSUB), :]
                rorder = 2 * n if layer == 0 else 2 * a0(1, 0) + (n - a0(1, 0))
                if layer == 0:
                    moments(b, row, 1.0, rorder)
                    need(dve, s_at, n - 1)
                    for s in range(BSUB):
                        m = nc.vector.tensor_scalar(xn[b][:, s, :], row(s), mv[b][:, s, 0:1], rstd[b][:, s:s + 1],
                                                    ALU.subtract, ALU.mult)
                    m.then_inc(s_xn, 1)
                    dve.wait_ge(s_conv, n + 1)
                    nc.vector.tensor_tensor(rows4, rows4, bk[4][:].rearrange("p (s d) -> p s d", s=BSUB), ALU.add
                                            ).then_inc(s_x1, 1)
                    dve.wait_ge(s_x1, n + 1).then_inc(s_alone, 1)
                    rorder = rorder + 1
                moments(b, row, 2.0 ** (-2 * XSCALE_LOG), rorder)
                for s in range(BSUB):
                    m = nc.vector.tensor_scalar(xs[b][:, s, :], row(s), mv[b][:, s, 0:1], rstd[b][:, s:s + 1],
                                                ALU.subtract, ALU.mult)
                m.then_inc(s_vx, 1)
                dve.wait_ge(s_vx, n + 1)
                hi = R[:, bass.ds((g * GBLK + i) * BSUB, BSUB), 0:D]
                nc.vector.tensor_copy(hi, xs[b][:]).then_inc(s_vh, 1)
                dve.wait_ge(s_vh, n + 1)
                nc.vector.tensor_tensor(R[:, bass.ds((g * GBLK + i) * BSUB, BSUB), D:2 * D], xs[b][:], hi, ALU.subtract
                                        ).then_inc(s_rows, 1)
            loop(dve, GBLK, 2, step, head=(layer, g) == (0, 0))
            ks.end(GBLK)

        def gate(layer, g):
            c = layer * NG + g
            J = 2 * GSUB
            dve.wait_ge(s_log, a0(layer, g) + GBLK)
            nc.vector.tensor_scalar(lg[:].rearrange("p s e -> p (s e)"), bk[7][:, 0:GSUB * EXPERTS], inv_l[:, layer:layer + 1],
                                    None, ALU.mult).then_inc(s_lgr, 1)
            dve.wait_ge(s_lgr, c + 1)
            if layer == 1:
                own(nc.vector.tensor_tensor(lg[:], lg[:], gate_bias[:].unsqueeze(1).broadcast_to([P, GSUB, EXPERTS]), ALU.add))
            src = lg
            for k in range(2):
                own(nc.vector.tensor_reduce(top[:, k, :], src[:], AX, ALU.max))
                own(nc.vector.tensor_tensor(keyed[:], src[:], top[:, k, :].unsqueeze(2).broadcast_to([P, GSUB, EXPERTS]),
                                            ALU.is_equal))
                own(nc.vector.tensor_tensor(keyed[:], keyed[:], rankkey[:].unsqueeze(1).broadcast_to([P, GSUB, EXPERTS]),
                                            ALU.mult))
                own(nc.vector.tensor_reduce(kmax[:], keyed[:], AX, ALU.max))
                m = nc.vector.tensor_tensor(sel[:, k], keyed[:], kmax[:].unsqueeze(2).broadcast_to([P, GSUB, EXPERTS]),
                                            ALU.is_equal)
                if k == 0:
                    own(m)
                    own(nc.vector.scalar_tensor_tensor(out=lg2[:], in0=sel[:, 0], scalar=-1e30, in1=lg[:], op0=ALU.mult,
                                                       op1=ALU.add))
                    src = lg2
            m.then_inc(s_sel, 1)
            nc.vector.tensor_tensor(den[:], top[:, 1, :], top[:, 0, :], ALU.subtract).then_inc(s_diff, 1)
            dve.wait_ge(s_tot, c + 1)
            own(nc.vector.tensor_copy(tot[:], bk[0][0:J, 0:EXPERTS]))
            nc.vector.tensor_tensor(totm[:], tot[:].unsqueeze(1).broadcast_to([J, J, EXPERTS]),
                                    upper[0:J, 0:J].unsqueeze(2).broadcast_to([J, J, EXPERTS]), ALU.mult).then_inc(s_totm, 1)
            dve.wait_ge(s_exp, c + 1)
            own(nc.vector.tensor_scalar(den[:], expd[:], 1.0, None, ALU.add))
            own(nc.vector.reciprocal(PW[g][:, 0, :], den[:]))
            nc.vector.tensor_tensor(PW[g][:, 1, :], PW[g][:, 0, :], expd[:], ALU.mult)
            dve.wait_ge(s_rank, c + 1)
            own(nc.vector.tensor_scalar(cnt[:], bk[2][:, 0:EXPERTS], float(TS - 1), None, ALU.add))
            own(nc.vector.tensor_copy(cnti[:], cnt[:]))
            own(nc.vector.tensor_scalar(cnti[:], cnti[:], TS.bit_length() - 1, None, ALU.logical_shift_right))
            own(nc.vector.tensor_copy(ntile[:], cnti[:]))
            prev = ntile
            for k in range(3):
                w = 1 << k
                nc.vector.tensor_copy(scan[k][:, 0:w], prev[:, 0:w])
                own(nc.vector.tensor_tensor(scan[k][:, w:], prev[:, w:], prev[:, 0:EXPERTS - w], ALU.add))
                prev = scan[k]
            own(nc.vector.tensor_tensor(start[:], prev[:], ntile[:], ALU.subtract))
            own(nc.vector.tensor_scalar(start[:], start[:], float(TS), None, ALU.mult))
            own(nc.vector.tensor_tensor(selw[:], bk[1][:, 0:J * EXPERTS].rearrange("p (j e) -> p j e", e=EXPERTS),
                                        start[:].unsqueeze(1).broadcast_to([P, J, EXPERTS]), ALU.add))
            own(nc.vector.tensor_tensor(selw[:], selw[:], sel[:].rearrange("p k s e -> p (k s) e"), ALU.mult))
            own(nc.vector.tensor_reduce(posf[:], selw[:], AX, ALU.add))
            nc.vector.tensor_copy(POS[g][:], posf[:])
            own(nc.vector.tensor_tensor(tcmp[:], tileno[:].unsqueeze(2).broadcast_to([1, TILES, EXPERTS]),
                                        prev[0:1].unsqueeze(1).broadcast_to([1, TILES, EXPERTS]), ALU.is_ge))
            own(nc.vector.tensor_reduce(texp[:], tcmp[:], AX, ALU.add))
            own(nc.vector.tensor_scalar(texp[:], texp[:], float(EXPERTS - 1), None, ALU.min))
            nc.vector.tensor_copy(EXP[g][:], texp[:]).then_inc(s_route, 1)

        def prep(layer):
            ps = pieces(layer)
            for r, (k, o, n) in enumerate(ps):
                p = piece0(layer, 0) + r
                dve.wait_ge(ld_w[p % 2], 16 * (p // 2 + 1))
                nc.vector.tensor_reduce(wmax[:, r:r + 1], wstage[p % 2][:, 0:n], AX, ALU.max, apply_absolute_value=True
                                        ).then_inc(s_wfree, 1)
            dve.wait_ge(s_wfree, piece0(layer, 1))
            half = len(ps) // 2
            for k in range(2):
                nc.vector.tensor_reduce(big[:, layer, k:k + 1], wmax[:, k * half:(k + 1) * half], AX, ALU.max)
            dve.wait_ge(ld_b1, 16 * (layer + 1))
            nc.vector.tensor_reduce(big[:, layer, 2:3], b1all[:, 0:NE[layer]].rearrange("p e c -> p (e c)"), AX, ALU.max,
                                    apply_absolute_value=True).then_inc(s_prep, 1)
            dve.wait_ge(s_prepall, layer + 1)
            own(nc.vector.scalar_tensor_tensor(out=big[:, layer, 2:3], in0=big[:, layer, 0:1], scalar=float(D),
                                               in1=big[:, layer, 2:3], op0=ALU.mult, op1=ALU.add))
            scales(layer, slice(0, 3))
            nc.vector.tensor_scalar(inv_z[:, layer:layer + 1], inv[:, layer, 0:1], 2.0 ** -XSCALE_LOG, None, ALU.mult)
            nc.vector.tensor_tensor(inv_y[:, layer:layer + 1], inv[:, layer, 1:2], inv[:, layer, 2:3], ALU.mult
                                    ).then_inc(s_scale, 1)
            for r, (k, o, n) in enumerate(ps):
                p = piece0(layer, 1) + r
                hi, lo = ((W1h, W1l), (W2h, W2l))[k]
                dve.wait_ge(s_whi, layer * len(pieces(0)) + r + 1)
                nc.vector.scalar_tensor_tensor(out=lo[:, o:o + n], in0=wstage[p % 2][:, 0:n], scalar=sc[:, layer, k:k + 1],
                                               in1=hi[:, o:o + n], op0=ALU.mult, op1=ALU.subtract).then_inc(s_wfree, 1)

        def tiles(base, n_tiles, layer, shared, g, first):
            def step(i, j):
                b = j % 2
                n = base + i
                for half in range(2):
                    cs = slice(2 * half, 2 * half + 2)
                    dve.wait_ge(s_act, 2 * n + half + 1)
                    if half == 0:
                        need(dve, s_yp, n - 1)
                    nc.vector.tensor_scalar(hh[b][:, cs], h32[b][:, cs], sc[:, layer, 2:3], None, ALU.mult).then_inc(s_hh, 1)
                    dve.wait_ge(s_hh, 2 * n + half + 1)
                    nc.vector.scalar_tensor_tensor(out=hl[b][:, cs], in0=h32[b][:, cs], scalar=sc[:, layer, 2:3],
                                                   in1=hh[b][:, cs], op0=ALU.mult, op1=ALU.subtract).then_inc(s_hl, 1)
                dve.wait_ge(s_yp, n + 1)
                y = ytmp[j % 4]
                bias = BBs if shared else BB[j % 4]
                if not shared:
                    r0 = (base - NG * STILES) // 4
                    need(dve, s_st[j % 4], 16 * (r0 + i // 4) if isinstance(i, int) else 16 * r0 + (i - j) * 4)
                nc.vector.scalar_tensor_tensor(out=y[:], in0=bk[6 + b][:, 0:TSUB * D].rearrange("p (s d) -> p s d", s=TSUB),
                                               scalar=inv_y[:, layer:layer + 1],
                                               in1=bias[:, CH:].unsqueeze(1).broadcast_to([P, TSUB, D]),
                                               op0=ALU.mult, op1=ALU.add).then_inc(s_y, 1)
                if shared:
                    rows = X[:, bass.ds(g * GSUB + i * TSUB, TSUB), :]
                    dve.wait_ge(s_y, n + 1)
                    nc.vector.tensor_tensor(rows, rows, y[:], ALU.add).then_inc(s_xsh, 1)
            loop(dve, n_tiles, 4, step, head=first)

        def combine(layer, g):
            def step(i, j):
                b = j % 4
                r0 = (layer * NG + g) * GSUB // 4
                dve.wait_ge(s_g[b], 32 * (r0 + 1) + (i - j) * 8)
                row = X[:, bass.ds(g * GSUB + i, 1), :].rearrange("p a d -> p (a d)")
                nc.vector.scalar_tensor_tensor(out=row, in0=G[b][:, 0, :], scalar=PW[g][:, 0, bass.ds(i, 1)], in1=row,
                                               op0=ALU.mult, op1=ALU.add).then_inc(s_half, 1)
                dve.wait_ge(s_half, (layer * NG + g) * GSUB + i + 1)
                nc.vector.scalar_tensor_tensor(out=row, in0=G[b][:, 1, :], scalar=PW[g][:, 1, bass.ds(i, 1)], in1=row,
                                               op0=ALU.mult, op1=ALU.add).then_inc(s_comb, 1)
            loop(dve, GSUB, 4, step, head=(layer, g) == (0, 0))

        def quads(g):
            ks = InLoop(9)

            def bc(ap, n):
                return ap.unsqueeze(2).broadcast_to([QR, NGRP, n])

            def front(i, j):
                b = j % 2
                n = q0(g) + i
                dve.wait_ge(ld_q[b], 16 * (QB + 1) * (q0(g) // 2 + 1) + (i - b) * (8 * (QB + 1)))
                ks.mark(nc.vector.tensor_tensor(a25[0:QR], Aq[b][0:QR], self25[0:QR], ALU.add))
                nc.vector.bn_stats(qst[b][0:QR, 0:6], xq[b][0:QR, :])
                ks.wait()
                ks.mark(nc.vector.tensor_tensor(am[b][0:QR], a25[0:QR].unsqueeze(1).broadcast_to([QR, NGRP, LIVE]),
                                                indc[0:QR], ALU.mult))
                ks.wait(alone=True)
                nc.vector.bn_aggr(qst[b][0:QR, 6:8], qst[b][0:QR, 0:6])
                ks.mark(nc.vector.tensor_reduce(deg[b][0:QR], am[b][0:QR], AX, ALU.add))
                ks.wait()
                ks.mark(nc.vector.tensor_scalar(isz[b][0:QR], deg[b][0:QR], 0.0, None, ALU.is_equal))
                nc.vector.tensor_scalar(qv[b][0:QR, NGRP:NGRP + 1], qst[b][0:QR, 7:8], EPS, None, ALU.add)
                ks.wait()
                nc.vector.tensor_tensor(qv[b][0:QR, 0:NGRP], deg[b][0:QR], isz[b][0:QR], ALU.add).then_inc(s_qv, 1)
                ks.mark(nc.vector.tensor_scalar(isz[b][0:QR], isz[b][0:QR], -1.0, 1.0, ALU.mult, ALU.add))
                dve.wait_ge(s_qp, n + 1)
                need(dve, s_qa, n - 1)
                nc.vector.tensor_scalar(xqn[b][0:QR], xq[b][0:QR], qst[b][0:QR, 6:7], qp[b][0:QR, NGRP:NGRP + 1],
                                        ALU.subtract, ALU.mult).then_inc(s_qn, 1)
                ks.wait()
                ks.mark(nc.vector.tensor_tensor(dinv[b][0:QR], qp[b][0:QR, 0:NGRP], isz[b][0:QR], ALU.mult))
                ks.wait()
                ks.mark(nc.vector.tensor_tensor(am[b][0:QR], am[b][0:QR], bc(dinv[b][0:QR], LIVE), ALU.mult))
                ks.wait()
                need(dve, s_nt, n - 1)
                for k in range(QB):
                    m = nc.vector.tensor_scalar(nb[b][0:QR, :, k, :], am[b][0:QR], diagq[0:QR, k:k + 1], None, ALU.mult)
                m.then_inc(s_nb, 1)
                dve.wait_ge(s_nt, n + 1)
                need(dve, s_o2, n - 1)
                nc.vector.tensor_tensor(NT[b][0:QR], bk[0][0:QR, 0:NGRP * QR].rearrange("p (g n) -> p g n", g=NGRP),
                                        bc(dinv[b][0:QR], QR), ALU.mult).then_inc(s_ntc, 1)

            def back(i, j):
                b = j % 2
                n = q0(g) + i
                dve.wait_ge(s_o2, n + 1)
                nc.vector.tensor_tensor(qt[0:QR, 0:4, :], bk[6][0:QR, :].rearrange("p (g d) -> p g d", g=4), gb2[0:QR, 0:4, :],
                                        ALU.add)
                nc.vector.tensor_tensor(qt[0:QR, 4, :], bk[7][0:QR, 0:D], gb2[0:QR, 4, :], ALU.add).then_inc(s_o2r, 1)
                dve.wait_ge(s_o2r, n + 1)
                ks.mark(nc.vector.scalar_tensor_tensor(out=qt2[0:QR], in0=qt[0:QR], scalar=0.0,
                                                       in1=wind[0:QR].unsqueeze(2).broadcast_to([QR, NGRP, D]),
                                                       op0=ALU.max, op1=ALU.mult))
                ks.wait()
                ks.mark(nc.vector.tensor_reduce(qsum[0:QR], qt2[0:QR].rearrange("p g d -> p d g"), AX, ALU.add))
                ks.wait()
                r0 = 16 * QB * (q0(g) // 2)
                need(dve, s_qst[b], (r0 + 16 * QB * (i // 2)) if isinstance(i, int) else r0 + (i - j) * 8 * QB)
                nc.vector.tensor_tensor(xo[b][0:QR], xq[b][0:QR], qsum[0:QR], ALU.add).then_inc(s_xo, 1)

            def step(i, j, last=False):
                ks.at(i)
                ks.first = ks.first + 7
                ks.k = 0
                if not last:
                    front(i + 1, j + 1)
                else:
                    ks.k = 0
                    ks.first = ks.first - 7 + 0
                back(i, j)

            ks.at(0)
            front(0, 0)
            assert ks.k == 7

            first = 0
            if g == 0:
                step(0, 0)
                step(1, 1)
                first = 1
            with dve.Fori(first, GQ // 2 - 1) as q:
                for j in range(2):
                    step(q * 2 + j, j)
            step(GQ - 2, 0)
            ks.first = ks.base + 7 + (GQ - 1) * 9
            ks.k = 0
            back(GQ - 1, 1)
            count[0] = ks.base + 9 * GQ

        for g in range(NG):
            blocks(0, g)
            gate(0, g)
        prep(0)
        for g in range(NG):
            tiles(g * STILES, STILES, 0, True, g, g == 0)
        for g in range(NG):
            tiles(e0(0, g), TILES, 0, False, g, g == 0)
            combine(0, g)
        prep(1)
        for g in range(NG):
            quads(g)
            blocks(1, g)
            gate(1, g)
        for g in range(NG):
            tiles(e0(1, g), TILES, 1, False, g, False)
            combine(1, g)


def kernel(**inputs):
    import concourse.bacc as _bacc
    from concourse import mybir as _mybir
    from concourse.bass_utils import run_bass_kernel_spmd as _run

    a = {k: np.asarray(x) for k, x in inputs.items()}
    c = np.ascontiguousarray

    def biases(b1, b2):
        n = b1.shape[0]
        return c(np.concatenate([b1.reshape(n, CH, P).transpose(0, 2, 1),
                                 np.broadcast_to(b2[:, None, :], (n, P, D))], axis=2))

    def chunks(w):
        return c(w.reshape(w.shape[0], CH, P, D).transpose(2, 0, 1, 3))

    member = np.zeros((NGRP, LIVE), np.float32)
    for k, nodes in enumerate(GRPS):
        member[k, nodes] = 1.0
    node = np.arange(QR) % LIVE
    graph = np.arange(QR) // LIVE
    arrays = {
        "x": a["x"].reshape(TOKENS, D),
        "adj2": a["adj"].reshape(SUBS, P, NODES),
        "adj25": c(a["adj"][:, :LIVE, :LIVE]).reshape(GRAPHS * LIVE, LIVE),
        "gnn_w": a["L0_gnn_weight"],
        "gnn_b": a["L0_gnn_bias"].reshape(1, D),
        "wr0": a["L0_ffn_Wr"],
        "wr1": c(a["L1_ffn_Wg"].T),
        "bg": a["L1_ffn_bg"].reshape(1, EXPERTS),
        "w1_0": c(np.concatenate([a["L0_ffn_W1p"], a["L0_ffn_W1s"][None]]).transpose(1, 0, 2)).reshape(P, -1),
        "w2_0": chunks(np.concatenate([a["L0_ffn_W2p"], a["L0_ffn_W2s"][None]])).reshape(P, -1),
        "bb0": biases(np.concatenate([a["L0_ffn_b1p"], a["L0_ffn_b1s"][None]]),
                      np.concatenate([a["L0_ffn_b2p"], a["L0_ffn_b2s"][None]])),
        "w1_1": c(a["L1_ffn_W1"].transpose(2, 0, 1)).reshape(P, -1),
        "w2_1": chunks(c(a["L1_ffn_W2"].transpose(0, 2, 1))).reshape(P, -1),
        "bb1": biases(a["L1_ffn_b1"], a["L1_ffn_b2"]),
        "gW1": c(a["L1_gnn_W1"].transpose(1, 0, 2)),
        "gW2": c(a["L1_gnn_W2"].reshape(NGRP, 2, P, D).transpose(2, 0, 1, 3)),
        "gb1": c(a["L1_gnn_b1"].reshape(NGRP, 2, P).transpose(2, 0, 1)),
        "gb2": a["L1_gnn_b2"].reshape(1, NGRP * D),
        "fusion": a["L1_gnn_fusion_w"].reshape(1, NGRP),
        "indc": c((member[:, node].T[:, :, None] * member[None]).reshape(QR, NGRP * LIVE)),
        "rowind": c(member[:, node].T),
        "self25": c(np.eye(LIVE, dtype=np.float32)[node]),
        "diagq": c(np.eye(QB, dtype=np.float32)[graph]),
    }
    nc = _bacc.Bacc("TRN2", target_bir_lowering=False, num_devices=1)
    t = {k: nc.dram_tensor(f"in_{k}", x.shape, _mybir.dt.from_np(x.dtype), kind="ExternalInput").ap()
         for k, x in arrays.items()}
    out = nc.dram_tensor("out_0", (TOKENS, D), F32, kind="ExternalOutput").ap()
    program(nc, t, out)
    r = _run(nc, [{f"in_{k}": x for k, x in arrays.items()}], core_ids=[0])
    return r.results[0]["out_0"].reshape(GRAPHS, NODES, D)
```

```python
from contextlib import ExitStack

import numpy as np

import concourse.bass as bass
from concourse import mybir

F32 = mybir.dt.float32
F16 = mybir.dt.float16
BF16 = mybir.dt.bfloat16
I32 = mybir.dt.int32
U32 = mybir.dt.uint32
ALU = mybir.AluOpType
ACT = mybir.ActivationFunctionType
AX = mybir.AxisListType.X
ABSMAX = bass.bass_isa.ReduceOp.absmax

P = 128
D = 128
NODES = 64
GRAPHS = 128
TOKENS = GRAPHS * NODES
SUBS = TOKENS // P
NG = 2
GSUB = SUBS // NG
BSUB = 4
GBLK = GSUB // BSUB
EXPERTS = 8
HID = 512
CH = HID // P
TS = 256
TSUB = TS // P
TILES = -(-(2 * GSUB * P // TS + EXPERTS - 1) // 4) * 4
STILES = GSUB * P // TS
GROWS = TILES * TS
EPS = 1e-5
XSCALE_LOG = 10
GRPS = [list(range(25)), list(range(9)), [0] + list(range(9, 15)), [6, 7, 8, 12, 13, 14], [3, 4, 5, 9, 10, 11]]
NGRP = len(GRPS)
LIVE = 25
QB = 4
QR = QB * LIVE
GQ = GRAPHS // NG // QB
QH = GQ // 2
GHID = 256
NE = [EXPERTS + 1, EXPERTS]
WP = 2 * HID


def pieces(layer):
    n = NE[layer] * HID
    return [(k, o, min(WP, n - o)) for k in range(2) for o in range(0, n, WP)]


def need(eng, sem, value):
    if not isinstance(value, int) or value > 0:
        eng.wait_ge(sem, value)


def loop(eng, n, unroll, step, head=False, tail=False):
    lo = unroll if head else 0
    hi = n - unroll if tail else n
    for i in range(lo):
        step(i, i)
    if hi > lo:
        with eng.Fori(lo // unroll, hi // unroll) as q:
            for j in range(unroll):
                step(q * unroll + j, j)
    for i in range(max(hi, lo), n):
        step(i, i % unroll)


def program(nc, t, out):
    ctx = ExitStack()
    with ctx:
        build(nc, ctx, t, out)


def build(nc, ctx, t, out):
    def sb(name, shape, dt=F32):
        return ctx.enter_context(nc.sbuf_tensor("sb_" + name, shape, dt))

    def sem(name):
        return ctx.enter_context(nc.semaphore(name))

    sorted_rows = [nc.dram_tensor(f"sorted_rows{g}", (GROWS, 2 * D), F16, kind="Internal").ap() for g in range(NG)]
    expert_rows = [nc.dram_tensor(f"expert_rows{g}", (GROWS, D), F32, kind="Internal").ap() for g in range(NG)]

    ident = sb("ident", [P, P])
    ident16 = sb("ident16", [P, P], F16)
    upper = sb("upper", [P, P], BF16)
    ones16 = sb("ones16", [P, P], BF16)
    neghalf = sb("neghalf", [P, QH * (NGRP + 1)])
    rankkey = sb("rankkey", [P, EXPERTS])
    tileno = sb("tileno", [1, TILES])
    ones_row = sb("ones_row", [1, P])
    zeros = sb("zeros", [P, 512], F16)
    X = sb("X", [P, SUBS, D])
    R = sb("R", [P, SUBS, 2 * D], F16)
    W1h = sb("W1h", [P, NE[0] * HID], F16)
    W1l = sb("W1l", [P, NE[0] * HID], F16)
    W2h = sb("W2h", [P, NE[0] * HID], F16)
    W2l = sb("W2l", [P, NE[0] * HID], F16)
    wstage = [sb(f"wstage{k}", [P, WP]) for k in range(2)]
    parked = ([w[:] for w in wstage]
              + [x[:, k * WP:(k + 1) * WP] for x in (X[:, GSUB:].rearrange("p s d -> p (s d)"),
                                                     R[:, GSUB:].rearrange("p s d -> p (s d)").bitcast(F32))
                 for k in range(GSUB * D // WP)])
    wmax = sb("wmax", [P, 16])
    b1all = sb("b1all", [P, NE[0], CH])
    rstage = sb("rstage", [P, 2, EXPERTS])
    Rh = sb("Rh", [P, 2, EXPERTS], F16)
    Rl = sb("Rl", [P, 2, EXPERTS], F16)
    gate_bias = sb("gate_bias", [P, EXPERTS])
    big = sb("big", [P, 2, 4])
    pw = sb("pw", [P, 2, 4])
    sc = sb("sc", [P, 2, 4])
    inv = sb("inv", [P, 2, 4])
    inv_z = sb("inv_z", [P, 2])
    inv_y = sb("inv_y", [P, 2])
    inv_l = sb("inv_l", [P, 2])
    Wg = sb("Wg", [P, D])
    bg4 = sb("bg4", [1, BSUB, D])
    AB = [sb(f"AB{b}", [P, BSUB, P]) for b in range(2)]
    aT2 = sb("aT", [P, 2, BSUB * P])
    aT = [aT2[:, b, :] for b in range(2)]
    xn2 = sb("xn", [P, 2, BSUB, D])
    xn = [xn2[:, b] for b in range(2)]
    stats = [[sb(f"stats{m}{b}", [P, BSUB, 6]) for b in range(2)] for m in range(2)]
    mv = [[sb(f"mv{m}{b}", [P, BSUB, 2]) for b in range(2)] for m in range(2)]
    ve = [[sb(f"ve{m}{b}", [P, BSUB]) for b in range(2)] for m in range(2)]
    rstd = [[sb(f"rstd{m}{b}", [P, BSUB]) for b in range(2)] for m in range(2)]
    xs = [sb(f"xs{b}", [P, BSUB, D]) for b in range(2)]
    RT = [sb(f"RT{b}", [P, 2, BSUB * P], F16) for b in range(2)]
    lg = sb("lg", [P, GSUB, EXPERTS])
    lg2 = sb("lg2", [P, GSUB, EXPERTS])
    keyed = sb("keyed", [P, GSUB, EXPERTS])
    top = sb("top", [P, 2, GSUB])
    kmax = sb("kmax", [P, GSUB])
    sel = sb("sel", [P, 2, GSUB, EXPERTS], BF16)
    selw = sb("selw", [P, 2 * GSUB, EXPERTS])
    tot = sb("tot", [2 * GSUB, EXPERTS], BF16)
    totm = sb("totm", [2 * GSUB, 2 * GSUB, EXPERTS], BF16)
    cnt = sb("cnt", [P, EXPERTS])
    cnti = sb("cnti", [P, EXPERTS], I32)
    ntile = sb("ntile", [P, EXPERTS])
    scan = [sb(f"scan{k}", [P, EXPERTS]) for k in range(3)]
    start = sb("start", [P, EXPERTS])
    posf = sb("posf", [P, 2 * GSUB])
    POS = [sb(f"POS{g}", [P, 2 * GSUB], U32) for g in range(NG)]
    PW = [sb(f"PW{g}", [P, 2, GSUB]) for g in range(NG)]
    expd = sb("expd", [P, GSUB])
    den = sb("den", [P, GSUB])
    tcmp = sb("tcmp", [1, TILES, EXPERTS])
    texp = sb("texp", [1, TILES])
    EXP = [sb(f"EXP{g}", [1, TILES], I32) for g in range(NG)]
    XR = [sb(f"XR{b}", [P, TSUB, 2 * D], F16) for b in range(4)]
    BB = [sb(f"BB{b}", [P, CH + D]) for b in range(4)]
    BBs = sb("BBs", [P, CH + D])
    XTt = [sb(f"XTt{b}", [P, 2, TS], F16) for b in range(2)]
    h32all = sb("h32", [P, 2, CH, TS])
    h32 = [h32all[:, b] for b in range(2)]
    halves = sb("halves", [P, 2, 2, CH, TS], F16)
    hh = [halves[:, 0, b] for b in range(2)]
    hl = [halves[:, 1, b] for b in range(2)]
    ytmp = [sb(f"ytmp{b}", [P, TSUB, D]) for b in range(4)]
    G = [sb(f"G{b}", [P, 2, D]) for b in range(4)]
    gW1 = sb("gW1", [P, NGRP, GHID])
    gW2 = sb("gW2", [P, NGRP, 2, D])
    gb1 = sb("gb1", [P, NGRP, 2])
    gb2 = sb("gb2", [P, NGRP, D])
    indc = sb("indc", [P, NGRP, LIVE])
    self25 = sb("self25", [P, LIVE])
    diagq = sb("diagq", [P, QB])
    wind = sb("wind", [P, NGRP])
    fw = sb("fw", [P, NGRP])
    fwt = sb("fwt", [P, 4])
    rowind = sb("rowind", [P, NGRP])
    qst = sb("qst", [P, GQ, 8])
    qv = sb("qv", [P, GQ, NGRP + 1])
    qp = sb("qp", [P, GQ, NGRP + 1])
    deg = sb("deg", [P, GQ, NGRP])
    isz = sb("isz", [P, GQ, NGRP])
    dinv = sb("dinv", [P, GQ, NGRP])
    xqn = [sb(f"xqn{b}", [P, D]) for b in range(2)]
    qaT = sb("qaT", [P, NGRP, QR])
    s2 = sb("s2", [P, NGRP, D])
    qt2 = sb("qt2", [P, NGRP, D])
    qsum = sb("qsum", [P, D])
    xq = h32all[:].rearrange("p b c t -> p (b c t)").rearrange("p (q d) -> p q d", d=D)
    Aq = [ytmp[b][:].rearrange("p s d -> p (s d)")[:, 0:QH * LIVE].rearrange("p (q m) -> p q m", q=QH) for b in range(2)]
    am = halves[:].rearrange("p h b c t -> p (h b c t)").bitcast(F32).rearrange("p (q n) -> p q n", q=GQ)
    nb = [AB[b][:].rearrange("p s m -> p (s m)")[:, 0:NGRP * QR].rearrange("p (g b m) -> p g b m", g=NGRP, b=QB)
          for b in range(2)]
    NT = [x[:, 0:NGRP * QR].rearrange("p (g n) -> p g n", g=NGRP)
          for x in [xs[b][:].rearrange("p s d -> p (s d)") for b in range(2)]
          + [RT[b][:].rearrange("p h t -> p (h t)").bitcast(F32) for b in range(2)]]
    h1T = aT2[:].rearrange("p b n -> p (b n)")[:, 0:2 * NGRP * QR].rearrange("p (c g n) -> p c g n", c=2, g=NGRP)
    qt = xn2[:].rearrange("p b s d -> p (b s) d")[:, 0:NGRP, :]

    bk = [ctx.enter_context(nc.psum_tensor(f"bank{k}", [P, 512], F32)) for k in range(8)]

    ld_small = sem("small_loaded")
    ld_w = [sem(f"weights_loaded{k}") for k in range(2)]
    s_const = sem("constants_made")
    s_vconst = sem("vector_constants_made")
    s_zero = [sem(f"sorted_rows_zeroed{g}") for g in range(NG)]
    s_rmax = sem("router_reduced")
    s_rall = sem("router_max_everywhere")
    s_rscale = sem("router_scaled")
    s_fusx = sem("fusion_exp")
    s_prep = sem("prep_reduced")
    s_prepall = sem("prep_max_everywhere")
    s_scale = sem("weights_scales_ready")
    s_whi = sem("weights_hi_ready")
    s_wfree = sem("weights_piece_used")
    ld_b1 = sem("hidden_biases_loaded")
    ld_g = sem("grouped_weights_loaded")
    v = sem("vector_step")
    ld_a = [sem(f"block_loaded{b}") for b in range(2)]
    s_var = [sem("variance_ready"), sem("sum_variance_ready")]
    s_rstd = [sem("rstd_ready"), sem("sum_rstd_ready")]
    s_xn = sem("normalised")
    s_at = sem("aggregated")
    s_atc = sem("aggregated_copied")
    s_conv = sem("convolved")
    s_x1 = sem("residual_added")
    s_rows = sem("rows_split")
    s_rt = sem("rows_transposed")
    s_rtc = sem("rowsT_copied")
    s_log = sem("logits_ready")
    s_lgr = sem("logits_read")
    s_sel = sem("selected")
    s_tot = sem("totals_ready")
    s_totm = sem("totals_masked")
    s_rank = sem("ranks_ready")
    s_diff = sem("logit_difference")
    s_exp = sem("gate_exp")
    s_route = sem("routes_ready")
    s_scat = [sem(f"rows_scattered{g}") for g in range(NG)]
    s_xr = [sem(f"tile_rows_loaded{b}") for b in range(4)]
    s_bb = [sem(f"tile_biases_loaded{b}") for b in range(4)]
    s_tt = sem("tile_transposed")
    s_ttc = sem("tileT_copied")
    s_h = sem("hidden_ready")
    s_act = sem("hidden_activated")
    s_hh = sem("hidden_hi")
    s_hl = sem("hidden_split")
    s_yp = sem("expert_out_ready")
    s_y = sem("expert_out_scaled")
    s_xsh = sem("shared_added")
    s_st = [sem(f"expert_rows_stored{b}") for b in range(4)]
    s_g = [sem(f"rows_gathered{b}") for b in range(4)]
    s_comb = sem("combined")
    ld_q = [sem(f"quad_loaded{b}") for b in range(2)]
    s_qv = sem("degrees_ready")
    s_qp = sem("degree_roots_ready")
    s_qn = sem("quad_normalised")
    s_nb = sem("norm_rows_ready")
    s_nt = sem("norm_transposed")
    s_ntc = sem("normT_ready")
    s_qa = sem("quad_aggregated")
    s_qac = sem("quad_aggregated_copied")
    s_h1 = sem("quad_hidden")
    s_h1c = sem("quad_hidden_activated")
    s_s2 = sem("quad_support")
    s_s2c = sem("quad_support_copied")
    s_o2 = sem("quad_out")
    s_o2r = sem("quad_out_read")
    s_xo = sem("quad_added")
    s_qst = [sem(f"quad_stored{b}") for b in range(2)]
    s_out = sem("outputs_stored")
    s_alone = sem("waits_alone")
    s_vx = sem("rows_normalised")
    s_vh = sem("rows_hi")
    s_half = sem("half_combined")

    block = ctx.enter_context(nc.Block())

    def a0(layer, g):
        return (layer * NG + g) * GBLK

    PHASES = [("A", 0, 0), ("M", 0, 0), ("R", 0, 0), ("W", 0, 0), ("S", 0, 0), ("A", 0, 1), ("R", 0, 1), ("E", 0, 0),
              ("S", 0, 1), ("E", 0, 1), ("W", 1, 0), ("Q", 1, 0), ("A", 1, 0), ("R", 1, 0), ("Q", 1, 1),
              ("A", 1, 1), ("R", 1, 1), ("E", 1, 0), ("E", 1, 1), ("C", 1, 1)]
    rides = {("E", 0, 1): (0, 0), ("Q", 1, 0): (0, 1), ("E", 1, 1): (1, 0)}

    def before(kinds, phase):
        return [p for p in PHASES[:PHASES.index(phase)] if p[0] in kinds]

    def t0(phase):
        return sum(STILES if p[0] == "S" else TILES for p in before("SE", phase))

    def r0(phase):
        return len(before("E", phase)) * TILES // 4

    def c0(layer, g):
        return (layer * NG + g) * GSUB

    def q0(g):
        return g * GQ

    def piece0(layer, again):
        return layer * 2 * len(pieces(0)) + again * len(pieces(layer))

    def piece(layer, p):
        if layer == 0:
            n = len(pieces(0))
            return parked[p % n], (ld_w[p % n * 2 // n], 16 * (n // 2))
        return wstage[p % 2][:], (ld_w[p % 2], 16 * (len(pieces(0)) // 2 + (p - piece0(1, 0)) // 2 + 1))

    NSMALL = 12 + 2 * 2

    @block.sync
    def _(sp):
        sp.dma_start(rstage[:, 0, :], t["wr0"]).then_inc(ld_small, 16)
        sp.dma_start(rstage[:, 1, :], t["wr1"]).then_inc(ld_small, 16)
        sp.dma_start(Wg[:], t["gnn_w"]).then_inc(ld_small, 16)
        for s in range(BSUB):
            sp.dma_start(bg4[0:1, s, :], t["gnn_b"]).then_inc(ld_small, 16)
        sp.dma_start(gate_bias[:], t["bg"].broadcast_to([P, EXPERTS])).then_inc(ld_small, 16)
        sp.dma_start(fw[:], t["fusion"].broadcast_to([P, NGRP])).then_inc(ld_small, 16)
        sp.dma_start(gb2[:].rearrange("p g d -> p (g d)"), t["gb2"].broadcast_to([P, NGRP * D])).then_inc(ld_small, 16)
        sp.dma_start(gb1[:], t["gb1"]).then_inc(ld_small, 16)
        sp.dma_start(BBs[:], t["bb0"][EXPERTS]).then_inc(ld_small, 16)
        sp.dma_start(indc[0:QR].rearrange("p g m -> p (g m)"), t["indc"]).then_inc(ld_small, 16)
        sp.dma_start(self25[0:QR], t["self25"]).then_inc(ld_small, 16)
        sp.dma_start(diagq[0:QR], t["diagq"]).then_inc(ld_small, 16)
        sp.dma_start(rowind[0:QR], t["rowind"]).then_inc(ld_small, 16)

        def load_block(g):
            def step(i, j):
                b = j % 2
                blk = g * GBLK + i
                need(sp, s_at, a0(0, g) + i - 1)
                for h in range(2):
                    hs = slice(h * NODES, (h + 1) * NODES)
                    sp.dma_start(AB[b][hs, :, hs],
                                 t["adjT2"][bass.ds(blk * BSUB, BSUB), hs, :].rearrange("s m n -> m s n")
                                 ).then_inc(ld_a[b], 16)
                sp.dma_start(X[:, bass.ds(blk * BSUB, BSUB), :],
                             t["x"][bass.ds(blk * (BSUB * P), BSUB * P), :].rearrange("(s p) d -> p s d", p=P)
                             ).then_inc(ld_a[b], 16)
            return step

        def zero_rows(g, i):
            n = GROWS // GBLK
            sp.dma_start(sorted_rows[g][bass.ds(i * n, n), :].rearrange("(p k j) d -> p k (j d)", p=P, j=2),
                         zeros[:].unsqueeze(1).broadcast_to([P, n // (2 * P), 512])).then_inc(s_zero[g], 16)

        def load_and_zero(g):
            load = load_block(g)

            def step(i, j):
                load(i, j)
                zero_rows(g, i)
            return step

        sp.wait_ge(s_const, 2)
        for i in range(2):
            load_block(0)(i, i)
        sp.dma_start(b1all[:], t["bb0"].rearrange("e p n -> p e n")[:, :, 0:CH]).then_inc(ld_b1, 16)
        for p, (k, o, n) in enumerate(pieces(0)):
            place, (loaded, _) = piece(0, p)
            sp.dma_start(place[:, 0:n], t[f"w{k + 1}_0"][:, o:o + n]).then_inc(loaded, 16)
        for i in range(2):
            zero_rows(0, i)
        with sp.Fori(1, GBLK // 2) as q:
            for j in range(2):
                load_and_zero(0)(q * 2 + j, j)
        sp.dma_start(gW1[:], t["gW1"]).then_inc(ld_g, 16)
        sp.dma_start(gW2[:], t["gW2"]).then_inc(ld_g, 16)

        def load_piece(r):
            p = piece0(1, 0) + r
            k, o, n = (2 * pieces(1))[r]
            place, (loaded, _) = piece(1, p)
            sp.wait_ge(s_wfree, p - 1)
            sp.dma_start(place[:, 0:n], t[f"w{k + 1}_1"][:, o:o + n]).then_inc(loaded, 16)

        def store_sub(layer, g, i):
            sp.wait_ge(s_comb, c0(layer, g) + i + 1)
            sp.dma_start(out[bass.ds((g * GSUB + i) * P, P), :], X[:, bass.ds(g * GSUB + i, 1), :].rearrange("p a d -> p (a d)")
                         ).then_inc(s_out, 16)

        def routed(phase):
            _, layer, g = phase
            base, ride = t0(phase), rides.get(phase)
            bb = t["bb0"] if layer == 0 else t["bb1"]

            def load_rows(i, j):
                need(sp, s_tt, base + i - 3)
                sp.dma_start(XR[j][:], sorted_rows[g][bass.ds(i * TS, TS), :].rearrange("(s p) d -> p s d", p=P)
                             ).then_inc(s_xr[j], 16)

            def load_biases(i, j):
                e = sp.value_load(EXP[g][0:1, bass.ds(i, 1)], min_val=0, max_val=EXPERTS - 1)
                need(sp, s_y, base + i - 3)
                sp.dma_start(BB[j][:], bb[bass.ds(e, 1)].rearrange("a p n -> p (a n)")).then_inc(s_bb[j], 16)

            def store(i, j):
                sp.wait_ge(s_y, base + i + 1)
                sp.dma_start(expert_rows[g][bass.ds(i * TS, TS), :].rearrange("(s p) d -> p s d", p=P),
                             ytmp[j][:]).then_inc(s_st[j], 16)

            def step(i, j):
                if not isinstance(i, int) or i + 4 < TILES:
                    load_rows(i + 4, j)
                store(i, j)
                if not isinstance(i, int) or i + 4 < TILES:
                    load_biases(i + 4, j)

            sp.wait_ge(s_route, layer * NG + g + 1)
            sp.wait_ge(s_scat[g], 16 * 2 * GSUB * (layer + 1))
            for i in range(4):
                load_rows(i, i)
                load_biases(i, i)
            if phase == ("E", 0, NG - 1):
                sp.dma_start(b1all[:, 0:NE[1]], t["bb1"].rearrange("e p n -> p e n")[:, :, 0:CH]).then_inc(ld_b1, 16)
                load_piece(0)
                load_piece(1)
            for i in range(4):
                step(i, i)
                if phase == ("E", 0, NG - 1):
                    for r in (2 * i + 2, 2 * i + 3):
                        if r < len(pieces(1)):
                            load_piece(r)
            with sp.Fori(1, TILES // 4 - 1) as q:
                for j in range(4):
                    step(q * 4 + j, j)
                    if ride and ride[0] == 1:
                        store_sub(*ride, (q - 1) * 4 + j)
            for i in range(TILES - 4, TILES):
                step(i, i % 4)

        def store_group(layer, g):
            loop(sp, GSUB, 4, lambda i, j: store_sub(layer, g, i))

        def quad_rows(g, half, k):
            rows = slice(k % 2 * NODES, k % 2 * NODES + LIVE)
            sub = g * GSUB + half * QH * 2 + k // 2
            return X[rows, sub:sub + 2 * QH - 1:2, :], xq[k * LIVE:(k + 1) * LIVE, half * QH:(half + 1) * QH, :]

        def quads(g):
            sp.wait_ge(s_comb, c0(0, g) + GSUB)
            if g == 0:
                sp.wait_ge(s_hl, 2 * t0(("Q", 1, 0)))
                for b in range(2):
                    sp.wait_ge(s_st[b], 16 * len(before("E", ("Q", 1, 0))) * TILES // 4)
            for half in range(2):
                if g == 1:
                    sp.wait_ge(s_nb, q0(1))
                for k in range(QB):
                    rows, quad = quad_rows(g, half, k)
                    sp.dma_start(quad, rows).then_inc(ld_q[half], 16)
                r = (g * GQ + half * QH) * QR
                sp.dma_start(Aq[half][0:QR], t["adj25"][r:r + QH * QR, :].rearrange("(q r) m -> r q m", r=QR)
                             ).then_inc(ld_q[half], 16)
            for half in range(2):
                if g == 0:
                    n = len(pieces(1)) // 2
                    for r in range(n):
                        load_piece((2 + half) * n + r)
                sp.wait_ge(s_xo, q0(g) + (half + 1) * QH)
                for k in range(QB):
                    rows, quad = quad_rows(g, half, k)
                    sp.dma_start(rows, quad).then_inc(s_qst[half], 16)
            for half in range(2):
                sp.wait_ge(s_qst[half], 16 * QB * (g + 1))

        for phase in PHASES[1:]:
            kind, layer, g = phase
            if kind == "A" and layer == 0:
                sp.wait_ge(s_wfree, piece0(1, 0))
                loop(sp, GBLK, 2, load_and_zero(g))
            elif kind == "E":
                routed(phase)
            elif kind == "Q":
                quads(g)
            elif kind == "C":
                store_group(layer, g)
        sp.wait_ge(s_out, 16 * SUBS)

    @block.gpsimd
    def _(pool):
        nc.gpsimd.memset(AB[0][:], 0.0)
        nc.gpsimd.memset(AB[1][:], 0.0).then_inc(s_const, 1)
        nc.gpsimd.memset(zeros[:], 0.0).then_inc(s_const, 1)
        nc.gpsimd.memset(ident[:], 0.0)
        nc.gpsimd.memset(upper[:], 0.0)
        nc.gpsimd.memset(ones16[:], 1.0)
        nc.gpsimd.memset(ones_row[:], 1.0)
        nc.gpsimd.memset(neghalf[:], -0.5)
        nc.gpsimd.iota(rankkey[:], pattern=[[-1, EXPERTS]], base=EXPERTS, channel_multiplier=0,
                       allow_small_or_imprecise_dtypes=True)
        nc.gpsimd.iota(tileno[:], pattern=[[1, TILES]], base=0, channel_multiplier=0,
                       allow_small_or_imprecise_dtypes=True).then_inc(s_const, 1)
        pool.wait_ge(s_const, 3)
        nc.gpsimd.affine_select(out=ident[:], in_=ident[:], compare_op=ALU.not_equal, fill=1.0, base=0,
                                pattern=[[-1, P]], channel_multiplier=1)
        nc.gpsimd.affine_select(out=upper[:], in_=upper[:], compare_op=ALU.is_ge, fill=1.0, base=0,
                                pattern=[[-1, P]], channel_multiplier=1).then_inc(s_const, 1)
        pool.wait_ge(s_const, 4)
        nc.gpsimd.tensor_copy(ident16[:], ident[:]).then_inc(s_const, 1)
        pool.wait_ge(s_rmax, 1)
        nc.gpsimd.partition_all_reduce(big[:, :, 3], big[:, :, 3], P, ABSMAX).then_inc(s_rall, 1)

        def rstds(layer, g):
            def root(m, n, b):
                pool.wait_ge(s_var[m], n + 1)
                nc.gpsimd.tensor_tensor(rstd[m][b][:], ve[m][b][:], neghalf[:, 0:BSUB], ALU.pow).then_inc(s_rstd[m], 1)

            def step(i, j, last=False):
                n = a0(layer, g) + i
                root(1, n, j % 2)
                if layer == 0 and not last:
                    root(0, n + 2, j % 2)

            if layer == 0:
                for i in range(2):
                    root(0, a0(0, g) + i, i)
            loop(pool, GBLK - 2, 2, step)
            for i in range(GBLK - 2, GBLK):
                step(i, i, last=True)

        def scatter_ready(layer, g):
            pool.wait_ge(s_route, layer * NG + g + 1)
            if layer == 0:
                pool.wait_ge(s_zero[g], 16 * GBLK)
            if layer == 1:
                for b in range(4):
                    pool.wait_ge(s_xr[b], 16 * (r0(("E", 0, g)) + TILES // 4))

        def scatter(g, subs):
            for s in subs:
                for k in range(2):
                    c = k * GSUB + s
                    nc.gpsimd.indirect_dma_start(sorted_rows[g], bass.IndirectOffsetOnAxis(ap=POS[g][:, c:c + 1], axis=0),
                                                 R[:, g * GSUB + s, :], None).then_inc(s_scat[g], 16)

        def everywhere(layer):
            pool.wait_ge(s_prep, layer + 1)
            nc.gpsimd.partition_all_reduce(big[:, layer, 0:3], big[:, layer, 0:3], P, ABSMAX).then_inc(s_prepall, 1)

        def all_stored(layer, g):
            for b in range(4):
                pool.wait_ge(s_st[b], 16 * (r0(("E", layer, g)) + TILES // 4))

        def gather(layer, g, s):
            need(pool, s_comb, c0(layer, g) + s - 3)
            for k in range(2):
                c = k * GSUB + s
                nc.gpsimd.indirect_dma_start(G[s % 4][:, k, :], None, expert_rows[g],
                                             bass.IndirectOffsetOnAxis(ap=POS[g][:, c:c + 1], axis=0)
                                             ).then_inc(s_g[s % 4], 16)

        def roots(g, half):
            qs = slice(half * QH, (half + 1) * QH)
            pool.wait_ge(s_qv, 2 * g + half + 1)
            nc.gpsimd.tensor_tensor(qp[0:QR, qs], qv[0:QR, qs], neghalf[0:QR].rearrange("p (q k) -> p q k", q=QH), ALU.pow
                                    ).then_inc(s_qp, 1)

        for phase in PHASES:
            kind, layer, g = phase
            if kind == "A":
                rstds(layer, g)
            elif kind == "M":
                everywhere(0)
            elif kind == "R" and (layer, g) != (1, 0):
                scatter_ready(layer, g)
                scatter(g, range(GSUB))
            elif kind == "Q":
                ahead = 8
                roots(g, 0)
                if phase in rides:
                    all_stored(*rides[phase])
                    for s in range(ahead):
                        gather(*rides[phase], s)
                    roots(g, 1)
                    for s in range(ahead, GSUB):
                        gather(*rides[phase], s)
                else:
                    scatter_ready(1, 0)
                    scatter(0, range(ahead))
                    roots(g, 1)
                    scatter(0, range(ahead, GSUB))
            elif kind == "E" and phase in rides:
                all_stored(*rides[phase])
                for s in range(GSUB):
                    gather(*rides[phase], s)
                    if s == 3 and layer == 0:
                        everywhere(1)
            elif kind == "C":
                all_stored(layer, g)
                for s in range(GSUB):
                    gather(layer, g, s)

    @block.scalar
    def _(act):
        act.wait_ge(ld_small, 16 * NSMALL)
        act.wait_ge(s_vconst, 2)
        nc.scalar.activation(fw[:], fw[:], ACT.Exp, bias=fwt[:, 1:2]).then_inc(s_fusx, 1)

        def blocks(layer, g):
            def aggregated(i, b):
                n = a0(layer, g) + i
                act.wait_ge(s_at, n + 1)
                need(act, s_conv, n - 1)
                nc.scalar.activation(aT[b][:], bk[2 + b][:], ACT.Copy).then_inc(s_atc, 1)

            def step(i, j, last=False):
                b = j % 2
                n = a0(layer, g) + i
                act.wait_ge(s_rt, n + 1)
                need(act, s_log, n - 1)
                nc.scalar.activation(RT[b][:].rearrange("p h t -> p (h t)"), bk[5 + b][:].bitcast(F16), ACT.Copy
                                     ).then_inc(s_rtc, 1)
                if layer == 0 and not last:
                    aggregated(i + 2, b)

            if layer == 0:
                for i in range(2):
                    aggregated(i, i)
            loop(act, GBLK - 2, 2, step, head=(layer, g) == (0, 0))
            for i in range(GBLK - 2, GBLK):
                step(i, i, last=True)

        def gate(layer, g):
            act.wait_ge(s_diff, layer * NG + g + 1)
            nc.scalar.activation(expd[:], den[:], ACT.Exp).then_inc(s_exp, 1)

        def hi_half(layer, r):
            k, o, n = pieces(layer)[r]
            place, loaded = piece(layer, piece0(layer, 1) + r)
            act.wait_ge(*loaded)
            nc.scalar.activation((W1h, W2h)[k][:, o:o + n], place[:, 0:n], ACT.Copy, scale=sc[:, layer, k:k + 1]
                                 ).then_inc(s_whi, 1)

        def prep(layer):
            act.wait_ge(s_scale, layer + 1)
            if layer == 0:
                for r in range(len(pieces(0))):
                    hi_half(0, r)
            else:
                act.wait_ge(s_yp, t0(("E", 1, 0)))

        def tiles(phase):
            kind, layer, g = phase
            base, shared, n_tiles = t0(phase), kind == "S", STILES if kind == "S" else TILES

            def step(i, j):
                b = j % 2
                n = base + i
                act.wait_ge(s_tt, n + 1)
                need(act, s_h, 2 * (n - 1))
                nc.scalar.activation(XTt[b][:].rearrange("p h t -> p (h t)"), bk[4 + b][:, 0:TS].bitcast(F16), ACT.Copy
                                     ).then_inc(s_ttc, 1)
                bias = BBs if shared else BB[j]
                if not shared:
                    act.wait_ge(s_bb[j], 16 * (r0(phase) + 1) + (i - j) * 4)
                for half in range(2):
                    act.wait_ge(s_h, 2 * n + half + 1)
                    need(act, s_hl, 2 * (n - 2) + half + 1)
                    for c in (2 * half, 2 * half + 1):
                        a = nc.scalar.activation(h32[b][:, c, :], bk[2 * b + half][:, (c % 2) * TS:(c % 2 + 1) * TS],
                                                 ACT.Gelu if layer == 0 else ACT.Relu,
                                                 bias=bias[:, c:c + 1], scale=inv_z[:, layer:layer + 1])
                    a.then_inc(s_act, 1)
            loop(act, n_tiles, 4, step, head=base == 0)

        def quads(g):
            def aggregated(i):
                n = q0(g) + i
                act.wait_ge(s_qa, n + 1)
                need(act, s_h1, 2 * n)
                nc.scalar.activation(qaT[:], bk[1][:, 0:NGRP * QR].rearrange("p (g n) -> p g n", g=NGRP), ACT.Copy
                                     ).then_inc(s_qac, 1)

            def hidden(i):
                n = q0(g) + i
                for c in range(2):
                    act.wait_ge(s_h1, 2 * n + c + 1)
                    if c == 0:
                        need(act, s_s2, n)
                    for k in range(NGRP):
                        a = nc.scalar.activation(h1T[:, c, k, :], bk[2 + c][:, k * QR:(k + 1) * QR], ACT.Relu,
                                                 bias=gb1[:, k, c:c + 1])
                    a.then_inc(s_h1c, 1)

            def step(i, j, last=False):
                n = q0(g) + i
                if not last:
                    aggregated(i + 1)
                act.wait_ge(s_s2, n + 1)
                need(act, s_o2, n)
                nc.scalar.activation(s2[0:QR, 0:4, :], bk[4][0:QR, :].rearrange("p (g d) -> p g d", g=4), ACT.Copy)
                nc.scalar.activation(s2[0:QR, 4, :], bk[5][0:QR, 0:D], ACT.Copy).then_inc(s_s2c, 1)
                if not last:
                    hidden(i + 1)

            aggregated(0)
            hidden(0)
            for i in range(4):
                step(i, i)
                if g == 0:
                    hi_half(1, i)
            with act.Fori(1, GQ // 4 - 1) as q:
                for j in range(4):
                    step(q * 4 + j, j)
            for i in range(GQ - 4, GQ):
                step(i, i, last=i == GQ - 1)
                if g == 0:
                    hi_half(1, i - GQ + 8)

        for phase in PHASES:
            kind, layer, g = phase
            if kind == "A":
                blocks(layer, g)
            elif kind == "R":
                gate(layer, g)
            elif kind == "W":
                prep(layer)
            elif kind in "SE":
                tiles(phase)
            elif kind == "Q":
                quads(g)

    @block.tensor
    def _(pe):
        pe.wait_ge(s_const, 5)
        pe.wait_ge(ld_small, 16 * NSMALL)
        pe.wait_ge(s_rscale, 1)

        def blocks(layer, g):
            def aggregate(i, b):
                n = a0(layer, g) + i
                pe.wait_ge(s_xn, n + 1)
                need(pe, s_atc, n - 1)
                for s in range(BSUB):
                    m = pe.matmul(bk[2 + b][:, s * P:(s + 1) * P], xn[b][:, s, :], AB[b][:, s, :], start=True, stop=True)
                m.then_inc(s_at, 1)

            def convolve(i, b):
                n = a0(layer, g) + i
                need(pe, s_x1, n - 1)
                pe.matmul(bk[b][:], ones_row[:], bg4[:].rearrange("p s d -> p (s d)"), start=True, stop=False,
                          skip_group_check=True)
                pe.wait_ge(s_atc, n + 1)
                for s in range(BSUB):
                    m = pe.matmul(bk[b][:, s * P:(s + 1) * P], aT[b][:, s * P:(s + 1) * P], Wg[:],
                                  start=False, stop=(s == BSUB - 1), skip_group_check=True)
                m.then_inc(s_conv, 1)

            def step(i, j, last=False):
                b = j % 2
                n = a0(layer, g) + i
                pe.wait_ge(s_rows, n + 1)
                need(pe, s_rtc, n - 1)
                bank = bk[5 + b][:].bitcast(F16)
                for h in range(2):
                    for s in range(BSUB):
                        o = (h * BSUB + s) * P
                        row = R[:, bass.ds((g * GBLK + i) * BSUB + s, 1), h * D:(h + 1) * D].rearrange("p a d -> p (a d)")
                        m = pe.transpose(bank[:, o:o + P], row, ident16[:])
                m.then_inc(s_rt, 1)
                if layer == 0 and not last:
                    aggregate(i + 2, b)
                pe.wait_ge(s_rtc, n + 1)
                for s in range(BSUB):
                    o = bk[7][:, bass.ds((i * BSUB + s) * EXPERTS, EXPERTS)]
                    terms = [(0, Rh), (1, Rh), (0, Rl), (1, Rl)]
                    for k, (h, w) in enumerate(terms):
                        m = pe.matmul(o, RT[b][:, h, s * P:(s + 1) * P], w[:, layer, :], start=k == 0, stop=k == 3)
                m.then_inc(s_log, 1)
                if layer == 0 and not last:
                    convolve(i + 2, b)

            if layer == 0:
                for i in range(2):
                    aggregate(i, i)
                    convolve(i, i)
            loop(pe, GBLK - 2, 2, step, head=(layer, g) == (0, 0))
            for i in range(GBLK - 2, GBLK):
                step(i, i, last=True)

        def gate(layer, g):
            c = layer * NG + g
            pe.wait_ge(s_sel, c + 1)
            J = 2 * GSUB
            selj = sel[:].rearrange("p k s e -> p (k s) e")
            for e in range(EXPERTS):
                m = pe.matmul(bk[0][0:J, e:e + 1], selj[:, :, e], ones16[:, 0:1], start=True, stop=True)
            m.then_inc(s_tot, 1)
            pe.wait_ge(s_totm, c + 1)
            pe.matmul(bk[1][:, 0:J * EXPERTS], upper[:], selj.rearrange("p j e -> p (j e)"), start=True, stop=False)
            pe.matmul(bk[1][:, 0:J * EXPERTS], ones16[0:J, :], totm[:].rearrange("q j e -> q (j e)"), start=False, stop=True)
            pe.matmul(bk[2][:, 0:EXPERTS], ones16[0:J, :], tot[:], start=True, stop=True).then_inc(s_rank, 1)

        def tiles(phase):
            kind, layer, g = phase
            base, shared, n_tiles = t0(phase), kind == "S", STILES if kind == "S" else TILES

            def wait_loaded(i, j):
                if not shared:
                    pe.wait_ge(s_xr[j % 4], 16 * (r0(phase) + 1) + (i - j % 4) * 4)

            def turn(i, j):
                b = j % 2
                wait_loaded(i, j)
                need(pe, s_ttc, base + i - 1)
                bank = bk[4 + b][:, 0:TS].bitcast(F16)
                for h in range(2):
                    for s in range(TSUB):
                        o = (h * TSUB + s) * P
                        if shared:
                            row = R[:, bass.ds(g * GSUB + i * TSUB + s, 1), h * D:(h + 1) * D].rearrange("p a d -> p (a d)")
                        else:
                            row = XR[j % 4][:, s, h * D:(h + 1) * D]
                        m = pe.transpose(bank[:, o:o + P], row, ident16[:])
                m.then_inc(s_tt, 1)

            def hidden(i, j, e):
                b = j % 2
                n = base + i
                pe.wait_ge(s_ttc, n + 1)
                for half in range(2):
                    need(pe, s_act, 2 * (n - 2) + half + 1)
                    for c in (2 * half, 2 * half + 1):
                        o = bk[2 * b + half][:, (c % 2) * TS:(c % 2 + 1) * TS]
                        for k, (w, h) in enumerate(((W1h, 0), (W1h, 1), (W1l, 0))):
                            m = pe.matmul(o, w[:, at(e, c)], XTt[b][:, h, :], start=k == 0, stop=k == 2)
                    m.then_inc(s_h, 1)

            def outs(i, j, e):
                b = j % 2
                n = base + i
                pe.wait_ge(s_hl, 2 * n + 2)
                need(pe, s_y, n - 1)
                for s in range(TSUB):
                    o = bk[6 + b][:, s * D:(s + 1) * D]
                    rows = slice(s * P, (s + 1) * P)
                    for c in range(CH):
                        for k, (h, w) in enumerate(((hh, W2h), (hl, W2h), (hh, W2l))):
                            m = pe.matmul(o, h[b][:, c, rows], w[:, at(e, c)],
                                          start=c == 0 and k == 0, stop=c == CH - 1 and k == 2)
                m.then_inc(s_yp, 1)

            def at(e, c):
                if isinstance(e, int):
                    return slice(e * HID + c * P, e * HID + (c + 1) * P)
                return bass.ds(e * HID + c * P, P)

            def experts(i, count):
                if shared:
                    return [EXPERTS] * count
                return nc.values_load_multi_w_load_instructions(
                    EXP[g][0:1, bass.ds(i, count)], engines=[mybir.EngineType.PE], min_val=0, max_val=EXPERTS - 1,
                    skip_runtime_bounds_check_because="the table's entries are clamped to the experts when it is made")[1]

            turn(0, 0)
            turn(1, 1)
            hidden(0, 0, experts(0, 1)[0])

            def steps(base_i, count, last):
                e = experts(base_i, count + (0 if last else 1))
                for j in range(count):
                    i = base_i + j
                    if not last or j + 2 < count:
                        turn(i + 2, (j + 2) % 4)
                    if not last or j + 1 < count:
                        hidden(i + 1, (j + 1) % 4, e[j + 1])
                    outs(i, j, e[j])

            first = 0
            if base == 0:
                steps(0, 4, False)
                first = 1
            with pe.Fori(first, n_tiles // 4 - 1) as q:
                steps(q * 4, 4, False)
            steps(n_tiles - 4, 4, True)

        def quads(g):
            def turn(i, j):
                b = j % 2
                n = q0(g) + i
                pe.wait_ge(s_nb, n + 1)
                need(pe, s_ntc, n)
                for k in range(NGRP):
                    m = pe.transpose(bk[0][0:QR, k * QR:(k + 1) * QR], nb[b][0:QR, k, :, :].rearrange("p b m -> p (b m)"),
                                     ident[0:QR, 0:QR])
                m.then_inc(s_nt, 1)

            def aggregate(i, j):
                b = j % 2
                n = q0(g) + i
                pe.wait_ge(s_ntc, n + 1)
                pe.wait_ge(s_qn, n + 1)
                need(pe, s_qac, n)
                pe.matmul(bk[1][:, 0:NGRP * QR], xqn[b][0:QR, :], NT[j % 4][0:QR].rearrange("p g n -> p (g n)"),
                          start=True, stop=True).then_inc(s_qa, 1)

            def hidden(i, j):
                n = q0(g) + i
                pe.wait_ge(s_qac, n + 1)
                for c in range(2):
                    need(pe, s_h1c, 2 * (n - 1) + c + 1)
                    for k in range(NGRP):
                        m = pe.matmul(bk[2 + c][:, k * QR:(k + 1) * QR], gW1[:, k, c * P:(c + 1) * P], qaT[:, k, :],
                                      start=True, stop=True)
                    m.then_inc(s_h1, 1)

            def support(i, j):
                n = q0(g) + i
                pe.wait_ge(s_h1c, 2 * n + 2)
                need(pe, s_s2c, n)
                for k in range(NGRP):
                    for c in range(2):
                        m = pe.matmul(bk[4 + k // 4][0:QR, (k % 4) * D:(k % 4 + 1) * D], h1T[:, c, k, :], gW2[:, k, c, :],
                                      start=c == 0, stop=c == 1)
                m.then_inc(s_s2, 1)

            def outs(i, j):
                n = q0(g) + i
                pe.wait_ge(s_s2c, n + 1)
                need(pe, s_o2r, n)
                for k in range(NGRP):
                    m = pe.matmul(bk[6 + k // 4][0:QR, (k % 4) * D:(k % 4 + 1) * D], NT[j % 4][0:QR, k, :], s2[0:QR, k, :],
                                  start=True, stop=True)
                m.then_inc(s_o2, 1)

            def step(i, j):
                if not isinstance(i, int) or i + 1 < GQ:
                    aggregate(i + 1, j + 1)
                if not isinstance(i, int) or i + 2 < GQ:
                    turn(i + 2, j + 2)
                if not isinstance(i, int) or i >= 0:
                    support(i, j)
                if not isinstance(i, int) or i + 1 < GQ:
                    hidden(i + 1, j + 1)
                if not isinstance(i, int) or i >= 0:
                    outs(i, j)

            turn(0, 0)
            step(-1, -1)
            loop(pe, GQ - 4, 4, step, head=g == 0)
            for i in range(GQ - 4, GQ):
                step(i, i)

        left = None
        for phase in PHASES:
            kind, layer, g = phase
            if kind in "ASEQ" and left is not None:
                pe.wait_ge(*left)
            if kind == "A":
                blocks(layer, g)
            elif kind == "R":
                gate(layer, g)
                left = s_route, layer * NG + g + 1
            elif kind == "W" and layer == 0:
                pe.wait_ge(s_wfree, piece0(1, 0))
            elif kind in "SE":
                if phase == ("E", 1, 0):
                    pe.wait_ge(s_wfree, piece0(1, 1) + len(pieces(1)))
                tiles(phase)
                left = s_y, t0(phase) + (STILES if kind == "S" else TILES)
            elif kind == "Q":
                if g == 0:
                    pe.wait_ge(ld_g, 32)
                quads(g)
                left = s_o2r, q0(g) + GQ

    @block.vector
    def _(dve):
        count = [0]

        def own(ins):
            count[0] += 1
            ins.then_inc(v, 1)
            dve.wait_ge(v, count[0])

        class InLoop:

            def __init__(self, per):
                self.base, self.per = count[0], per

            def at(self, i):
                self.first, self.k = self.base + i * self.per, 0

            def mark(self, ins):
                self.k += 1
                ins.then_inc(v, 1)

            def wait(self, alone=False):
                w = dve.wait_ge(v, self.first + self.k)
                if alone:
                    w.then_inc(s_alone, 1)

        dve.wait_ge(ld_small, 16 * NSMALL)
        for l in range(2):
            m = nc.vector.tensor_reduce(big[:, l, 3:4], rstage[:, l, :], AX, ALU.max, apply_absolute_value=True)
        m.then_inc(s_rmax, 1)
        own(nc.vector.tensor_reduce(fwt[:, 0:1], fw[:], AX, ALU.max))
        nc.vector.memset(wind[:], 0.0).then_inc(s_vconst, 1)
        nc.vector.tensor_scalar(fwt[:, 1:2], fwt[:, 0:1], -1.0, None, ALU.mult).then_inc(s_vconst, 1)
        dve.wait_ge(s_fusx, 1)
        own(nc.vector.tensor_reduce(fwt[:, 2:3], fw[:], AX, ALU.add))
        own(nc.vector.reciprocal(fwt[:, 3:4], fwt[:, 2:3]))
        own(nc.vector.tensor_scalar(fw[:], fw[:], fwt[:, 3:4], None, ALU.mult))
        nc.vector.tensor_tensor(wind[0:QR], fw[0:QR], rowind[0:QR], ALU.mult)

        def scales(layer, cols):
            own(nc.vector.tensor_scalar(big[:, layer, cols], big[:, layer, cols], 1e-30, None, ALU.max))
            own(nc.vector.tensor_scalar(pw[:, layer, cols].bitcast(U32), big[:, layer, cols].bitcast(U32), 0x7F800000, None,
                                        ALU.bitwise_and))
            own(nc.vector.reciprocal(sc[:, layer, cols], pw[:, layer, cols]))
            own(nc.vector.tensor_scalar(sc[:, layer, cols], sc[:, layer, cols], 2.0 ** 14, None, ALU.mult))
            own(nc.vector.tensor_scalar(inv[:, layer, cols], pw[:, layer, cols], 2.0 ** -14, None, ALU.mult))

        dve.wait_ge(s_rall, 1)
        for l in range(2):
            scales(l, slice(3, 4))
            nc.vector.tensor_scalar(inv_l[:, l:l + 1], inv[:, l, 3:4], 2.0 ** -XSCALE_LOG, None, ALU.mult)
            own(nc.vector.tensor_scalar(Rh[:, l, :], rstage[:, l, :], sc[:, l, 3:4], None, ALU.mult))
            m = nc.vector.scalar_tensor_tensor(out=Rl[:, l, :], in0=rstage[:, l, :], scalar=sc[:, l, 3:4], in1=Rh[:, l, :],
                                               op0=ALU.mult, op1=ALU.subtract)
        m.then_inc(s_rscale, 1)

        def blocks(layer, g):
            ks = InLoop(4 if layer == 0 else 2)

            def row(i, s):
                return X[:, bass.ds((g * GBLK + i) * BSUB + s, 1), :].rearrange("p a d -> p (a d)")

            def rows4(i):
                return X[:, bass.ds((g * GBLK + i) * BSUB, BSUB), :]

            def moments(m, i, b, scale):
                for s in range(BSUB):
                    x = nc.vector.bn_stats(stats[m][b][:, s, :], row(i, s))
                ks.mark(x)
                ks.wait(alone=True)
                for s in range(BSUB):
                    x = nc.vector.bn_aggr(mv[m][b][:, s, :], stats[m][b][:, s, :])
                ks.mark(x)
                ks.wait()
                nc.vector.tensor_scalar(ve[m][b][:], mv[m][b][:, :, 1], EPS, scale, ALU.add, ALU.mult).then_inc(s_var[m], 1)

            def input_moments(i, b):
                dve.wait_ge(ld_a[b], 48 * (a0(0, g) // 2 + 1) + (i - b) * 24).then_inc(s_alone, 1)
                moments(0, i, b, 1.0)

            def normalise(i, b):
                n = a0(layer, g) + i
                dve.wait_ge(s_rstd[0], n + 1)
                need(dve, s_at, n - 1)
                for s in range(BSUB):
                    m = nc.vector.tensor_scalar(xn[b][:, s, :], row(i, s), mv[0][b][:, s, 0:1], rstd[0][b][:, s:s + 1],
                                                ALU.subtract, ALU.mult)
                m.then_inc(s_xn, 1)

            def sum_moments(i, b):
                n = a0(layer, g) + i
                if layer == 0:
                    dve.wait_ge(s_conv, n + 1)
                    nc.vector.tensor_tensor(rows4(i), rows4(i), bk[b][:].rearrange("p (s d) -> p s d", s=BSUB), ALU.add
                                            ).then_inc(s_x1, 1)
                    dve.wait_ge(s_x1, n + 1).then_inc(s_alone, 1)
                moments(1, i, b, 2.0 ** (-2 * XSCALE_LOG))

            def split(i, b):
                n = a0(layer, g) + i
                dve.wait_ge(s_rstd[1], n + 1)
                for s in range(BSUB):
                    m = nc.vector.tensor_scalar(xs[b][:, s, :], row(i, s), mv[1][b][:, s, 0:1], rstd[1][b][:, s:s + 1],
                                                ALU.subtract, ALU.mult)
                m.then_inc(s_vx, 1)
                dve.wait_ge(s_vx, n + 1)
                hi = R[:, bass.ds((g * GBLK + i) * BSUB, BSUB), 0:D]
                nc.vector.tensor_copy(hi, xs[b][:]).then_inc(s_vh, 1)
                dve.wait_ge(s_vh, n + 1)
                nc.vector.tensor_tensor(R[:, bass.ds((g * GBLK + i) * BSUB, BSUB), D:2 * D], xs[b][:], hi, ALU.subtract
                                        ).then_inc(s_rows, 1)

            if layer == 0:
                for i in range(2):
                    ks.at(0)
                    input_moments(i, i)
                    normalise(i, i)
                    ks.base += 2

                def step(i, j):
                    b = j % 2
                    ks.at(i)
                    sum_moments(i, b)
                    input_moments(i + 2, b)
                    split(i, b)
                    normalise(i + 2, b)

                loop(dve, GBLK - 2, 2, step, head=g == 0)
                ks.base += 4 * (GBLK - 2)
                for i in range(GBLK - 2, GBLK):
                    ks.at(0)
                    sum_moments(i, i % 2)
                    split(i, i % 2)
                    ks.base += 2
            else:
                for half in range(2):
                    dve.wait_ge(s_qst[half], 16 * QB * (g + 1))
                ks.at(0)
                sum_moments(0, 0)

                def step(i, j):
                    ks.at(i + 1)
                    sum_moments(i + 1, (j + 1) % 2)
                    split(i, j % 2)

                loop(dve, GBLK - 2, 2, step)
                step(GBLK - 2, 0)
                split(GBLK - 1, 1)
                ks.base += 2 * GBLK
            count[0] = ks.base

        def gate(layer, g):
            c = layer * NG + g
            J = 2 * GSUB
            dve.wait_ge(s_log, a0(layer, g) + GBLK)
            nc.vector.tensor_scalar(lg[:].rearrange("p s e -> p (s e)"), bk[7][:, 0:GSUB * EXPERTS], inv_l[:, layer:layer + 1],
                                    None, ALU.mult).then_inc(s_lgr, 1)
            dve.wait_ge(s_lgr, c + 1)
            if layer == 1:
                own(nc.vector.tensor_tensor(lg[:], lg[:], gate_bias[:].unsqueeze(1).broadcast_to([P, GSUB, EXPERTS]), ALU.add))
            src = lg
            for k in range(2):
                own(nc.vector.tensor_reduce(top[:, k, :], src[:], AX, ALU.max))
                own(nc.vector.tensor_tensor(keyed[:], src[:], top[:, k, :].unsqueeze(2).broadcast_to([P, GSUB, EXPERTS]),
                                            ALU.is_equal))
                own(nc.vector.tensor_tensor(keyed[:], keyed[:], rankkey[:].unsqueeze(1).broadcast_to([P, GSUB, EXPERTS]),
                                            ALU.mult))
                own(nc.vector.tensor_reduce(kmax[:], keyed[:], AX, ALU.max))
                m = nc.vector.tensor_tensor(sel[:, k], keyed[:], kmax[:].unsqueeze(2).broadcast_to([P, GSUB, EXPERTS]),
                                            ALU.is_equal)
                if k == 0:
                    own(m)
                    own(nc.vector.scalar_tensor_tensor(out=lg2[:], in0=sel[:, 0], scalar=-1e30, in1=lg[:], op0=ALU.mult,
                                                       op1=ALU.add))
                    src = lg2
            m.then_inc(s_sel, 1)
            nc.vector.tensor_tensor(den[:], top[:, 1, :], top[:, 0, :], ALU.subtract).then_inc(s_diff, 1)
            dve.wait_ge(s_tot, c + 1)
            own(nc.vector.tensor_copy(tot[:], bk[0][0:J, 0:EXPERTS]))
            nc.vector.tensor_tensor(totm[:], tot[:].unsqueeze(1).broadcast_to([J, J, EXPERTS]),
                                    upper[0:J, 0:J].unsqueeze(2).broadcast_to([J, J, EXPERTS]), ALU.mult).then_inc(s_totm, 1)
            dve.wait_ge(s_exp, c + 1)
            own(nc.vector.tensor_scalar(den[:], expd[:], 1.0, None, ALU.add))
            own(nc.vector.reciprocal(PW[g][:, 0, :], den[:]))
            nc.vector.tensor_tensor(PW[g][:, 1, :], PW[g][:, 0, :], expd[:], ALU.mult)
            dve.wait_ge(s_rank, c + 1)
            own(nc.vector.tensor_scalar(cnt[:], bk[2][:, 0:EXPERTS], float(TS - 1), None, ALU.add))
            own(nc.vector.tensor_copy(cnti[:], cnt[:]))
            own(nc.vector.tensor_scalar(cnti[:], cnti[:], TS.bit_length() - 1, None, ALU.logical_shift_right))
            own(nc.vector.tensor_copy(ntile[:], cnti[:]))
            prev = ntile
            for k in range(3):
                w = 1 << k
                nc.vector.tensor_copy(scan[k][:, 0:w], prev[:, 0:w])
                own(nc.vector.tensor_tensor(scan[k][:, w:], prev[:, w:], prev[:, 0:EXPERTS - w], ALU.add))
                prev = scan[k]
            own(nc.vector.tensor_tensor(start[:], prev[:], ntile[:], ALU.subtract))
            own(nc.vector.tensor_scalar(start[:], start[:], float(TS), None, ALU.mult))
            own(nc.vector.tensor_tensor(selw[:], bk[1][:, 0:J * EXPERTS].rearrange("p (j e) -> p j e", e=EXPERTS),
                                        start[:].unsqueeze(1).broadcast_to([P, J, EXPERTS]), ALU.add))
            own(nc.vector.tensor_tensor(selw[:], selw[:], sel[:].rearrange("p k s e -> p (k s) e"), ALU.mult))
            own(nc.vector.tensor_reduce(posf[:], selw[:], AX, ALU.add))
            nc.vector.tensor_copy(POS[g][:], posf[:])
            own(nc.vector.tensor_tensor(tcmp[:], tileno[:].unsqueeze(2).broadcast_to([1, TILES, EXPERTS]),
                                        prev[0:1].unsqueeze(1).broadcast_to([1, TILES, EXPERTS]), ALU.is_ge))
            own(nc.vector.tensor_reduce(texp[:], tcmp[:], AX, ALU.add))
            own(nc.vector.tensor_scalar(texp[:], texp[:], float(EXPERTS - 1), None, ALU.min))
            nc.vector.tensor_copy(EXP[g][:], texp[:]).then_inc(s_route, 1)

        def magnitude(layer, r):
            k, o, n = pieces(layer)[r]
            place, loaded = piece(layer, piece0(layer, 0) + r)
            dve.wait_ge(*loaded)
            nc.vector.tensor_reduce(wmax[:, r:r + 1], place[:, 0:n], AX, ALU.max, apply_absolute_value=True
                                    ).then_inc(s_wfree, 1)

        def magnitudes_all(layer):
            half = len(pieces(layer)) // 2
            dve.wait_ge(s_wfree, piece0(layer, 1))
            for k in range(2):
                nc.vector.tensor_reduce(big[:, layer, k:k + 1], wmax[:, k * half:(k + 1) * half], AX, ALU.max)
            dve.wait_ge(ld_b1, 16 * (layer + 1))
            nc.vector.tensor_reduce(big[:, layer, 2:3], b1all[:, 0:NE[layer]].rearrange("p e c -> p (e c)"), AX, ALU.max,
                                    apply_absolute_value=True).then_inc(s_prep, 1)

        def lo_half(layer, r):
            k, o, n = pieces(layer)[r]
            place, _ = piece(layer, piece0(layer, 1) + r)
            hi, lo = ((W1h, W1l), (W2h, W2l))[k]
            dve.wait_ge(s_whi, layer * len(pieces(0)) + r + 1)
            nc.vector.scalar_tensor_tensor(out=lo[:, o:o + n], in0=place[:, 0:n], scalar=sc[:, layer, k:k + 1],
                                           in1=hi[:, o:o + n], op0=ALU.mult, op1=ALU.subtract).then_inc(s_wfree, 1)

        def prep(layer):
            dve.wait_ge(s_prepall, layer + 1)
            own(nc.vector.scalar_tensor_tensor(out=big[:, layer, 2:3], in0=big[:, layer, 0:1], scalar=float(D),
                                               in1=big[:, layer, 2:3], op0=ALU.mult, op1=ALU.add))
            scales(layer, slice(0, 3))
            nc.vector.tensor_scalar(inv_z[:, layer:layer + 1], inv[:, layer, 0:1], 2.0 ** -XSCALE_LOG, None, ALU.mult)
            nc.vector.tensor_tensor(inv_y[:, layer:layer + 1], inv[:, layer, 1:2], inv[:, layer, 2:3], ALU.mult
                                    ).then_inc(s_scale, 1)
            if layer == 0:
                for r in range(len(pieces(0))):
                    lo_half(0, r)

        def combine_sub(layer, g, i, b):
            dve.wait_ge(s_g[b], 32 * (c0(layer, g) // 4 + 1) + (i - b) * 8)
            row = X[:, bass.ds(g * GSUB + i, 1), :].rearrange("p a d -> p (a d)")
            nc.vector.scalar_tensor_tensor(out=row, in0=G[b][:, 0, :], scalar=PW[g][:, 0, bass.ds(i, 1)], in1=row,
                                           op0=ALU.mult, op1=ALU.add).then_inc(s_half, 1)
            dve.wait_ge(s_half, c0(layer, g) + i + 1)
            nc.vector.scalar_tensor_tensor(out=row, in0=G[b][:, 1, :], scalar=PW[g][:, 1, bass.ds(i, 1)], in1=row,
                                           op0=ALU.mult, op1=ALU.add).then_inc(s_comb, 1)

        def tiles(phase):
            kind, layer, g = phase
            base, shared, n_tiles = t0(phase), kind == "S", STILES if kind == "S" else TILES
            ride = rides.get(phase)

            def split(i, j):
                b = j % 2
                n = base + i
                parts = [slice(0, CH // 2), slice(CH // 2, CH)]
                for half, cs in enumerate(parts):
                    dve.wait_ge(s_act, 2 * n + half + 1)
                    if half == 0:
                        need(dve, s_yp, n - 1)
                    nc.vector.tensor_scalar(hh[b][:, cs], h32[b][:, cs], sc[:, layer, 2:3], None, ALU.mult).then_inc(s_hh, 1)
                for half, cs in enumerate(parts):
                    dve.wait_ge(s_hh, 2 * n + half + 1)
                    nc.vector.scalar_tensor_tensor(out=hl[b][:, cs], in0=h32[b][:, cs], scalar=sc[:, layer, 2:3],
                                                   in1=hh[b][:, cs], op0=ALU.mult, op1=ALU.subtract).then_inc(s_hl, 1)

            def scale_out(i, j):
                b = j % 2
                n = base + i
                dve.wait_ge(s_yp, n + 1)
                y = ytmp[j]
                bias = BBs if shared else BB[j]
                if not shared:
                    need(dve, s_st[j], 16 * r0(phase) + (i - j) * 4)
                elif base:
                    dve.wait_ge(s_st[j], 16 * len(before("E", phase)) * TILES // 4)
                nc.vector.scalar_tensor_tensor(out=y[:], in0=bk[6 + b][:, 0:TSUB * D].rearrange("p (s d) -> p s d", s=TSUB),
                                               scalar=inv_y[:, layer:layer + 1],
                                               in1=bias[:, CH:].unsqueeze(1).broadcast_to([P, TSUB, D]),
                                               op0=ALU.mult, op1=ALU.add).then_inc(s_y, 1)
                if shared:
                    rows = X[:, bass.ds(g * GSUB + i * TSUB, TSUB), :]
                    dve.wait_ge(s_y, n + 1)
                    nc.vector.tensor_tensor(rows, rows, y[:], ALU.add).then_inc(s_xsh, 1)

            split(0, 0)
            for j in range(4):
                split(j + 1, (j + 1) % 4)
                scale_out(j, j)
                if phase == ("E", 0, NG - 1):
                    for r in (2 * j, 2 * j + 1):
                        magnitude(1, r)
            if phase == ("E", 0, NG - 1):
                magnitudes_all(1)
            with dve.Fori(1, n_tiles // 4 - 1) as q:
                for j in range(4):
                    split(q * 4 + j + 1, (j + 1) % 4)
                    scale_out(q * 4 + j, j)
                    if ride:
                        combine_sub(*ride, (q - 1) * 4 + j, j)
            for i in range(n_tiles - 4, n_tiles):
                if i + 1 < n_tiles:
                    split(i + 1, (i + 1) % 4)
                scale_out(i, i % 4)

        def quads(phase):
            g, ride = phase[2], rides.get(phase)
            ks = InLoop(2)

            def prepare(half):
                qs = slice(half * QH, (half + 1) * QH)
                amh = am[0:QR, qs, 0:NGRP * LIVE].rearrange("p q (g m) -> p q g m", g=NGRP)
                dve.wait_ge(ld_q[half], 16 * (QB + 1) * (g + 1))
                for q in range(half * QH, (half + 1) * QH):
                    m = nc.vector.bn_stats(qst[0:QR, q, 0:6], xq[0:QR, q, :])
                own(nc.vector.tensor_tensor(Aq[half][0:QR], Aq[half][0:QR],
                                            self25[0:QR].unsqueeze(1).broadcast_to([QR, QH, LIVE]), ALU.add))
                for q in range(half * QH, (half + 1) * QH):
                    m = nc.vector.bn_aggr(qst[0:QR, q, 6:8], qst[0:QR, q, 0:6])
                for k in range(NGRP):
                    m = nc.vector.tensor_tensor(amh[:, :, k, :], Aq[half][0:QR],
                                                indc[0:QR, k, :].unsqueeze(1).broadcast_to([QR, QH, LIVE]), ALU.mult)
                own(m)
                own(nc.vector.tensor_reduce(deg[0:QR, qs], amh, AX, ALU.add))
                own(nc.vector.tensor_scalar(isz[0:QR, qs], deg[0:QR, qs], 0.0, None, ALU.is_equal))
                nc.vector.tensor_scalar(qv[0:QR, qs, NGRP:NGRP + 1], qst[0:QR, qs, 7:8], EPS, None, ALU.add)
                nc.vector.tensor_tensor(qv[0:QR, qs, 0:NGRP], deg[0:QR, qs], isz[0:QR, qs], ALU.add).then_inc(s_qv, 1)
                own(nc.vector.tensor_scalar(isz[0:QR, qs], isz[0:QR, qs], -1.0, 1.0, ALU.mult, ALU.add))
                dve.wait_ge(s_qp, 2 * g + half + 1)
                own(nc.vector.tensor_tensor(dinv[0:QR, qs], qp[0:QR, qs, 0:NGRP], isz[0:QR, qs], ALU.mult))
                own(nc.vector.tensor_tensor(amh, amh, dinv[0:QR, qs].unsqueeze(3).broadcast_to([QR, QH, NGRP, LIVE]),
                                            ALU.mult))

            def one(ap, i):
                return ap[0:QR, bass.ds(i, 1)].rearrange("p a n -> p (a n)")

            def rows(i, j):
                b = j % 2
                n = q0(g) + i
                need(dve, s_qa, n - 1)
                nc.vector.tensor_scalar(xqn[b][0:QR], one(xq, i), one(qst, i)[:, 6:7], one(qp, i)[:, NGRP:NGRP + 1],
                                        ALU.subtract, ALU.mult).then_inc(s_qn, 1)
                need(dve, s_nt, n - 1)
                a = one(am, i)[:, 0:NGRP * LIVE].rearrange("p (g m) -> p g m", g=NGRP)
                for k in range(QB):
                    m = nc.vector.tensor_scalar(nb[b][0:QR, :, k, :], a, diagq[0:QR, k:k + 1], None, ALU.mult)
                m.then_inc(s_nb, 1)

            def columns(i, j):
                n = q0(g) + i
                dve.wait_ge(s_nt, n + 1)
                need(dve, s_o2, n - 3)
                nc.vector.tensor_tensor(NT[j % 4][0:QR], bk[0][0:QR, 0:NGRP * QR].rearrange("p (g n) -> p g n", g=NGRP),
                                        one(dinv, i).unsqueeze(2).broadcast_to([QR, NGRP, QR]), ALU.mult
                                        ).then_inc(s_ntc, 1)

            def back(i):
                n = q0(g) + i
                ks.at(i)
                dve.wait_ge(s_o2, n + 1)
                nc.vector.tensor_tensor(qt[0:QR, 0:4, :], bk[6][0:QR, :].rearrange("p (g d) -> p g d", g=4), gb2[0:QR, 0:4, :],
                                        ALU.add)
                nc.vector.tensor_tensor(qt[0:QR, 4, :], bk[7][0:QR, 0:D], gb2[0:QR, 4, :], ALU.add).then_inc(s_o2r, 1)
                dve.wait_ge(s_o2r, n + 1)
                ks.mark(nc.vector.scalar_tensor_tensor(out=qt2[0:QR], in0=qt[0:QR], scalar=0.0,
                                                       in1=wind[0:QR].unsqueeze(2).broadcast_to([QR, NGRP, D]),
                                                       op0=ALU.max, op1=ALU.mult))
                ks.wait()
                ks.mark(nc.vector.tensor_reduce(qsum[0:QR], qt2[0:QR].rearrange("p g d -> p d g"), AX, ALU.add))
                ks.wait()
                nc.vector.tensor_tensor(one(xq, i), one(xq, i), qsum[0:QR], ALU.add).then_inc(s_xo, 1)

            def step(i, j):
                if not isinstance(i, int) or i >= 1:
                    back(i - 1)
                if not isinstance(i, int) or i + 2 < GQ:
                    columns(i + 2, j + 2)
                if not isinstance(i, int) or i + 3 < GQ:
                    rows(i + 3, j + 3)
                if ride:
                    for k in range(2):
                        combine_sub(*ride, i * 2 + k, (j * 2 + k) % 4)

            if g == 0:
                dve.wait_ge(s_yp, t0(("E", 1, 0)))
            prepare(0)
            ks.base = count[0]
            rows(0, 0)
            rows(1, 1)
            columns(0, 0)
            rows(2, 2)
            columns(1, 1)
            for i in range(4):
                step(i, i)
                if g == 0:
                    lo_half(1, i)
            count[0] += 2 * 3
            seen = count[0]
            prepare(1)
            ks.base += count[0] - seen
            with dve.Fori(1, GQ // 4 - 1) as q:
                for j in range(4):
                    step(q * 4 + j, j)
            for i in range(GQ - 4, GQ):
                step(i, i)
                if g == 0:
                    lo_half(1, i - GQ + 8)
            back(GQ - 1)
            count[0] = ks.base + 2 * GQ

        for phase in PHASES:
            kind, layer, g = phase
            if kind == "A":
                blocks(layer, g)
            elif kind == "R":
                gate(layer, g)
            elif kind == "M":
                for r in range(len(pieces(0))):
                    magnitude(0, r)
                magnitudes_all(0)
            elif kind == "W":
                prep(layer)
            elif kind in "SE":
                tiles(phase)
            elif kind == "Q":
                quads(phase)
            elif kind == "C":
                loop(dve, GSUB, 4, lambda i, j: combine_sub(layer, g, i, j))


def kernel(**inputs):
    import concourse.bacc as _bacc
    from concourse import mybir as _mybir
    from concourse.bass_utils import run_bass_kernel_spmd as _run

    a = {k: np.asarray(x) for k, x in inputs.items()}
    c = np.ascontiguousarray

    def biases(b1, b2):
        n = b1.shape[0]
        return c(np.concatenate([b1.reshape(n, CH, P).transpose(0, 2, 1),
                                 np.broadcast_to(b2[:, None, :], (n, P, D))], axis=2))

    def chunks(w):
        return c(w.reshape(w.shape[0], CH, P, D).transpose(2, 0, 1, 3))

    member = np.zeros((NGRP, LIVE), np.float32)
    for k, nodes in enumerate(GRPS):
        member[k, nodes] = 1.0
    node = np.arange(QR) % LIVE
    graph = np.arange(QR) // LIVE
    arrays = {
        "x": a["x"].reshape(TOKENS, D),
        "adjT2": c(a["adj"].transpose(0, 2, 1)).reshape(SUBS, P, NODES),
        "adj25": c(a["adj"][:, :LIVE, :LIVE]).reshape(GRAPHS * LIVE, LIVE),
        "gnn_w": a["L0_gnn_weight"],
        "gnn_b": a["L0_gnn_bias"].reshape(1, D),
        "wr0": a["L0_ffn_Wr"],
        "wr1": c(a["L1_ffn_Wg"].T),
        "bg": a["L1_ffn_bg"].reshape(1, EXPERTS),
        "w1_0": c(np.concatenate([a["L0_ffn_W1p"], a["L0_ffn_W1s"][None]]).transpose(1, 0, 2)).reshape(P, -1),
        "w2_0": chunks(np.concatenate([a["L0_ffn_W2p"], a["L0_ffn_W2s"][None]])).reshape(P, -1),
        "bb0": biases(np.concatenate([a["L0_ffn_b1p"], a["L0_ffn_b1s"][None]]),
                      np.concatenate([a["L0_ffn_b2p"], a["L0_ffn_b2s"][None]])),
        "w1_1": c(a["L1_ffn_W1"].transpose(2, 0, 1)).reshape(P, -1),
        "w2_1": chunks(c(a["L1_ffn_W2"].transpose(0, 2, 1))).reshape(P, -1),
        "bb1": biases(a["L1_ffn_b1"], a["L1_ffn_b2"]),
        "gW1": c(a["L1_gnn_W1"].transpose(1, 0, 2)),
        "gW2": c(a["L1_gnn_W2"].reshape(NGRP, 2, P, D).transpose(2, 0, 1, 3)),
        "gb1": c(a["L1_gnn_b1"].reshape(NGRP, 2, P).transpose(2, 0, 1)),
        "gb2": a["L1_gnn_b2"].reshape(1, NGRP * D),
        "fusion": a["L1_gnn_fusion_w"].reshape(1, NGRP),
        "indc": c((member[:, node].T[:, :, None] * member[None]).reshape(QR, NGRP * LIVE)),
        "rowind": c(member[:, node].T),
        "self25": c(np.eye(LIVE, dtype=np.float32)[node]),
        "diagq": c(np.eye(QB, dtype=np.float32)[graph]),
    }
    nc = _bacc.Bacc("TRN2", target_bir_lowering=False, num_devices=1)
    t = {k: nc.dram_tensor(f"in_{k}", x.shape, _mybir.dt.from_np(x.dtype), kind="ExternalInput").ap()
         for k, x in arrays.items()}
    out = nc.dram_tensor("out_0", (TOKENS, D), F32, kind="ExternalOutput").ap()
    program(nc, t, out)
    r = _run(nc, [{f"in_{k}": x for k, x in arrays.items()}], core_ids=[0])
    return r.results[0]["out_0"].reshape(GRAPHS, NODES, D)
```

```python
from contextlib import ExitStack

import numpy as np

import concourse.bass as bass
from concourse import mybir

F32 = mybir.dt.float32
F16 = mybir.dt.float16
BF16 = mybir.dt.bfloat16
I32 = mybir.dt.int32
U32 = mybir.dt.uint32
ALU = mybir.AluOpType
ACT = mybir.ActivationFunctionType
AX = mybir.AxisListType.X
ABSMAX = bass.bass_isa.ReduceOp.absmax

P = 128
D = 128
NODES = 64
GRAPHS = 128
TOKENS = GRAPHS * NODES
SUBS = TOKENS // P
NG = 2
GSUB = SUBS // NG
BSUB = 4
GBLK = GSUB // BSUB
EXPERTS = 8
HID = 512
CH = HID // P
TS = 256
TSUB = TS // P
TILES = -(-(2 * GSUB * P // TS + EXPERTS - 1) // 4) * 4
STILES = GSUB * P // TS
GROWS = TILES * TS
EPS = 1e-5
XSCALE_LOG = 10
GRPS = [list(range(25)), list(range(9)), [0] + list(range(9, 15)), [6, 7, 8, 12, 13, 14], [3, 4, 5, 9, 10, 11]]
NGRP = len(GRPS)
LIVE = 25
QB = 4
QR = QB * LIVE
GQ = GRAPHS // NG // QB
QH = GQ // 2
QP = GQ // 4
GHID = 256
NE = [EXPERTS + 1, EXPERTS]
WP = 2 * HID


def pieces(layer):
    n = NE[layer] * HID
    return [(k, o, min(WP, n - o)) for k in range(2) for o in range(0, n, WP)]


def need(eng, sem, value):
    if not isinstance(value, int) or value > 0:
        eng.wait_ge(sem, value)


def loop(eng, n, unroll, step, head=False, tail=False):
    lo = unroll if head else 0
    hi = n - unroll if tail else n
    for i in range(lo):
        step(i, i)
    if hi > lo:
        with eng.Fori(lo // unroll, hi // unroll) as q:
            for j in range(unroll):
                step(q * unroll + j, j)
    for i in range(max(hi, lo), n):
        step(i, i % unroll)


def program(nc, t, out):
    ctx = ExitStack()
    with ctx:
        build(nc, ctx, t, out)


def build(nc, ctx, t, out):
    def sb(name, shape, dt=F32):
        return ctx.enter_context(nc.sbuf_tensor("sb_" + name, shape, dt))

    def sem(name):
        return ctx.enter_context(nc.semaphore(name))

    sorted_rows = [nc.dram_tensor(f"sorted_rows{g}", (GROWS, 2 * D), F16, kind="Internal").ap() for g in range(NG)]
    expert_rows = [nc.dram_tensor(f"expert_rows{g}", (GROWS, D), F32, kind="Internal").ap() for g in range(NG)]

    ident = sb("ident", [P, P])
    ident16 = sb("ident16", [P, P], F16)
    upper = sb("upper", [P, P], BF16)
    ones16 = sb("ones16", [P, P], BF16)
    neghalf = sb("neghalf", [P, QP * (NGRP + 1)])
    rankkey = sb("rankkey", [P, EXPERTS])
    tileno = sb("tileno", [1, TILES])
    zeros = sb("zeros", [P, 512], F16)
    X = sb("X", [P, SUBS, D])
    R = sb("R", [P, SUBS, 2 * D], F16)
    W1h = sb("W1h", [P, NE[0] * HID], F16)
    W1l = sb("W1l", [P, NE[0] * HID], F16)
    W2h = sb("W2h", [P, NE[0] * HID], F16)
    W2l = sb("W2l", [P, NE[0] * HID], F16)
    wstage = [sb(f"wstage{k}", [P, WP]) for k in range(2)]
    wmax = sb("wmax", [P, 16])
    b1all = sb("b1all", [P, NE[0], CH])
    rstage = sb("rstage", [P, 2, EXPERTS])
    Rh = sb("Rh", [P, 2, EXPERTS], F16)
    Rl = sb("Rl", [P, 2, EXPERTS], F16)
    gate_bias = sb("gate_bias", [P, EXPERTS])
    big = sb("big", [P, 2, 4])
    pw = sb("pw", [P, 2, 4])
    sc = sb("sc", [P, 2, 4])
    inv = sb("inv", [P, 2, 4])
    inv_z = sb("inv_z", [P, 2])
    inv_y = sb("inv_y", [P, 2])
    inv_l = sb("inv_l", [P, 2])
    Wg = sb("Wg", [P, D])
    bg = sb("bg", [1, D])
    bgrest = sb("bgrest", [1, 2, D])
    bgpart = sb("bgpart", [1, 3, D], BF16)
    AB = [sb(f"AB{b}", [P, BSUB, P]) for b in range(2)]
    aT2 = sb("aT", [P, 2, BSUB * P])
    aT = [aT2[:, b, :] for b in range(2)]
    xn2 = sb("xn", [P, 2, BSUB, D])
    xn = [xn2[:, b] for b in range(2)]
    stats = [[sb(f"stats{m}{b}", [P, BSUB, 6]) for b in range(2)] for m in range(2)]
    mv = [[sb(f"mv{m}{b}", [P, BSUB, 2]) for b in range(2)] for m in range(2)]
    ve = [[sb(f"ve{m}{b}", [P, BSUB]) for b in range(2)] for m in range(2)]
    negmean = [[sb(f"negmean{m}{b}", [P, BSUB]) for b in range(2)] for m in range(2)]
    rstd = [[sb(f"rstd{m}{b}", [P, BSUB]) for b in range(2)] for m in range(2)]
    shift = [[sb(f"shift{m}{b}", [P, BSUB]) for b in range(2)] for m in range(2)]
    xs = [sb(f"xs{b}", [P, BSUB, D]) for b in range(2)]
    RT = [sb(f"RT{b}", [P, 2, BSUB * P], F16) for b in range(2)]
    lgs = [sb(f"lg{g}", [P, GSUB, EXPERTS]) for g in range(NG)]
    lg2 = sb("lg2", [P, GSUB, EXPERTS])
    keyed = sb("keyed", [P, GSUB, EXPERTS])
    top = sb("top", [P, 2, GSUB])
    kmax = sb("kmax", [P, GSUB])
    sel = sb("sel", [P, 2, GSUB, EXPERTS], BF16)
    selw = sb("selw", [P, 2 * GSUB, EXPERTS])
    tot = sb("tot", [2 * GSUB, EXPERTS], BF16)
    totm = sb("totm", [2 * GSUB, 2 * GSUB, EXPERTS], BF16)
    cnt = sb("cnt", [P, EXPERTS])
    cnti = sb("cnti", [P, EXPERTS], I32)
    ntile = sb("ntile", [P, EXPERTS])
    scan = [sb(f"scan{k}", [P, EXPERTS]) for k in range(3)]
    start = sb("start", [P, EXPERTS])
    posf = sb("posf", [P, 2 * GSUB])
    POS = [sb(f"POS{g}", [P, 2 * GSUB], U32) for g in range(NG)]
    PW = [sb(f"PW{g}", [P, 2, GSUB]) for g in range(NG)]
    expd = sb("expd", [P, GSUB])
    den = sb("den", [P, GSUB])
    tcmp = sb("tcmp", [1, TILES, EXPERTS])
    texp = sb("texp", [1, TILES])
    EXP = [sb(f"EXP{g}", [1, TILES], I32) for g in range(NG)]
    WOFF = [sb(f"WOFF{g}", [1, TILES], I32) for g in range(NG)]
    XR = [sb(f"XR{b}", [P, TSUB, 2 * D], F16) for b in range(4)]
    BB = [sb(f"BB{b}", [P, CH + D]) for b in range(4)]
    BBs = sb("BBs", [P, CH + D])
    XTt = [sb(f"XTt{b}", [P, 2, TS], F16) for b in range(2)]
    h32all = sb("h32", [P, 2, CH, TS])
    h32 = [h32all[:, b] for b in range(2)]
    halves = sb("halves", [P, 2, 2, CH, TS], F16)
    hh = [halves[:, 0, b] for b in range(2)]
    hl = [halves[:, 1, b] for b in range(2)]
    ytmp = [sb(f"ytmp{b}", [P, TSUB, D]) for b in range(4)]
    G = [sb(f"G{b}", [P, 2, D]) for b in range(4)]
    gW1 = sb("gW1", [P, NGRP, GHID])
    gW2 = sb("gW2", [P, NGRP, 2, D])
    gb1 = sb("gb1", [P, NGRP, 2])
    gb2 = sb("gb2", [P, NGRP, D])
    indc = sb("indc", [P, NGRP, LIVE])
    self25 = sb("self25", [P, LIVE])
    diagq = sb("diagq", [P, QB])
    wind = sb("wind", [P, NGRP])
    fw = sb("fw", [P, NGRP])
    fwt = sb("fwt", [P, 4])
    rowind = sb("rowind", [P, NGRP])
    qst = sb("qst", [P, GQ, 8])
    qv = sb("qv", [P, GQ, NGRP + 1])
    qp = sb("qp", [P, GQ, NGRP + 1])
    deg = sb("deg", [P, GQ, NGRP])
    isz = sb("isz", [P, GQ, NGRP])
    dinv = sb("dinv", [P, GQ, NGRP])
    xqn = [sb(f"xqn{b}", [P, D]) for b in range(2)]
    qaT = sb("qaT", [P, NGRP, QR])
    s2 = sb("s2", [P, NGRP, D])
    qt2 = sb("qt2", [P, NGRP, D])
    qsum = sb("qsum", [P, D])
    parked = ([x[:, k * WP:(k + 1) * WP] for x in (h32all[:].rearrange("p b c t -> p (b c t)"),
                                                   halves[:].rearrange("p h b c t -> p (h b c t)").bitcast(F32))
               for k in range(2)] + [w[:] for w in wstage]
              + [R[:, GSUB:].rearrange("p s d -> p (s d)").bitcast(F32)[:, k * WP:(k + 1) * WP] for k in range(4)])
    xq = h32all[:].rearrange("p b c t -> p (b c t)").rearrange("p (q d) -> p q d", d=D)
    Aq = [ytmp[b][:].rearrange("p s d -> p (s d)")[:, 0:QH * LIVE].rearrange("p (q m) -> p q m", q=QH) for b in range(2)]
    am = halves[:].rearrange("p h b c t -> p (h b c t)").bitcast(F32).rearrange("p (q n) -> p q n", q=GQ)
    nb = [AB[b][:].rearrange("p s m -> p (s m)")[:, 0:NGRP * QR].rearrange("p (g b m) -> p g b m", g=NGRP, b=QB)
          for b in range(2)]
    NT = [x[:, 0:NGRP * QR].rearrange("p (g n) -> p g n", g=NGRP)
          for x in [xs[b][:].rearrange("p s d -> p (s d)") for b in range(2)]
          + [RT[b][:].rearrange("p h t -> p (h t)").bitcast(F32) for b in range(2)]]
    h1T = aT2[:].rearrange("p b n -> p (b n)")[:, 0:2 * NGRP * QR].rearrange("p (c g n) -> p c g n", c=2, g=NGRP)
    qt = xn2[:].rearrange("p b s d -> p (b s) d")[:, 0:NGRP, :]

    bk = [ctx.enter_context(nc.psum_tensor(f"bank{k}", [P, 512], F32)) for k in range(8)]

    ld_small = sem("small_loaded")
    ld_late = sem("later_small_loaded")
    ld_w = [sem(f"weights_loaded{k}") for k in range(2)]
    s_const = sem("constants_made")
    s_vconst = sem("vector_constants_made")
    s_zero = [sem(f"sorted_rows_zeroed{g}") for g in range(NG)]
    s_rmax = sem("router_reduced")
    s_rall = sem("router_max_everywhere")
    s_rscale = sem("router_scaled")
    s_fusx = sem("fusion_exp")
    s_prep = sem("prep_reduced")
    s_prepall = sem("prep_max_everywhere")
    s_scale = sem("weights_scales_ready")
    s_max = sem("parked_weights_reduced")
    s_whi = sem("weights_hi_ready")
    s_wfree = sem("weights_piece_used")
    ld_b1 = sem("hidden_biases_loaded")
    ld_g = sem("grouped_weights_loaded")
    v = sem("vector_step")
    ld_a = [sem(f"block_loaded{b}") for b in range(2)]
    s_var = [sem("variance_ready"), sem("sum_variance_ready")]
    s_root = [sem("root_ready"), sem("sum_root_ready")]
    s_rstd = [sem("rstd_ready"), sem("sum_rstd_ready")]
    s_xn = sem("normalised")
    s_at = sem("aggregated")
    s_atc = sem("aggregated_copied")
    s_conv = sem("convolved")
    s_x1 = sem("residual_added")
    s_rows = sem("rows_split")
    s_rt = sem("rows_transposed")
    s_rtc = sem("rowsT_copied")
    s_log = sem("logits_ready")
    s_lgr = sem("logits_read")
    s_sel = sem("selected")
    s_tot = sem("totals_ready")
    s_totm = sem("totals_masked")
    s_cnt = sem("counts_ready")
    s_cntr = sem("counts_read")
    s_rank = sem("ranks_ready")
    s_diff = sem("logit_difference")
    s_exp = sem("gate_exp")
    s_route = sem("routes_ready")
    s_scat = [sem(f"rows_scattered{g}") for g in range(NG)]
    s_xr = [sem(f"tile_rows_loaded{b}") for b in range(4)]
    s_bb = [sem(f"tile_biases_loaded{b}") for b in range(4)]
    s_tt = sem("tile_transposed")
    s_ttc = sem("tileT_copied")
    s_h = sem("hidden_ready")
    s_act = sem("hidden_activated")
    s_hh = sem("hidden_hi")
    s_hl = sem("hidden_split")
    s_yp = sem("expert_out_ready")
    s_y = sem("expert_out_scaled")
    s_xsh = sem("shared_added")
    s_st = [sem(f"expert_rows_stored{b}") for b in range(4)]
    s_g = [sem(f"rows_gathered{b}") for b in range(4)]
    s_comb = sem("combined")
    ld_q = [sem(f"quad_loaded{b}") for b in range(2)]
    s_qv = sem("degrees_ready")
    s_qp = sem("degree_roots_ready")
    s_qn = sem("quad_normalised")
    s_nb = sem("norm_rows_ready")
    s_nt = sem("norm_transposed")
    s_ntc = sem("normT_ready")
    s_qa = sem("quad_aggregated")
    s_qac = sem("quad_aggregated_copied")
    s_h1 = sem("quad_hidden")
    s_h1c = sem("quad_hidden_activated")
    s_s2 = sem("quad_support")
    s_s2c = sem("quad_support_copied")
    s_o2 = sem("quad_out")
    s_o2r = sem("quad_out_read")
    s_qw = sem("quad_out_weighted")
    s_xo = sem("quad_added")
    s_qst = [sem(f"quad_stored{b}") for b in range(2)]
    s_out = sem("outputs_stored")
    s_alone = sem("waits_alone")
    s_aalone = sem("scalar_waits_alone")
    s_vx = sem("rows_normalised")
    s_vh = sem("rows_hi")
    s_half = sem("half_combined")
    s_phalf = sem("part_combined_by_pool")

    block = ctx.enter_context(nc.Block())

    PHASES = [("A", 0, 0), ("M", 0, 0), ("W", 0, 0), ("A", 0, 1), ("S", 0, 0), ("S", 0, 1),
              ("E", 0, 0), ("E", 0, 1), ("W", 1, 0), ("Q", 1, 0), ("A", 1, 0), ("Q", 1, 1),
              ("A", 1, 1), ("E", 1, 0), ("E", 1, 1), ("C", 1, 1)]
    rides = {("E", 0, 1): (0, 0), ("Q", 1, 0): (0, 1), ("E", 1, 1): (1, 0)}
    gated = {("S", 0, 0): (0, 0), ("E", 0, 0): (0, 1), ("Q", 1, 1): (1, 0), ("E", 1, 0): (1, 1)}
    GATE_STEPS = {"S": {"DVE": (0, 0, 1, 1, 3, 5, 5, 7, 7), "PE": (2, 4, 6), "ACT": (3,)},
                  "E": {"DVE": (0, 1, 2, 3, 5, 7, 8, 9, 10), "PE": (4, 6, 8), "ACT": (5,)},
                  "Q": {"DVE": (0, 0, 0, 0, 1, 2, 2, 3, 3), "PE": (0, 1, 2), "ACT": (0,)}}
    GATE_HEAD = 12

    def gate_stages(phase, engine, i):
        if phase not in gated or not isinstance(i, int):
            return []
        return [k for k, at in enumerate(GATE_STEPS[phase[0]][engine]) if at == i]

    def gate_bank(phase):
        return bk[7] if phase[0] == "Q" else bk[5]

    def before(kinds, phase):
        return [p for p in PHASES[:PHASES.index(phase)] if p[0] in kinds]

    def a0(layer, g):
        return (layer * NG + g) * GBLK

    def t0(phase):
        return sum(STILES if p[0] == "S" else TILES for p in before("SE", phase))

    def r0(phase):
        return len(before("E", phase)) * TILES // 4

    def c0(layer, g):
        return (layer * NG + g) * GSUB

    def q0(g):
        return g * GQ

    def piece0(layer, again):
        return len(pieces(0)) + again * len(pieces(1)) if layer == 1 else 0

    def piece(layer, p):
        if layer == 0:
            n = len(pieces(0))
            return parked[p % n], (ld_w[p % n * 2 // n], 16 * (n // 2))
        return wstage[p % 2][:], (ld_w[p % 2], 16 * (len(pieces(0)) // 2 + (p - piece0(1, 0)) // 2 + 1))

    NSMALL = 5
    NLATE = 8

    @block.sync
    def _(sp):
        for dst, src in ((rstage[:, 0, :], t["wr0"]), (rstage[:, 1, :], t["wr1"]), (Wg[:], t["gnn_w"]),
                         (bg[:], t["gnn_b"]),
                         (fw[:], t["fusion"].broadcast_to([P, NGRP]))):
            sp.dma_start(dst, src).then_inc(ld_small, 16)

        def load_block(g):
            def step(i, j):
                b = j % 2
                blk = g * GBLK + i
                need(sp, s_at, a0(0, g) + i - 1)
                for h in range(2):
                    hs = slice(h * NODES, (h + 1) * NODES)
                    sp.dma_start(AB[b][hs, :, hs],
                                 t["adjT2"][bass.ds(blk * BSUB, BSUB), hs, :].rearrange("s m n -> m s n")
                                 ).then_inc(ld_a[b], 16)
                sp.dma_start(X[:, bass.ds(blk * BSUB, BSUB), :],
                             t["x"][bass.ds(blk * (BSUB * P), BSUB * P), :].rearrange("(s p) d -> p s d", p=P)
                             ).then_inc(ld_a[b], 16)
            return step

        def zero_rows(g, i):
            n = GROWS // GBLK
            sp.dma_start(sorted_rows[g][bass.ds(i * n, n), :].rearrange("(p k j) d -> p k (j d)", p=P, j=2),
                         zeros[:].unsqueeze(1).broadcast_to([P, n // (2 * P), 512])).then_inc(s_zero[g], 16)

        sp.wait_ge(s_const, 2)
        for i in range(2):
            load_block(0)(i, i)
        for dst, src in ((gate_bias[:], t["bg"].broadcast_to([P, EXPERTS])),
                         (gb2[:].rearrange("p g d -> p (g d)"), t["gb2"].broadcast_to([P, NGRP * D])),
                         (gb1[:], t["gb1"]), (BBs[:], t["bb0"][EXPERTS]),
                         (indc[0:QR].rearrange("p g m -> p (g m)"), t["indc"]), (self25[0:QR], t["self25"]),
                         (diagq[0:QR], t["diagq"]), (rowind[0:QR], t["rowind"])):
            sp.dma_start(dst, src).then_inc(ld_late, 16)
        sp.dma_start(b1all[:], t["bb0"].rearrange("e p n -> p e n")[:, :, 0:CH]).then_inc(ld_b1, 16)
        for i in range(2, GBLK):
            load_block(0)(i, i)
            for p in range((i - 2) * 2, min(i * 2 - 2, len(pieces(0)))):
                k, o, n = pieces(0)[p]
                place, (loaded, _) = piece(0, p)
                sp.dma_start(place[:, 0:n], t[f"w{k + 1}_0"][:, o:o + n]).then_inc(loaded, 16)
        for i in range(GBLK):
            zero_rows(0, i)
        sp.dma_start(gW1[:], t["gW1"]).then_inc(ld_g, 16)
        sp.dma_start(gW2[:], t["gW2"]).then_inc(ld_g, 16)

        def load_piece(r):
            p = piece0(1, 0) + r
            k, o, n = (2 * pieces(1))[r]
            place, (loaded, _) = piece(1, p)
            sp.wait_ge(s_wfree, p - 1)
            sp.dma_start(place[:, 0:n], t[f"w{k + 1}_1"][:, o:o + n]).then_inc(loaded, 16)

        def store_sub(layer, g, i):
            sp.wait_ge(s_comb, c0(layer, g) + i + 1)
            row = X[:, bass.ds(g * GSUB + i, 1), :].rearrange("p a d -> p (a d)")
            sp.dma_start(out[bass.ds((g * GSUB + i) * P, P), :], row).then_inc(s_out, 16)

        def routed(phase):
            _, layer, g = phase
            base, ride = t0(phase), rides.get(phase)
            after = PHASES[PHASES.index(phase) + 1]
            after = after if after[0] == "E" else None

            def load_rows(i, j, g=g, base=base):
                need(sp, s_tt, base + i - 3)
                sp.dma_start(XR[j][:], sorted_rows[g][bass.ds(i * TS, TS), :].rearrange("(s p) d -> p s d", p=P)
                             ).then_inc(s_xr[j], 16)

            def load_biases(i, j, g=g, base=base):
                e = sp.value_load(EXP[g][0:1, bass.ds(i, 1)], min_val=0, max_val=EXPERTS - 1)
                need(sp, s_y, base + i - 3)
                sp.dma_start(BB[j][:], t[f"bb{layer}"][bass.ds(e, 1)].rearrange("a p n -> p (a n)")).then_inc(s_bb[j], 16)

            def store(i, j):
                sp.wait_ge(s_y, base + i + 1)
                sp.dma_start(expert_rows[g][bass.ds(i * TS, TS), :].rearrange("(s p) d -> p s d", p=P),
                             ytmp[j][:]).then_inc(s_st[j], 16)

            def step(i, j):
                if not isinstance(i, int) or i + 4 < TILES:
                    load_rows(i + 4, j)
                elif after:
                    load_rows(i + 4 - TILES, j, after[2], t0(after))
                store(i, j)
                if not isinstance(i, int) or i + 4 < TILES:
                    load_biases(i + 4, j)
                elif after:
                    load_biases(i + 4 - TILES, j, after[2], t0(after))

            def sorted_ready(layer, g):
                sp.wait_ge(s_route, layer * NG + g + 1)
                sp.wait_ge(s_scat[g], 16 * 2 * GSUB * (layer + 1))

            if PHASES[PHASES.index(phase) - 1][0] != "E":
                sorted_ready(layer, g)
                for i in range(4):
                    load_rows(i, i)
                    load_biases(i, i)
            if phase == ("E", 0, NG - 1):
                sp.dma_start(b1all[:, 0:NE[1]], t["bb1"].rearrange("e p n -> p e n")[:, :, 0:CH]).then_inc(ld_b1, 16)
                load_piece(0)
                load_piece(1)
            for i in range(4):
                step(i, i)
                if phase == ("E", 0, NG - 1):
                    for r in (2 * i + 2, 2 * i + 3):
                        if r < len(pieces(1)):
                            load_piece(r)
            with sp.Fori(1, TILES // 4 - 1) as q:
                for j in range(4):
                    step(q * 4 + j, j)
                    if ride and ride[0] == 1:
                        store_sub(*ride, (q - 1) * 4 + j)
            if after:
                sorted_ready(*after[1:])
            for i in range(TILES - 4, TILES):
                step(i, i % 4)

        def store_group(layer, g):
            loop(sp, GSUB, 4, lambda i, j: store_sub(layer, g, i))

        def quad_rows(g, half, k):
            rows = slice(k % 2 * NODES, k % 2 * NODES + LIVE)
            sub = g * GSUB + half * QH * 2 + k // 2
            return X[rows, sub:sub + 2 * QH - 1:2, :], xq[k * LIVE:(k + 1) * LIVE, half * QH:(half + 1) * QH, :]

        def quads(g):
            sp.wait_ge(s_comb, c0(0, g) + GSUB)
            if g == 0:
                sp.wait_ge(s_hl, 2 * t0(("Q", 1, 0)))
                for b in range(2):
                    sp.wait_ge(s_st[b], 16 * len(before("E", ("Q", 1, 0))) * TILES // 4)
            for half in range(2):
                if g == 1:
                    sp.wait_ge(s_nb, q0(1))
                for k in range(QB):
                    rows, quad = quad_rows(g, half, k)
                    sp.dma_start(quad, rows).then_inc(ld_q[half], 16)
                r = (g * GQ + half * QH) * QR
                sp.dma_start(Aq[half][0:QR], t["adj25"][r:r + QH * QR, :].rearrange("(q r) m -> r q m", r=QR)
                             ).then_inc(ld_q[half], 16)
            for half in range(2):
                if (g, half) == (0, 1):
                    for r in range(len(pieces(1))):
                        load_piece(len(pieces(1)) + r)
                sp.wait_ge(s_xo, q0(g) + (half + 1) * QH)
                for k in range(QB):
                    rows, quad = quad_rows(g, half, k)
                    sp.dma_start(rows, quad).then_inc(s_qst[half], 16)
            for half in range(2):
                sp.wait_ge(s_qst[half], 16 * QB * (g + 1))

        for phase in PHASES[1:]:
            kind, layer, g = phase
            if kind == "A" and layer == 0:
                load = load_block(g)

                def step(i, j):
                    load(i, j)
                    zero_rows(g, i)
                loop(sp, GBLK, 2, step)
            elif kind == "E":
                routed(phase)
            elif kind == "Q":
                quads(g)
            elif kind == "C":
                store_group(layer, g)
        sp.wait_ge(s_out, 16 * SUBS)

    @block.gpsimd
    def _(pool):
        nc.gpsimd.memset(AB[0][:], 0.0)
        nc.gpsimd.memset(AB[1][:], 0.0).then_inc(s_const, 1)
        nc.gpsimd.memset(zeros[:], 0.0).then_inc(s_const, 1)
        nc.gpsimd.memset(ident[:], 0.0)
        nc.gpsimd.memset(upper[:], 0.0)
        nc.gpsimd.memset(ones16[:], 1.0)
        nc.gpsimd.memset(neghalf[:], -0.5)
        nc.gpsimd.iota(rankkey[:], pattern=[[-1, EXPERTS]], base=EXPERTS, channel_multiplier=0,
                       allow_small_or_imprecise_dtypes=True)
        nc.gpsimd.iota(tileno[:], pattern=[[1, TILES]], base=0, channel_multiplier=0,
                       allow_small_or_imprecise_dtypes=True).then_inc(s_const, 1)
        pool.wait_ge(s_const, 3)
        nc.gpsimd.affine_select(out=ident[:], in_=ident[:], compare_op=ALU.not_equal, fill=1.0, base=0,
                                pattern=[[-1, P]], channel_multiplier=1)
        nc.gpsimd.affine_select(out=upper[:], in_=upper[:], compare_op=ALU.is_ge, fill=1.0, base=0,
                                pattern=[[-1, P]], channel_multiplier=1).then_inc(s_const, 1)
        pool.wait_ge(s_const, 4)
        nc.gpsimd.tensor_copy(ident16[:], ident[:]).then_inc(s_const, 1)
        pool.wait_ge(s_rmax, 1)
        nc.gpsimd.partition_all_reduce(big[:, :, 3], big[:, :, 3], P, ABSMAX).then_inc(s_rall, 1)

        def rstds(layer, g):
            def root(m, n, b):
                pool.wait_ge(s_var[m], n + 1)
                nc.gpsimd.tensor_tensor(rstd[m][b][:], ve[m][b][:], neghalf[:, 0:BSUB], ALU.pow).then_inc(s_root[m], 1)
                pool.wait_ge(s_root[m], n + 1)
                nc.gpsimd.tensor_tensor(shift[m][b][:], negmean[m][b][:], rstd[m][b][:], ALU.mult).then_inc(s_rstd[m], 1)

            def step(i, j, last=False):
                n = a0(layer, g) + i
                root(1, n, j % 2)
                if layer == 0 and not last:
                    root(0, n + 2, j % 2)

            if layer == 0:
                for i in range(2):
                    root(0, a0(0, g) + i, i)
            loop(pool, GBLK - 2, 2, step)
            for i in range(GBLK - 2, GBLK):
                step(i, i, last=True)

        def scatter_ready(layer, g):
            pool.wait_ge(s_route, layer * NG + g + 1)
            if layer == 0:
                pool.wait_ge(s_zero[g], 16 * GBLK)
            if layer == 1:
                for b in range(4):
                    pool.wait_ge(s_xr[b], 16 * (r0(("E", 0, g)) + TILES // 4))

        def scatter(g, subs):
            for s in subs:
                for k in range(2):
                    c = k * GSUB + s
                    nc.gpsimd.indirect_dma_start(sorted_rows[g], bass.IndirectOffsetOnAxis(ap=POS[g][:, c:c + 1], axis=0),
                                                 R[:, g * GSUB + s, :], None).then_inc(s_scat[g], 16)

        def everywhere(layer):
            pool.wait_ge(s_prep, layer + 1)
            nc.gpsimd.partition_all_reduce(big[:, layer, 0:3], big[:, layer, 0:3], P, ABSMAX).then_inc(s_prepall, 1)

        def all_stored(layer, g):
            for b in range(4):
                pool.wait_ge(s_st[b], 16 * (r0(("E", layer, g)) + TILES // 4))

        def gather(layer, g, s):
            need(pool, s_comb, c0(layer, g) + s - 3)
            for k in range(2):
                c = k * GSUB + s
                nc.gpsimd.indirect_dma_start(G[s % 4][:, k, :], None, expert_rows[g],
                                             bass.IndirectOffsetOnAxis(ap=POS[g][:, c:c + 1], axis=0)
                                             ).then_inc(s_g[s % 4], 16)

        def combine(layer, g, s):
            b, done = s % 4, c0(layer, g) + s
            pool.wait_ge(s_g[b], 32 * (done // 4 + 1))
            row = X[:, g * GSUB + s, :]
            nc.gpsimd.tensor_tensor(G[b][:], G[b][:], PW[g][:, :, s:s + 1].broadcast_to([P, 2, D]), ALU.mult
                                    ).then_inc(s_phalf, 1)
            pool.wait_ge(s_phalf, 2 * (layer * GSUB + s) + 1)
            nc.gpsimd.tensor_tensor(row, row, G[b][:, 0, :], ALU.add).then_inc(s_phalf, 1)
            pool.wait_ge(s_phalf, 2 * (layer * GSUB + s) + 2)
            nc.gpsimd.tensor_tensor(row, row, G[b][:, 1, :], ALU.add).then_inc(s_comb, 1)

        def ride_along(layer, g, also=lambda s: None):
            all_stored(layer, g)
            if layer == 0:
                pool.wait_ge(s_xsh, STILES * (g + 1))
            for s in range(GSUB + 3):
                if s < GSUB:
                    gather(layer, g, s)
                if s >= 3:
                    combine(layer, g, s - 3)
                also(s)

        def roots(g, quarter):
            qs = slice(quarter * QP, (quarter + 1) * QP)
            pool.wait_ge(s_qv, 4 * g + quarter + 1)
            nc.gpsimd.tensor_tensor(qp[0:QR, qs], qv[0:QR, qs], neghalf[0:QR].rearrange("p (q k) -> p q k", q=QP), ALU.pow
                                    ).then_inc(s_qp, 1)

        for phase in PHASES:
            kind, layer, g = phase
            if kind == "A":
                rstds(layer, g)
            elif kind == "M":
                everywhere(0)
            elif kind in "SE" and phase in gated:
                of = gated[phase]
                scatter_ready(*of)
                scatter(of[1], range(GSUB))
            elif kind == "Q":
                roots(g, 0)
                roots(g, 1)
                if phase in rides:
                    all_stored(*rides[phase])
                    for s in range(GSUB):
                        gather(*rides[phase], s)
                        if s in (3, 5):
                            roots(g, (s + 1) // 2)
                else:
                    roots(g, 2)
                    scatter_ready(1, 0)
                    scatter(0, range(6))
                    roots(g, 3)
                    scatter(0, range(6, GSUB))
            elif kind == "E" and phase in rides:
                ride_along(*rides[phase], lambda s: everywhere(1) if (s, layer) == (3, 0) else None)
            elif kind == "C":
                all_stored(layer, g)
                for s in range(GSUB):
                    gather(layer, g, s)

    @block.scalar
    def _(act):
        def blocks(layer, g):
            def normalise(m, i, b):
                n = a0(layer, g) + i
                act.wait_ge(s_rstd[m], n + 1).then_inc(s_aalone, 1)
                last, dst, done = ((s_at, xn, s_xn), (s_rows, xs, s_vx))[m]
                if not isinstance(n, int) or n > 1:
                    act.wait_ge(last, n - 1).then_inc(s_aalone, 1)
                for s in range(BSUB):
                    row = X[:, bass.ds((g * GBLK + i) * BSUB + s, 1), :].rearrange("p a d -> p (a d)")
                    a = nc.scalar.activation(dst[b][:, s, :], row, ACT.Identity, bias=shift[m][b][:, s:s + 1],
                                             scale=rstd[m][b][:, s:s + 1])
                a.then_inc(done, 1)

            def aggregated(i, b):
                n = a0(layer, g) + i
                act.wait_ge(s_at, n + 1)
                need(act, s_conv, n - 1)
                nc.scalar.activation(aT[b][:], bk[2 + b][:], ACT.Copy).then_inc(s_atc, 1)

            def turned(i, b):
                n = a0(layer, g) + i
                act.wait_ge(s_rt, n + 1)
                need(act, s_log, n - 1)
                nc.scalar.activation(RT[b][:].rearrange("p h t -> p (h t)"), bk[5 + b][:].bitcast(F16), ACT.Copy
                                     ).then_inc(s_rtc, 1)

            def step(i, j):
                def is_block(k):
                    return not isinstance(k, int) or 0 <= k < GBLK

                if layer == 0 and is_block(i + 1):
                    aggregated(i + 1, (j + 1) % 2)
                if is_block(i):
                    normalise(1, i, j % 2)
                if layer == 0 and is_block(i + 2):
                    normalise(0, i + 2, j % 2)
                if is_block(i - 1):
                    turned(i - 1, (j + 1) % 2)

            if layer == 0:
                normalise(0, 0, 0)
                aggregated(0, 0)
                normalise(0, 1, 1)
            for i in range(2):
                step(i, i)
            with act.Fori(1, GBLK // 2 - 1) as q:
                for j in range(2):
                    step(q * 2 + j, j)
            for i in range(GBLK - 2, GBLK + 1):
                step(i, i)

        def gate(layer, g):
            act.wait_ge(s_diff, layer * NG + g + 1)
            nc.scalar.activation(expd[:], den[:], ACT.Exp).then_inc(s_exp, 1)

        def hi_half(layer, r):
            k, o, n = pieces(layer)[r]
            place, loaded = piece(layer, piece0(layer, 1) + r)
            act.wait_ge(*loaded)
            nc.scalar.activation((W1h, W2h)[k][:, o:o + n], place[:, 0:n], ACT.Copy, scale=sc[:, layer, k:k + 1]
                                 ).then_inc(s_whi, 1)

        def prep(layer):
            act.wait_ge(s_scale, layer + 1)
            if layer == 0:
                act.wait_ge(ld_late, 16 * NLATE)
                for r in range(len(pieces(0))):
                    hi_half(0, r)
            else:
                act.wait_ge(s_yp, t0(("E", 1, 0)))

        def tiles(phase):
            kind, layer, g = phase
            base, shared, n_tiles = t0(phase), kind == "S", STILES if kind == "S" else TILES

            def turned(i, j):
                n = base + i
                act.wait_ge(s_tt, n + 1)
                need(act, s_h, 2 * (n - 1))
                nc.scalar.activation(XTt[j % 2][:].rearrange("p h t -> p (h t)"), bk[4][:, 0:TS].bitcast(F16), ACT.Copy
                                     ).then_inc(s_ttc, 1)

            def step(i, j, last=False):
                b = j % 2
                n = base + i
                if not last:
                    turned(i + 1, j + 1)
                bias = BBs if shared else BB[j]
                if not shared:
                    act.wait_ge(s_bb[j], 16 * (r0(phase) + 1) + (i - j) * 4)
                for half in range(2):
                    act.wait_ge(s_h, 2 * n + half + 1)
                    need(act, s_hl, 2 * (n - 2) + half + 1)
                    for c in (2 * half, 2 * half + 1):
                        a = nc.scalar.activation(h32[b][:, c, :], bk[2 * b + half][:, (c % 2) * TS:(c % 2 + 1) * TS],
                                                 ACT.Gelu if layer == 0 else ACT.Relu,
                                                 bias=bias[:, c:c + 1], scale=inv_z[:, layer:layer + 1])
                    a.then_inc(s_act, 1)
            turned(0, 0)
            head = GATE_HEAD if phase in gated else 4
            for i in range(head):
                step(i, i % 4)
                for _ in gate_stages(phase, "ACT", i):
                    gate(*gated[phase])
            if head < n_tiles - 4:
                with act.Fori(head // 4, n_tiles // 4 - 1) as q:
                    for j in range(4):
                        step(q * 4 + j, j)
            for i in range(n_tiles - 4, n_tiles):
                step(i, i % 4, last=i == n_tiles - 1)

        def quads(phase):
            g = phase[2]

            def aggregated(i):
                n = q0(g) + i
                act.wait_ge(s_qa, n + 1)
                need(act, s_h1, 2 * n)
                nc.scalar.activation(qaT[:], bk[1][:, 0:NGRP * QR].rearrange("p (g n) -> p g n", g=NGRP), ACT.Copy
                                     ).then_inc(s_qac, 1)

            def hidden(i):
                n = q0(g) + i
                for c in range(2):
                    act.wait_ge(s_h1, 2 * n + c + 1)
                    if c == 0:
                        need(act, s_s2, n)
                    for k in range(NGRP):
                        a = nc.scalar.activation(h1T[:, c, k, :], bk[2 + c][:, k * QR:(k + 1) * QR], ACT.Relu,
                                                 bias=gb1[:, k, c:c + 1])
                    a.then_inc(s_h1c, 1)

            def weighted(i):
                n = q0(g) + i
                act.wait_ge(s_o2r, n + 1)
                need(act, s_xo, n)
                for k in range(NGRP):
                    a = nc.scalar.activation(qt2[0:QR, k, :], qt[0:QR, k, :], ACT.Relu, scale=wind[0:QR, k:k + 1])
                a.then_inc(s_qw, 1)

            def step(i, j, last=False):
                n = q0(g) + i
                if not last:
                    aggregated(i + 1)
                if not isinstance(i, int) or i > 0:
                    weighted(i - 1)
                act.wait_ge(s_s2, n + 1)
                need(act, s_o2, n)
                nc.scalar.activation(s2[0:QR, 0:4, :], bk[4][0:QR, :].rearrange("p (g d) -> p g d", g=4), ACT.Copy)
                nc.scalar.activation(s2[0:QR, 4, :], bk[5][0:QR, 0:D], ACT.Copy).then_inc(s_s2c, 1)
                if not last:
                    hidden(i + 1)

            aggregated(0)
            hidden(0)
            head = GATE_HEAD if phase in gated else 4
            for i in range(head):
                step(i, i)
                for _ in gate_stages(phase, "ACT", i):
                    gate(*gated[phase])
            if head < GQ - 4:
                with act.Fori(head // 4, GQ // 4 - 1) as q:
                    for j in range(4):
                        step(q * 4 + j, j)
            for i in range(GQ - 4, GQ):
                step(i, i, last=i == GQ - 1)
                if g == 0:
                    for r in range(2):
                        hi_half(1, 2 * (i - GQ + 4) + r)
            weighted(GQ - 1)

        for phase in PHASES:
            kind, layer, g = phase
            if kind == "A":
                blocks(layer, g)
            elif kind == "M":
                act.wait_ge(s_vconst, 1)
                nc.scalar.activation(fw[:], fw[:], ACT.Exp, bias=fwt[:, 1:2]).then_inc(s_fusx, 1)
            elif kind == "W":
                prep(layer)
            elif kind in "SE":
                tiles(phase)
            elif kind == "Q":
                quads(phase)

    @block.tensor
    def _(pe):
        pe.wait_ge(s_const, 5)

        def blocks(layer, g):
            def aggregate(i, b):
                n = a0(layer, g) + i
                pe.wait_ge(s_xn, n + 1)
                need(pe, s_atc, n - 1)
                for s in range(BSUB):
                    m = pe.matmul(bk[2 + b][:, s * P:(s + 1) * P], xn[b][:, s, :], AB[b][:, s, :], start=True, stop=True)
                m.then_inc(s_at, 1)

            def convolve(i, b):
                n = a0(layer, g) + i
                need(pe, s_x1, n - 1)
                for k in range(3):
                    pe.matmul(bk[b][:], ones16[0:1, :], bgpart[:, k].unsqueeze(1).broadcast_to([1, BSUB, D]),
                              start=k == 0, stop=False, skip_group_check=True)
                pe.wait_ge(s_atc, n + 1)
                for s in range(BSUB):
                    m = pe.matmul(bk[b][:, s * P:(s + 1) * P], aT[b][:, s * P:(s + 1) * P], Wg[:],
                                  start=False, stop=(s == BSUB - 1), skip_group_check=True)
                m.then_inc(s_conv, 1)

            def turn(i, b):
                n = a0(layer, g) + i
                pe.wait_ge(s_rows, n + 1)
                need(pe, s_rtc, n - 1)
                bank = bk[5 + b][:].bitcast(F16)
                for h in range(2):
                    for s in range(BSUB):
                        o = (h * BSUB + s) * P
                        row = R[:, bass.ds((g * GBLK + i) * BSUB + s, 1), h * D:(h + 1) * D].rearrange("p a d -> p (a d)")
                        m = pe.transpose(bank[:, o:o + P], row, ident16[:])
                m.then_inc(s_rt, 1)

            def logits(i, b):
                pe.wait_ge(s_rtc, a0(layer, g) + i + 1)
                for s in range(BSUB):
                    o = bk[7][:, bass.ds((i * BSUB + s) * EXPERTS, EXPERTS)]
                    terms = [(0, Rh), (1, Rh), (0, Rl), (1, Rl)]
                    for k, (h, w) in enumerate(terms):
                        m = pe.matmul(o, RT[b][:, h, s * P:(s + 1) * P], w[:, layer, :], start=k == 0, stop=k == 3)
                m.then_inc(s_log, 1)

            def step(i, j):
                def is_block(k):
                    return not isinstance(k, int) or 0 <= k < GBLK

                if layer == 0 and is_block(i + 1):
                    convolve(i + 1, (j + 1) % 2)
                if is_block(i - 1):
                    turn(i - 1, (j + 1) % 2)
                if layer == 0 and is_block(i + 2):
                    aggregate(i + 2, j % 2)
                if is_block(i - 1):
                    logits(i - 1, (j + 1) % 2)

            if layer == 0:
                aggregate(0, 0)
                if g == 0:
                    pe.wait_ge(s_rscale, 1)
                convolve(0, 0)
                aggregate(1, 1)
            for i in range(2):
                step(i, i)
            with pe.Fori(1, GBLK // 2 - 1) as q:
                for j in range(2):
                    step(q * 2 + j, j)
            for i in range(GBLK - 2, GBLK + 1):
                step(i, i)

        def gate(layer, g, bank):
            c = layer * NG + g
            J = 2 * GSUB
            selj = sel[:].rearrange("p k s e -> p (k s) e")

            def totals():
                pe.wait_ge(s_sel, c + 1)
                for e in range(EXPERTS):
                    m = pe.matmul(bank[0:J, e:e + 1], selj[:, :, e], ones16[:, 0:1], start=True, stop=True)
                m.then_inc(s_tot, 1)

            def counts():
                pe.wait_ge(s_totm, c + 1)
                pe.matmul(bank[:, 0:EXPERTS], ones16[0:J, :], tot[:], start=True, stop=True).then_inc(s_cnt, 1)

            def ranks():
                pe.wait_ge(s_cntr, c + 1)
                pe.matmul(bank[:, 0:J * EXPERTS], upper[:], selj.rearrange("p j e -> p (j e)"), start=True, stop=False)
                pe.matmul(bank[:, 0:J * EXPERTS], ones16[0:J, :], totm[:].rearrange("q j e -> q (j e)"), start=False,
                          stop=True).then_inc(s_rank, 1)

            return totals, counts, ranks

        def tiles(phase):
            kind, layer, g = phase
            base, shared, n_tiles = t0(phase), kind == "S", STILES if kind == "S" else TILES

            def wait_loaded(i, j):
                if not shared:
                    pe.wait_ge(s_xr[j % 4], 16 * (r0(phase) + 1) + (i - j % 4) * 4)

            def turn(i, j):
                wait_loaded(i, j)
                need(pe, s_ttc, base + i)
                bank = bk[4][:, 0:TS].bitcast(F16)
                for h in range(2):
                    for s in range(TSUB):
                        o = (h * TSUB + s) * P
                        if shared:
                            row = R[:, bass.ds(g * GSUB + i * TSUB + s, 1), h * D:(h + 1) * D].rearrange("p a d -> p (a d)")
                        else:
                            row = XR[j % 4][:, s, h * D:(h + 1) * D]
                        m = pe.transpose(bank[:, o:o + P], row, ident16[:])
                m.then_inc(s_tt, 1)

            def hidden(i, j, e):
                b = j % 2
                n = base + i
                pe.wait_ge(s_ttc, n + 1)
                for half in range(2):
                    need(pe, s_act, 2 * (n - 2) + half + 1)
                    for c in (2 * half, 2 * half + 1):
                        o = bk[2 * b + half][:, (c % 2) * TS:(c % 2 + 1) * TS]
                        for k, (w, h) in enumerate(((W1h, 0), (W1h, 1), (W1l, 0))):
                            m = pe.matmul(o, w[:, at(e, c)], XTt[b][:, h, :], start=k == 0, stop=k == 2)
                    m.then_inc(s_h, 1)

            def outs(i, j, e):
                b = j % 2
                n = base + i
                pe.wait_ge(s_hl, 2 * n + 2)
                need(pe, s_y, n - 1)
                for s in range(TSUB):
                    o = bk[6 + b][:, s * D:(s + 1) * D]
                    rows = slice(s * P, (s + 1) * P)
                    for c in range(CH):
                        for k, (h, w) in enumerate(((hh, W2h), (hl, W2h), (hh, W2l))):
                            m = pe.matmul(o, h[b][:, c, rows], w[:, at(e, c)],
                                          start=c == 0 and k == 0, stop=c == CH - 1 and k == 2)
                m.then_inc(s_yp, 1)

            def at(e, c):
                if isinstance(e, int):
                    return slice(e + c * P, e + (c + 1) * P)
                return bass.ds(e + c * P, P)

            def experts(i, count):
                if shared:
                    return [EXPERTS * HID] * count
                return nc.values_load_multi_w_load_instructions(
                    WOFF[g][0:1, bass.ds(i, count)], engines=[mybir.EngineType.PE], min_val=0, max_val=(EXPERTS - 1) * HID,
                    skip_runtime_bounds_check_because="the table's entries are clamped to the experts when it is made")[1]

            turn(0, 0)
            turn(1, 1)
            hidden(0, 0, experts(0, 1)[0])

            def steps(base_i, count, last):
                e = experts(base_i, count + (0 if last else 1))
                for j in range(count):
                    i = base_i + j
                    if not last or j + 2 < count:
                        turn(i + 2, (j + 2) % 4)
                    if not last or j + 1 < count:
                        hidden(i + 1, (j + 1) % 4, e[j + 1])
                    outs(i, j, e[j])
                    for k in gate_stages(phase, "PE", i):
                        gate(*gated[phase], gate_bank(phase))[k]()

            head = GATE_HEAD if phase in gated else 4 if base == 0 else 0
            for i in range(0, head, 4):
                steps(i, 4, False)
            if head < n_tiles - 4:
                with pe.Fori(head // 4, n_tiles // 4 - 1) as q:
                    steps(q * 4, 4, False)
            steps(n_tiles - 4, 4, True)

        def quads(phase):
            g = phase[2]

            def turn(i, j):
                b = j % 2
                n = q0(g) + i
                pe.wait_ge(s_nb, n + 1)
                need(pe, s_ntc, n)
                for k in range(NGRP):
                    m = pe.transpose(bk[0][0:QR, k * QR:(k + 1) * QR], nb[b][0:QR, k, :, :].rearrange("p b m -> p (b m)"),
                                     ident[0:QR, 0:QR])
                m.then_inc(s_nt, 1)

            def aggregate(i, j):
                b = j % 2
                n = q0(g) + i
                pe.wait_ge(s_ntc, n + 1)
                pe.wait_ge(s_qn, n + 1)
                need(pe, s_qac, n)
                pe.matmul(bk[1][:, 0:NGRP * QR], xqn[b][0:QR, :], NT[j % 4][0:QR].rearrange("p g n -> p (g n)"),
                          start=True, stop=True).then_inc(s_qa, 1)

            def hidden(i, j):
                n = q0(g) + i
                pe.wait_ge(s_qac, n + 1)
                for c in range(2):
                    need(pe, s_h1c, 2 * (n - 1) + c + 1)
                    for k in range(NGRP):
                        m = pe.matmul(bk[2 + c][:, k * QR:(k + 1) * QR], gW1[:, k, c * P:(c + 1) * P], qaT[:, k, :],
                                      start=True, stop=True)
                    m.then_inc(s_h1, 1)

            def support(i, j):
                n = q0(g) + i
                pe.wait_ge(s_h1c, 2 * n + 2)
                need(pe, s_s2c, n)
                for k in range(NGRP):
                    if k == 4:
                        need(pe, s_o2r, n)
                    for c in range(2):
                        m = pe.matmul(bk[4 + k // 4][0:QR, (k % 4) * D:(k % 4 + 1) * D], h1T[:, c, k, :], gW2[:, k, c, :],
                                      start=c == 0, stop=c == 1)
                m.then_inc(s_s2, 1)

            def outs(i, j):
                n = q0(g) + i
                pe.wait_ge(s_s2c, n + 1)
                need(pe, s_o2r, n)
                for k in range(NGRP):
                    o = bk[6][0:QR, k * D:(k + 1) * D] if k < 4 else bk[5][0:QR, D:2 * D]
                    m = pe.matmul(o, NT[j % 4][0:QR, k, :], s2[0:QR, k, :], start=True, stop=True)
                m.then_inc(s_o2, 1)

            def step(i, j):
                if not isinstance(i, int) or i + 1 < GQ:
                    aggregate(i + 1, j + 1)
                if not isinstance(i, int) or i + 2 < GQ:
                    turn(i + 2, j + 2)
                if not isinstance(i, int) or i >= 0:
                    support(i, j)
                if not isinstance(i, int) or i + 1 < GQ:
                    hidden(i + 1, j + 1)
                if not isinstance(i, int) or i >= 0:
                    outs(i, j)
                for k in gate_stages(phase, "PE", i):
                    gate(*gated[phase], gate_bank(phase))[k]()

            turn(0, 0)
            step(-1, -1)
            head = GATE_HEAD if phase in gated else 4
            for i in range(head):
                step(i, i)
            if head < GQ - 4:
                with pe.Fori(head // 4, GQ // 4 - 1) as q:
                    for j in range(4):
                        step(q * 4 + j, j)
            for i in range(GQ - 4, GQ):
                step(i, i)

        left, before_kind = None, ""
        for phase in PHASES:
            kind, layer, g = phase
            if kind in "ASEQ" and left is not None and not (kind in "SE" and before_kind in "SE"):
                pe.wait_ge(*left)
            if kind in "ASEQ":
                before_kind = kind
            if kind == "A":
                blocks(layer, g)
                left = s_lgr, layer * NG + g + 1
            elif kind in "SE":
                if phase == ("S", 0, 0):
                    pe.wait_ge(s_wfree, piece0(1, 0))
                elif phase == ("E", 1, 0):
                    pe.wait_ge(s_wfree, piece0(1, 1) + len(pieces(1)))
                tiles(phase)
                left = s_y, t0(phase) + (STILES if kind == "S" else TILES)
            elif kind == "Q":
                if g == 0:
                    pe.wait_ge(ld_g, 32)
                quads(phase)
                left = s_o2r, q0(g) + GQ

    @block.vector
    def _(dve):
        count = [0]

        def own(ins):
            count[0] += 1
            ins.then_inc(v, 1)
            dve.wait_ge(v, count[0])

        class InLoop:

            def __init__(self, per):
                self.base, self.per = count[0], per

            def at(self, i):
                self.first, self.k = self.base + i * self.per, 0

            def mark(self, ins):
                self.k += 1
                ins.then_inc(v, 1)

            def wait(self, alone=False):
                w = dve.wait_ge(v, self.first + self.k)
                if alone:
                    w.then_inc(s_alone, 1)

        def scales(layer, cols):
            own(nc.vector.tensor_scalar(big[:, layer, cols], big[:, layer, cols], 1e-30, None, ALU.max))
            own(nc.vector.tensor_scalar(pw[:, layer, cols].bitcast(U32), big[:, layer, cols].bitcast(U32), 0x7F800000, None,
                                        ALU.bitwise_and))
            own(nc.vector.reciprocal(sc[:, layer, cols], pw[:, layer, cols]))
            own(nc.vector.tensor_scalar(sc[:, layer, cols], sc[:, layer, cols], 2.0 ** 14, None, ALU.mult))
            own(nc.vector.tensor_scalar(inv[:, layer, cols], pw[:, layer, cols], 2.0 ** -14, None, ALU.mult))

        def small_operands():
            rest = bg[:]
            for k in range(3):
                own(nc.vector.tensor_copy(bgpart[:, k], rest))
                if k < 2:
                    own(nc.vector.tensor_tensor(bgrest[:, k], rest, bgpart[:, k], ALU.subtract))
                    rest = bgrest[:, k]
            dve.wait_ge(s_rall, 1)
            for l in range(2):
                scales(l, slice(3, 4))
                nc.vector.tensor_scalar(inv_l[:, l:l + 1], inv[:, l, 3:4], 2.0 ** -XSCALE_LOG, None, ALU.mult)
                own(nc.vector.tensor_scalar(Rh[:, l, :], rstage[:, l, :], sc[:, l, 3:4], None, ALU.mult))
                m = nc.vector.scalar_tensor_tensor(out=Rl[:, l, :], in0=rstage[:, l, :], scalar=sc[:, l, 3:4],
                                                   in1=Rh[:, l, :], op0=ALU.mult, op1=ALU.subtract)
            m.then_inc(s_rscale, 1)

        dve.wait_ge(ld_small, 16 * NSMALL)
        for l in range(2):
            m = nc.vector.tensor_reduce(big[:, l, 3:4], rstage[:, l, :], AX, ALU.max, apply_absolute_value=True)
        m.then_inc(s_rmax, 1)

        def fusion_weights():
            own(nc.vector.tensor_reduce(fwt[:, 0:1], fw[:], AX, ALU.max))
            nc.vector.tensor_scalar(fwt[:, 1:2], fwt[:, 0:1], -1.0, None, ALU.mult).then_inc(s_vconst, 1)

        def fusion_weights_end():
            dve.wait_ge(s_fusx, 1)
            own(nc.vector.tensor_reduce(fwt[:, 2:3], fw[:], AX, ALU.add))
            own(nc.vector.reciprocal(fwt[:, 3:4], fwt[:, 2:3]))
            own(nc.vector.tensor_scalar(fw[:], fw[:], fwt[:, 3:4], None, ALU.mult))
            nc.vector.tensor_tensor(wind[0:QR], fw[0:QR], rowind[0:QR], ALU.mult)

        def blocks(layer, g):
            ks = InLoop(4 if layer == 0 else 2)

            def row(i, s):
                return X[:, bass.ds((g * GBLK + i) * BSUB + s, 1), :].rearrange("p a d -> p (a d)")

            def rows4(i):
                return X[:, bass.ds((g * GBLK + i) * BSUB, BSUB), :]

            def moments(m, i, b, scale):
                for s in range(BSUB):
                    x = nc.vector.bn_stats(stats[m][b][:, s, :], row(i, s))
                ks.mark(x)
                ks.wait(alone=True)
                for s in range(BSUB):
                    x = nc.vector.bn_aggr(mv[m][b][:, s, :], stats[m][b][:, s, :])
                ks.mark(x)
                ks.wait()
                nc.vector.tensor_scalar(negmean[m][b][:], mv[m][b][:, :, 0], -1.0, None, ALU.mult)
                nc.vector.tensor_scalar(ve[m][b][:], mv[m][b][:, :, 1], EPS, scale, ALU.add, ALU.mult).then_inc(s_var[m], 1)

            def input_moments(i, b):
                dve.wait_ge(ld_a[b], 48 * (a0(0, g) // 2 + 1) + (i - b) * 24).then_inc(s_alone, 1)
                moments(0, i, b, 1.0)

            def sum_moments(i, b):
                n = a0(layer, g) + i
                if layer == 0:
                    dve.wait_ge(s_conv, n + 1)
                    nc.vector.tensor_tensor(rows4(i), rows4(i), bk[b][:].rearrange("p (s d) -> p s d", s=BSUB), ALU.add
                                            ).then_inc(s_x1, 1)
                    dve.wait_ge(s_x1, n + 1).then_inc(s_alone, 1)
                moments(1, i, b, 2.0 ** (-2 * XSCALE_LOG))

            def split(i, b):
                n = a0(layer, g) + i
                dve.wait_ge(s_vx, n + 1)
                hi = R[:, bass.ds((g * GBLK + i) * BSUB, BSUB), 0:D]
                nc.vector.tensor_copy(hi, xs[b][:]).then_inc(s_vh, 1)
                dve.wait_ge(s_vh, n + 1)
                nc.vector.tensor_tensor(R[:, bass.ds((g * GBLK + i) * BSUB, BSUB), D:2 * D], xs[b][:], hi, ALU.subtract
                                        ).then_inc(s_rows, 1)

            def step(i, j):
                if not isinstance(i, int) or i < GBLK:
                    if layer == 1 and isinstance(i, int) and i % (GBLK // 2) == 0:
                        dve.wait_ge(s_qst[2 * i // GBLK], 16 * QB * (g + 1))
                    sum_moments(i, j % 2)
                if layer == 0 and (not isinstance(i, int) or i + 2 < GBLK):
                    input_moments(i + 2, j % 2)
                if not isinstance(i, int) or i > 0:
                    split(i - 1, (j + 1) % 2)

            if layer == 0:
                for i in range(2):
                    ks.at(0)
                    input_moments(i, i)
                    ks.base += 2
                seen = count[0] = ks.base
                if g == 0:
                    small_operands()
                else:
                    for r in range(LO_AHEAD, len(pieces(0))):
                        lo_half(0, r)
                ks.base += count[0] - seen
                for i in range(2):
                    ks.at(i)
                    step(i, i)
                with dve.Fori(1, GBLK // 2 - 1) as q:
                    for j in range(2):
                        ks.at(q * 2 + j)
                        step(q * 2 + j, j)
                ks.base += 4 * (GBLK - 2)
                ks.per = 2
                for i in range(GBLK - 2, GBLK + 1):
                    ks.at(i - GBLK + 2)
                    step(i, i)
                ks.base += 4
            else:
                for i in range(GBLK + 1):
                    ks.at(i)
                    step(i, i)
                ks.base += 2 * GBLK
            count[0] = ks.base

        def read_logits(layer, g):
            dve.wait_ge(s_log, a0(layer, g) + GBLK)
            nc.vector.tensor_scalar(lgs[g][:].rearrange("p s e -> p (s e)"), bk[7][:, 0:GSUB * EXPERTS],
                                    inv_l[:, layer:layer + 1], None, ALU.mult).then_inc(s_lgr, 1)

        def gate(layer, g, bank):
            c = layer * NG + g
            J = 2 * GSUB

            def over(ap, n, width=EXPERTS):
                return ap.unsqueeze(1).broadcast_to([ap.shape[0], n, width])

            def each(ap):
                return ap.unsqueeze(2).broadcast_to([P, GSUB, EXPERTS])

            def largest(k):
                lg = lgs[g]
                src = (lg, lg2)[k]
                if k == 0:
                    dve.wait_ge(s_lgr, c + 1)
                    if layer == 1:
                        own(nc.vector.tensor_tensor(lg[:], lg[:], over(gate_bias[:], GSUB), ALU.add))
                own(nc.vector.tensor_reduce(top[:, k, :], src[:], AX, ALU.max))
                own(nc.vector.tensor_tensor(keyed[:], src[:], each(top[:, k, :]), ALU.is_equal))

            def chosen(k):
                own(nc.vector.tensor_tensor(keyed[:], keyed[:], over(rankkey[:], GSUB), ALU.mult))
                own(nc.vector.tensor_reduce(kmax[:], keyed[:], AX, ALU.max))
                m = nc.vector.tensor_tensor(sel[:, k], keyed[:], each(kmax[:]), ALU.is_equal)
                if k == 0:
                    own(m)
                    own(nc.vector.scalar_tensor_tensor(out=lg2[:], in0=sel[:, 0], scalar=-1e30, in1=lgs[g][:], op0=ALU.mult,
                                                       op1=ALU.add))
                else:
                    m.then_inc(s_sel, 1)
                    nc.vector.tensor_tensor(den[:], top[:, 1, :], top[:, 0, :], ALU.subtract).then_inc(s_diff, 1)

            def mask_totals():
                dve.wait_ge(s_tot, c + 1)
                own(nc.vector.tensor_copy(tot[:], bank[0:J, 0:EXPERTS]))
                nc.vector.tensor_tensor(totm[:], over(tot[:], J), upper[0:J, 0:J].unsqueeze(2).broadcast_to([J, J, EXPERTS]),
                                        ALU.mult).then_inc(s_totm, 1)
                dve.wait_ge(s_exp, c + 1)
                own(nc.vector.tensor_scalar(den[:], expd[:], 1.0, None, ALU.add))
                own(nc.vector.reciprocal(PW[g][:, 0, :], den[:]))
                nc.vector.tensor_tensor(PW[g][:, 1, :], PW[g][:, 0, :], expd[:], ALU.mult)

            def count_tiles():
                dve.wait_ge(s_cnt, c + 1)
                nc.vector.tensor_scalar(cnt[:], bank[:, 0:EXPERTS], float(TS - 1), None, ALU.add).then_inc(s_cntr, 1)
                dve.wait_ge(s_cntr, c + 1)
                own(nc.vector.tensor_copy(cnti[:], cnt[:]))
                own(nc.vector.tensor_scalar(cnti[:], cnti[:], TS.bit_length() - 1, None, ALU.logical_shift_right))
                own(nc.vector.tensor_copy(ntile[:], cnti[:]))

            def starts():
                prev = ntile
                for k in range(3):
                    w = 1 << k
                    nc.vector.tensor_copy(scan[k][:, 0:w], prev[:, 0:w])
                    own(nc.vector.tensor_tensor(scan[k][:, w:], prev[:, w:], prev[:, 0:EXPERTS - w], ALU.add))
                    prev = scan[k]
                nc.vector.tensor_tensor(start[:], prev[:], ntile[:], ALU.subtract)
                own(nc.vector.tensor_tensor(tcmp[:], tileno[:].unsqueeze(2).broadcast_to([1, TILES, EXPERTS]),
                                            over(prev[0:1], TILES), ALU.is_ge))
                nc.vector.tensor_scalar(start[:], start[:], float(TS), None, ALU.mult)
                own(nc.vector.tensor_reduce(texp[:], tcmp[:], AX, ALU.add))
                own(nc.vector.tensor_scalar(texp[:], texp[:], float(EXPERTS - 1), None, ALU.min))
                nc.vector.tensor_copy(EXP[g][:], texp[:])
                nc.vector.tensor_scalar(WOFF[g][:], texp[:], float(HID), None, ALU.mult)

            def places():
                dve.wait_ge(s_rank, c + 1)
                own(nc.vector.tensor_tensor(selw[:], bank[:, 0:J * EXPERTS].rearrange("p (j e) -> p j e", e=EXPERTS),
                                            over(start[:], J), ALU.add))
                own(nc.vector.tensor_tensor(selw[:], selw[:], sel[:].rearrange("p k s e -> p (k s) e"), ALU.mult))

            def places_end():
                own(nc.vector.tensor_reduce(posf[:], selw[:], AX, ALU.add))
                nc.vector.tensor_copy(POS[g][:], posf[:]).then_inc(s_route, 1)

            return (lambda: largest(0), lambda: chosen(0), lambda: largest(1), lambda: chosen(1), mask_totals, count_tiles,
                    starts, places, places_end)

        def magnitude(layer, r):
            k, o, n = pieces(layer)[r]
            place, loaded = piece(layer, piece0(layer, 0) + r)
            dve.wait_ge(*loaded)
            nc.vector.tensor_reduce(wmax[:, r:r + 1], place[:, 0:n], AX, ALU.max, apply_absolute_value=True
                                    ).then_inc(s_wfree if layer == 1 else s_max, 1)

        def magnitudes_all(layer):
            if layer == 0:
                dve.wait_ge(s_max, len(pieces(0)))
            else:
                dve.wait_ge(s_wfree, piece0(1, 1))
            half = len(pieces(layer)) // 2
            for k in range(2):
                nc.vector.tensor_reduce(big[:, layer, k:k + 1], wmax[:, k * half:(k + 1) * half], AX, ALU.max)
            dve.wait_ge(ld_b1, 16 * (layer + 1))
            nc.vector.tensor_reduce(big[:, layer, 2:3], b1all[:, 0:NE[layer]].rearrange("p e c -> p (e c)"), AX, ALU.max,
                                    apply_absolute_value=True).then_inc(s_prep, 1)

        LO_AHEAD = 3

        def lo_half(layer, r):
            k, o, n = pieces(layer)[r]
            place, _ = piece(layer, piece0(layer, 1) + r)
            hi, lo = ((W1h, W1l), (W2h, W2l))[k]
            dve.wait_ge(s_whi, layer * len(pieces(0)) + r + 1)
            nc.vector.scalar_tensor_tensor(out=lo[:, o:o + n], in0=place[:, 0:n], scalar=sc[:, layer, k:k + 1],
                                           in1=hi[:, o:o + n], op0=ALU.mult, op1=ALU.subtract).then_inc(s_wfree, 1)

        def prep(layer):
            dve.wait_ge(s_prepall, layer + 1)
            own(nc.vector.scalar_tensor_tensor(out=big[:, layer, 2:3], in0=big[:, layer, 0:1], scalar=float(D),
                                               in1=big[:, layer, 2:3], op0=ALU.mult, op1=ALU.add))
            scales(layer, slice(0, 3))
            nc.vector.tensor_scalar(inv_z[:, layer:layer + 1], inv[:, layer, 0:1], 2.0 ** -XSCALE_LOG, None, ALU.mult)
            nc.vector.tensor_tensor(inv_y[:, layer:layer + 1], inv[:, layer, 1:2], inv[:, layer, 2:3], ALU.mult
                                    ).then_inc(s_scale, 1)
            if layer == 0:
                for r in range(LO_AHEAD):
                    lo_half(0, r)

        def combine_sub(layer, g, i, b):
            dve.wait_ge(s_g[b], 32 * (c0(layer, g) // 4 + 1) + (i - b) * 8)
            row = X[:, bass.ds(g * GSUB + i, 1), :].rearrange("p a d -> p (a d)")
            nc.vector.scalar_tensor_tensor(out=row, in0=G[b][:, 0, :], scalar=PW[g][:, 0, bass.ds(i, 1)], in1=row,
                                           op0=ALU.mult, op1=ALU.add).then_inc(s_half, 1)
            dve.wait_ge(s_half, (0 if layer == 0 else GSUB) + i + 1)
            nc.vector.scalar_tensor_tensor(out=row, in0=G[b][:, 1, :], scalar=PW[g][:, 1, bass.ds(i, 1)], in1=row,
                                           op0=ALU.mult, op1=ALU.add).then_inc(s_comb, 1)

        def tiles(phase):
            kind, layer, g = phase
            base, shared, n_tiles = t0(phase), kind == "S", STILES if kind == "S" else TILES

            def split(i, j):
                b = j % 2
                n = base + i
                parts = [slice(0, CH // 2), slice(CH // 2, CH)]
                for half, cs in enumerate(parts):
                    dve.wait_ge(s_act, 2 * n + half + 1)
                    if half == 0:
                        need(dve, s_yp, n - 1)
                    nc.vector.tensor_scalar(hh[b][:, cs], h32[b][:, cs], sc[:, layer, 2:3], None, ALU.mult).then_inc(s_hh, 1)
                for half, cs in enumerate(parts):
                    dve.wait_ge(s_hh, 2 * n + half + 1)
                    nc.vector.scalar_tensor_tensor(out=hl[b][:, cs], in0=h32[b][:, cs], scalar=sc[:, layer, 2:3],
                                                   in1=hh[b][:, cs], op0=ALU.mult, op1=ALU.subtract).then_inc(s_hl, 1)

            def scale_out(i, j):
                b = j % 2
                n = base + i
                dve.wait_ge(s_yp, n + 1)
                y = ytmp[j]
                bias = BBs if shared else BB[j]
                if not shared:
                    need(dve, s_st[j], 16 * r0(phase) + (i - j) * 4)
                else:
                    need(dve, s_st[j], 16 * len(before("E", phase)) * TILES // 4)
                nc.vector.scalar_tensor_tensor(out=y[:], in0=bk[6 + b][:, 0:TSUB * D].rearrange("p (s d) -> p s d", s=TSUB),
                                               scalar=inv_y[:, layer:layer + 1],
                                               in1=bias[:, CH:].unsqueeze(1).broadcast_to([P, TSUB, D]),
                                               op0=ALU.mult, op1=ALU.add).then_inc(s_y, 1)
                if shared:
                    rows = X[:, bass.ds(g * GSUB + i * TSUB, TSUB), :]
                    dve.wait_ge(s_y, n + 1)
                    nc.vector.tensor_tensor(rows, rows, y[:], ALU.add).then_inc(s_xsh, 1)

            split(0, 0)
            head = GATE_HEAD if phase in gated else 4
            for j in range(head):
                split(j + 1, (j + 1) % 4)
                scale_out(j, j % 4)
                for k in gate_stages(phase, "DVE", j):
                    gate(*gated[phase], gate_bank(phase))[k]()
                if phase == ("E", 0, NG - 1):
                    for r in (2 * j, 2 * j + 1):
                        magnitude(1, r)
            if phase == ("E", 0, NG - 1):
                magnitudes_all(1)
            if head < n_tiles - 4:
                with dve.Fori(head // 4, n_tiles // 4 - 1) as q:
                    for j in range(4):
                        split(q * 4 + j + 1, (j + 1) % 4)
                        scale_out(q * 4 + j, j)
            for i in range(n_tiles - 4, n_tiles):
                if i + 1 < n_tiles:
                    split(i + 1, (i + 1) % 4)
                scale_out(i, i % 4)

        def quads(phase):
            g = phase[2]
            ks = InLoop(1)

            def prepare(quarter):
                half = quarter // 2
                qs = slice(quarter * QP, (quarter + 1) * QP)
                a = Aq[half][0:QR, quarter % 2 * QP:(quarter % 2 + 1) * QP]
                if quarter % 2 == 0:
                    dve.wait_ge(ld_q[half], 16 * (QB + 1) * (g + 1))
                for q in range(quarter * QP, (quarter + 1) * QP):
                    m = nc.vector.bn_stats(qst[0:QR, q, 0:6], xq[0:QR, q, :])
                own(nc.vector.tensor_tensor(a, a, self25[0:QR].unsqueeze(1).broadcast_to([QR, QP, LIVE]), ALU.add))
                for q in range(quarter * QP, (quarter + 1) * QP):
                    m = nc.vector.bn_aggr(qst[0:QR, q, 6:8], qst[0:QR, q, 0:6])
                for k in range(NGRP):
                    m = nc.vector.tensor_tensor(masked(quarter)[:, :, k, :], a,
                                                indc[0:QR, k, :].unsqueeze(1).broadcast_to([QR, QP, LIVE]), ALU.mult)
                own(m)
                own(nc.vector.tensor_reduce(deg[0:QR, qs], masked(quarter), AX, ALU.add))
                own(nc.vector.tensor_scalar(isz[0:QR, qs], deg[0:QR, qs], 0.0, None, ALU.is_equal))
                nc.vector.tensor_scalar(qv[0:QR, qs, NGRP:NGRP + 1], qst[0:QR, qs, 7:8], EPS, None, ALU.add)
                nc.vector.tensor_tensor(qv[0:QR, qs, 0:NGRP], deg[0:QR, qs], isz[0:QR, qs], ALU.add).then_inc(s_qv, 1)

            def masked(quarter):
                return am[0:QR, quarter * QP:(quarter + 1) * QP, 0:NGRP * LIVE].rearrange("p q (g m) -> p q g m", g=NGRP)

            def scale_rows(quarter):
                qs = slice(quarter * QP, (quarter + 1) * QP)
                own(nc.vector.tensor_scalar(isz[0:QR, qs], isz[0:QR, qs], -1.0, 1.0, ALU.mult, ALU.add))
                dve.wait_ge(s_qp, 4 * g + quarter + 1)
                own(nc.vector.tensor_tensor(dinv[0:QR, qs], qp[0:QR, qs, 0:NGRP], isz[0:QR, qs], ALU.mult))
                own(nc.vector.tensor_tensor(masked(quarter), masked(quarter),
                                            dinv[0:QR, qs].unsqueeze(3).broadcast_to([QR, QP, NGRP, LIVE]), ALU.mult))

            def one(ap, i):
                return ap[0:QR, bass.ds(i, 1)].rearrange("p a n -> p (a n)")

            def rows(i, j):
                b = j % 2
                n = q0(g) + i
                need(dve, s_qa, n - 1)
                nc.vector.tensor_scalar(xqn[b][0:QR], one(xq, i), one(qst, i)[:, 6:7], one(qp, i)[:, NGRP:NGRP + 1],
                                        ALU.subtract, ALU.mult).then_inc(s_qn, 1)
                need(dve, s_nt, n - 1)
                a = one(am, i)[:, 0:NGRP * LIVE].rearrange("p (g m) -> p g m", g=NGRP)
                for k in range(QB):
                    m = nc.vector.tensor_scalar(nb[b][0:QR, :, k, :], a, diagq[0:QR, k:k + 1], None, ALU.mult)
                m.then_inc(s_nb, 1)

            def columns(i, j):
                n = q0(g) + i
                dve.wait_ge(s_nt, n + 1)
                need(dve, s_o2, n - 3)
                nc.vector.tensor_tensor(NT[j % 4][0:QR], bk[0][0:QR, 0:NGRP * QR].rearrange("p (g n) -> p g n", g=NGRP),
                                        one(dinv, i).unsqueeze(2).broadcast_to([QR, NGRP, QR]), ALU.mult
                                        ).then_inc(s_ntc, 1)

            def biased(i):
                n = q0(g) + i
                dve.wait_ge(s_o2, n + 1)
                need(dve, s_qw, n)
                nc.vector.tensor_tensor(qt[0:QR, 0:4, :], bk[6][0:QR, :].rearrange("p (g d) -> p g d", g=4),
                                        gb2[0:QR, 0:4, :], ALU.add)
                nc.vector.tensor_tensor(qt[0:QR, 4, :], bk[5][0:QR, D:2 * D], gb2[0:QR, 4, :], ALU.add).then_inc(s_o2r, 1)

            def back(i):
                ks.at(i)
                dve.wait_ge(s_qw, q0(g) + i + 1)
                ks.mark(nc.vector.tensor_reduce(qsum[0:QR], qt2[0:QR].rearrange("p g d -> p d g"), AX, ALU.add))
                ks.wait()
                nc.vector.tensor_tensor(one(xq, i), one(xq, i), qsum[0:QR], ALU.add).then_inc(s_xo, 1)

            def step(i, j):
                if not isinstance(i, int) or i >= 1:
                    biased(i - 1)
                if not isinstance(i, int) or i + 2 < GQ:
                    columns(i + 2, j + 2)
                if not isinstance(i, int) or i + 3 < GQ:
                    rows(i + 3, j + 3)
                if phase in rides:
                    for k in range(2):
                        combine_sub(*rides[phase], i * 2 + k, (j * 2 + k) % 4)
                if not isinstance(i, int) or i >= 1:
                    back(i - 1)

            if g == 0:
                dve.wait_ge(s_yp, t0(("E", 1, 0)))
            QUARTER_STEPS = (((0, 2), (1, 3)), ((2, 4), (5, 8)))

            def between(i):
                seen = count[0]
                if i == 0:
                    scale_rows(1)
                at = QUARTER_STEPS[phase in gated]
                for quarter in (2, 3):
                    if i == at[quarter - 2][0]:
                        prepare(quarter)
                    if i == at[quarter - 2][1]:
                        scale_rows(quarter)
                for k in gate_stages(phase, "DVE", i):
                    gate(*gated[phase], gate_bank(phase))[k]()
                ks.base += count[0] - seen

            prepare(0)
            prepare(1)
            scale_rows(0)
            ks.base = count[0]
            rows(0, 0)
            rows(1, 1)
            columns(0, 0)
            rows(2, 2)
            columns(1, 1)
            head = GATE_HEAD if phase in gated else 4
            for i in range(head):
                step(i, i)
                count[0] = ks.base + i
                between(i)
            if head < GQ - 4:
                with dve.Fori(head // 4, GQ // 4 - 1) as q:
                    for j in range(4):
                        step(q * 4 + j, j)
            for i in range(GQ - 4, GQ):
                step(i, i)
                if g == 0:
                    for r in range(2):
                        lo_half(1, 2 * (i - GQ + 4) + r)
            biased(GQ - 1)
            back(GQ - 1)
            count[0] = ks.base + GQ

        for phase in PHASES:
            kind, layer, g = phase
            if kind == "A":
                blocks(layer, g)
                read_logits(layer, g)
            elif kind == "M":
                dve.wait_ge(ld_late, 16 * NLATE)
                fusion_weights()
                for r in range(len(pieces(0))):
                    magnitude(0, r)
                magnitudes_all(0)
                fusion_weights_end()
            elif kind == "W":
                prep(layer)
            elif kind in "SE":
                tiles(phase)
            elif kind == "Q":
                quads(phase)
            elif kind == "C":
                loop(dve, GSUB, 4, lambda i, j: combine_sub(layer, g, i, j))


def kernel(**inputs):
    import concourse.bacc as _bacc
    from concourse import mybir as _mybir
    from concourse.bass_utils import run_bass_kernel_spmd as _run

    a = {k: np.asarray(x) for k, x in inputs.items()}
    c = np.ascontiguousarray

    def biases(b1, b2):
        n = b1.shape[0]
        return c(np.concatenate([b1.reshape(n, CH, P).transpose(0, 2, 1),
                                 np.broadcast_to(b2[:, None, :], (n, P, D))], axis=2))

    def chunks(w):
        return c(w.reshape(w.shape[0], CH, P, D).transpose(2, 0, 1, 3))

    member = np.zeros((NGRP, LIVE), np.float32)
    for k, nodes in enumerate(GRPS):
        member[k, nodes] = 1.0
    node = np.arange(QR) % LIVE
    graph = np.arange(QR) // LIVE
    arrays = {
        "x": a["x"].reshape(TOKENS, D),
        "adjT2": c(a["adj"].transpose(0, 2, 1)).reshape(SUBS, P, NODES),
        "adj25": c(a["adj"][:, :LIVE, :LIVE]).reshape(GRAPHS * LIVE, LIVE),
        "gnn_w": a["L0_gnn_weight"],
        "gnn_b": a["L0_gnn_bias"].reshape(1, D),
        "wr0": a["L0_ffn_Wr"],
        "wr1": c(a["L1_ffn_Wg"].T),
        "bg": a["L1_ffn_bg"].reshape(1, EXPERTS),
        "w1_0": c(np.concatenate([a["L0_ffn_W1p"], a["L0_ffn_W1s"][None]]).transpose(1, 0, 2)).reshape(P, -1),
        "w2_0": chunks(np.concatenate([a["L0_ffn_W2p"], a["L0_ffn_W2s"][None]])).reshape(P, -1),
        "bb0": biases(np.concatenate([a["L0_ffn_b1p"], a["L0_ffn_b1s"][None]]),
                      np.concatenate([a["L0_ffn_b2p"], a["L0_ffn_b2s"][None]])),
        "w1_1": c(a["L1_ffn_W1"].transpose(2, 0, 1)).reshape(P, -1),
        "w2_1": chunks(c(a["L1_ffn_W2"].transpose(0, 2, 1))).reshape(P, -1),
        "bb1": biases(a["L1_ffn_b1"], a["L1_ffn_b2"]),
        "gW1": c(a["L1_gnn_W1"].transpose(1, 0, 2)),
        "gW2": c(a["L1_gnn_W2"].reshape(NGRP, 2, P, D).transpose(2, 0, 1, 3)),
        "gb1": c(a["L1_gnn_b1"].reshape(NGRP, 2, P).transpose(2, 0, 1)),
        "gb2": a["L1_gnn_b2"].reshape(1, NGRP * D),
        "fusion": a["L1_gnn_fusion_w"].reshape(1, NGRP),
        "indc": c((member[:, node].T[:, :, None] * member[None]).reshape(QR, NGRP * LIVE)),
        "rowind": c(member[:, node].T),
        "self25": c(np.eye(LIVE, dtype=np.float32)[node]),
        "diagq": c(np.eye(QB, dtype=np.float32)[graph]),
    }
    nc = _bacc.Bacc("TRN2", target_bir_lowering=False, num_devices=1)
    t = {k: nc.dram_tensor(f"in_{k}", x.shape, _mybir.dt.from_np(x.dtype), kind="ExternalInput").ap()
         for k, x in arrays.items()}
    out = nc.dram_tensor("out_0", (TOKENS, D), F32, kind="ExternalOutput").ap()
    program(nc, t, out)
    r = _run(nc, [{f"in_{k}": x for k, x in arrays.items()}], core_ids=[0])
    return r.results[0]["out_0"].reshape(GRAPHS, NODES, D)
```
